# Optimizing a Trainium2 kernel written in Bass

```python
import numpy as np
import jax
import jax.numpy as jnp

def _softmax(x, axis=-1):
    return jax.nn.softmax(x, axis=axis)

def _gelu(x):
    return jax.nn.gelu(x, approximate=True)

def _silu(x):
    return jax.nn.silu(x)

def _sigmoid(x):
    return jax.nn.sigmoid(x)

def _layernorm(x, axis=-1, eps=1e-05):
    m = jnp.mean(x, axis=axis, keepdims=True)
    v = jnp.var(x, axis=axis, keepdims=True)
    return (x - m) / jnp.sqrt(v + eps)

def _scatter_add(tgt, idx, src, axis=0):
    return tgt.at[idx].add(src)

def _segment_sum(src, seg, n):
    return jax.ops.segment_sum(src, seg, n)
kernel_name = 'mk_audio_tower_d1_tok_aud1d512_r4_2396b3'

def setup_inputs(seed: int=0):
    np.random.seed(seed)
    _w = jnp.asarray

    def _rec_inputs():
        import jax
        import jax.numpy as jnp
        _rk = jax.random.key(seed)
        x = -0.000928989 + 1.00043 * jax.random.normal(jax.random.fold_in(_rk, 1), (32, 2048), jnp.float32)
        return x
    x = _rec_inputs()

    def _L0_tok_setup():
        import jax, jax.numpy as jnp
        import numpy as np
        SEG_LEN = 48
        STRIDE = SEG_LEN // 2
        CURVATURE = 1.0
        BALL_EPS = 0.004
        MIN_NORM = 1e-15
        key = jax.random.key(seed)
        k1, k2, k3 = jax.random.split(key, 3)
        B, L, D = (128, 2048, 128)
        x_raw = jax.random.normal(k1, (B, L), dtype=jnp.float32)
        W = jax.random.normal(k2, (SEG_LEN, D), dtype=jnp.float32) * (1.0 / np.sqrt(SEG_LEN))
        b = jax.random.normal(k3, (D,), dtype=jnp.float32) * 0.01
        effective_scale = jnp.ones((1,), dtype=jnp.float32)
        return {'x_raw': x_raw, 'W': W, 'b': b, 'effective_scale': effective_scale}
    _L0_tok_all = _L0_tok_setup()
    _L0_tok_in = {k: v for k, v in _L0_tok_all.items() if k in ('W', 'b', 'effective_scale')}
    del _L0_tok_all

    def _L0_attn_setup():
        import jax, jax.numpy as jnp
        import numpy as np
        B, N, C = (4, 256, 128)
        HEADS, DIM_HEAD = (8, 64)
        DIM_E, DIM_S, DIM_H = (64, 64, 32)
        INNER = HEADS * DIM_HEAD

        def _sqdist(a, b):
            an = jnp.sum(a * a, -1)
            bn = jnp.sum(b * b, -1)
            return an[..., :, None] + bn[..., None, :] - 2.0 * jnp.einsum('bhnd,bhmd->bhnm', a, b)
        key = jax.random.key(seed)
        ks = jax.random.split(key, 10)
        s = 0.02
        return {'x': jax.random.normal(ks[0], (B, N, C), jnp.float32), 'w_qkv': jax.random.normal(ks[1], (3 * INNER, C), jnp.float32) * s, 'w_proj': jax.random.normal(ks[2], (C, INNER), jnp.float32) * s, 'b_proj': jnp.zeros((C,), jnp.float32), 'w_e': jax.random.normal(ks[3], (DIM_E, DIM_HEAD), jnp.float32) * s, 'b_e': jax.random.normal(ks[4], (DIM_E,), jnp.float32) * s, 'w_s': jax.random.normal(ks[5], (DIM_S, DIM_HEAD), jnp.float32) * s, 'b_s': jax.random.normal(ks[6], (DIM_S,), jnp.float32) * s, 'w_h': jax.random.normal(ks[7], (DIM_H, DIM_HEAD), jnp.float32) * s, 'b_h': jax.random.normal(ks[8], (DIM_H,), jnp.float32) * s, 'alpha': jnp.float32(1.0), 'beta': jnp.float32(1.0), 'gamma': jnp.float32(1.0), 'temperature': jnp.float32(1.0)}
    _L0_attn_all = _L0_attn_setup()
    _L0_attn_in = {k: v for k, v in _L0_attn_all.items() if k in ('w_qkv', 'w_proj', 'b_proj', 'w_e', 'b_e', 'w_s', 'b_s', 'w_h', 'b_h', 'alpha', 'beta', 'gamma', 'temperature')}
    del _L0_attn_all

    def _L0_ffn_setup():
        import jax, jax.numpy as jnp
        import numpy as np
        B, T, D = (4, 2048, 128)
        E, F, CAP = (8, 512, 1024)
        key = jax.random.key(seed)
        ks = jax.random.split(key, 6)
        s = 0.02
        return {'x': jax.random.normal(ks[0], (B, T, D), dtype=jnp.float32), 'Wr': jax.random.normal(ks[1], (D, E), dtype=jnp.float32) * s, 'W1': jax.random.normal(ks[2], (E, D, F), dtype=jnp.float32) * s, 'b1': jax.random.normal(ks[3], (E, F), dtype=jnp.float32) * s, 'W2': jax.random.normal(ks[4], (E, F, D), dtype=jnp.float32) * s, 'b2': jax.random.normal(ks[5], (E, D), dtype=jnp.float32) * s}
    _L0_ffn_all = _L0_ffn_setup()
    _L0_ffn_in = {k: v for k, v in _L0_ffn_all.items() if k in ('Wr', 'W1', 'b1', 'W2', 'b2')}
    del _L0_ffn_all
    return {'x': x, 'L0_tok_W': _L0_tok_in['W'], 'L0_tok_b': _L0_tok_in['b'], 'L0_tok_effective_scale': _L0_tok_in['effective_scale'], 'L0_attn_w_qkv': _L0_attn_in['w_qkv'], 'L0_attn_w_proj': _L0_attn_in['w_proj'], 'L0_attn_b_proj': _L0_attn_in['b_proj'], 'L0_attn_w_e': _L0_attn_in['w_e'], 'L0_attn_b_e': _L0_attn_in['b_e'], 'L0_attn_w_s': _L0_attn_in['w_s'], 'L0_attn_b_s': _L0_attn_in['b_s'], 'L0_attn_w_h': _L0_attn_in['w_h'], 'L0_attn_b_h': _L0_attn_in['b_h'], 'L0_attn_alpha': _L0_attn_in['alpha'], 'L0_attn_beta': _L0_attn_in['beta'], 'L0_attn_gamma': _L0_attn_in['gamma'], 'L0_attn_temperature': _L0_attn_in['temperature'], 'L0_ffn_Wr': _L0_ffn_in['Wr'], 'L0_ffn_W1': _L0_ffn_in['W1'], 'L0_ffn_b1': _L0_ffn_in['b1'], 'L0_ffn_W2': _L0_ffn_in['W2'], 'L0_ffn_b2': _L0_ffn_in['b2']}

def reference(x, L0_tok_W, L0_tok_b, L0_tok_effective_scale, L0_attn_w_qkv, L0_attn_w_proj, L0_attn_b_proj, L0_attn_w_e, L0_attn_b_e, L0_attn_w_s, L0_attn_b_s, L0_attn_w_h, L0_attn_b_h, L0_attn_alpha, L0_attn_beta, L0_attn_gamma, L0_attn_temperature, L0_ffn_Wr, L0_ffn_W1, L0_ffn_b1, L0_ffn_W2, L0_ffn_b2):
    import jax
    import jax.numpy as jnp

    def _L0_tok_ref(x_raw, W, b, effective_scale):
        import jax, jax.numpy as jnp
        import numpy as np
        SEG_LEN = 48
        STRIDE = SEG_LEN // 2
        CURVATURE = 1.0
        BALL_EPS = 0.004
        MIN_NORM = 1e-15
        B, L = x_raw.shape
        seg_len, D = W.shape
        N = (L - seg_len) // STRIDE + 1
        idx = jnp.arange(N)[:, None] * STRIDE + jnp.arange(seg_len)[None, :]
        segs = x_raw[:, idx]
        z = jnp.einsum('bnl,ld->bnd', segs, W) + b
        scale = jnp.tanh(effective_scale[0])
        u = z * scale
        sqrt_c = jnp.sqrt(jnp.float32(CURVATURE))
        u_norm = jnp.maximum(jnp.linalg.norm(u, axis=-1, keepdims=True), MIN_NORM)
        y = jnp.tanh(sqrt_c * u_norm) * u / (sqrt_c * u_norm)
        y_norm = jnp.maximum(jnp.linalg.norm(y, axis=-1, keepdims=True), MIN_NORM)
        maxnorm = (1.0 - BALL_EPS) / sqrt_c
        y = jnp.where(y_norm > maxnorm, y / y_norm * maxnorm, y)
        return y

    def _L0_attn_ref(x, w_qkv, w_proj, b_proj, w_e, b_e, w_s, b_s, w_h, b_h, alpha, beta, gamma, temperature):
        import jax, jax.numpy as jnp
        import numpy as np
        B, N, C = (4, 256, 128)
        HEADS, DIM_HEAD = (8, 64)
        DIM_E, DIM_S, DIM_H = (64, 64, 32)
        INNER = HEADS * DIM_HEAD

        def _sqdist(a, b):
            an = jnp.sum(a * a, -1)
            bn = jnp.sum(b * b, -1)
            return an[..., :, None] + bn[..., None, :] - 2.0 * jnp.einsum('bhnd,bhmd->bhnm', a, b)
        Bx, Nx, Cx = x.shape
        dh = w_e.shape[1]
        H = w_qkv.shape[0] // 3 // dh
        qkv = x @ w_qkv.T
        q, k, v = jnp.split(qkv, 3, axis=-1)
        to_heads = lambda t: t.reshape(Bx, Nx, H, dh).transpose(0, 2, 1, 3)
        q, k, v = (to_heads(q), to_heads(k), to_heads(v))
        eq, ek = (q @ w_e.T + b_e, k @ w_e.T + b_e)
        sq, sk = (q @ w_s.T + b_s, k @ w_s.T + b_s)
        sq = sq / jnp.maximum(jnp.linalg.norm(sq, axis=-1, keepdims=True), 1e-12)
        sk = sk / jnp.maximum(jnp.linalg.norm(sk, axis=-1, keepdims=True), 1e-12)
        hq, hk = (jnp.tanh(q @ w_h.T + b_h), jnp.tanh(k @ w_h.T + b_h))
        dE = jnp.sqrt(jnp.maximum(_sqdist(eq, ek), 1e-12))
        sim = jnp.einsum('bhnd,bhmd->bhnm', sq, sk)
        dS = jnp.arccos(jnp.clip(sim, -1.0 + 1e-06, 1.0 - 1e-06))
        un = jnp.sum(hq * hq, -1)
        vn = jnp.sum(hk * hk, -1)
        dns = jnp.maximum(_sqdist(hq, hk), 0.0)
        denom = (1.0 - un)[..., :, None] * (1.0 - vn)[..., None, :]
        arg = jnp.maximum(1.0 + 2.0 * dns / (denom + 1e-08), 1.0 + 1e-06)
        dH = jnp.arccosh(arg)
        sp = jax.nn.softplus
        D = sp(alpha) * dE + sp(beta) * dS + sp(gamma) * dH
        attn = jax.nn.softmax(-D / sp(temperature), axis=-1)
        out = jnp.einsum('bhnm,bhmd->bhnd', attn, v)
        out = out.transpose(0, 2, 1, 3).reshape(Bx, Nx, H * dh)
        return out @ w_proj.T + b_proj

    def _L0_ffn_ref(x, Wr, W1, b1, W2, b2):
        import jax, jax.numpy as jnp
        import numpy as np
        B, T, D = (4, 2048, 128)
        E, F, CAP = (8, 512, 1024)
        Bb, Tt, Dd = x.shape
        N = Bb * Tt
        C = min(CAP, N)
        x_flat = x.reshape(N, Dd)
        logits = x_flat @ Wr
        probs = jax.nn.softmax(logits, axis=0)
        vals, idx = jax.lax.top_k(probs.T, C)
        selected = x_flat[idx]
        h = jax.nn.gelu(jnp.einsum('ecd,edf->ecf', selected, W1) + b1[:, None, :], approximate=False)
        out_e = jnp.einsum('ecf,efd->ecd', h, W2) + b2[:, None, :]
        weighted = vals[..., None] * out_e
        output = jnp.zeros_like(x_flat).at[idx.reshape(-1)].add(weighted.reshape(-1, Dd))
        return output.reshape(Bb, Tt, Dd)
    h = _L0_tok_ref(x, L0_tok_W, L0_tok_b, L0_tok_effective_scale)
    h = h + _L0_attn_ref(_layernorm(h, axis=-1), L0_attn_w_qkv, L0_attn_w_proj, L0_attn_b_proj, L0_attn_w_e, L0_attn_b_e, L0_attn_w_s, L0_attn_b_s, L0_attn_w_h, L0_attn_b_h, L0_attn_alpha, L0_attn_beta, L0_attn_gamma, L0_attn_temperature)
    h = h + _L0_ffn_ref(_layernorm(h, axis=-1), L0_ffn_Wr, L0_ffn_W1, L0_ffn_b1, L0_ffn_W2, L0_ffn_b2)
    return h

_drawn_inputs = setup_inputs


def setup_inputs(seed=0):
    import zlib

    import numpy as np

    out = dict(_drawn_inputs(seed))
    spreads = {'L0_attn_b_proj': (0.0, 0.1)}
    factors = {'L0_tok_b': 5.509,
     'L0_attn_w_e': 8.0,
     'L0_attn_b_e': 64.0,
     'L0_attn_w_s': 18.783,
     'L0_attn_b_s': 64.0,
     'L0_attn_w_h': 6.771,
     'L0_attn_b_h': 8.0,
     'L0_ffn_Wr': 8.0,
     'L0_ffn_W1': 8.0,
     'L0_ffn_b1': 64.0,
     'L0_ffn_W2': 8.0,
     'L0_ffn_b2': 64.0}
    for name, (base, spread) in spreads.items():
        noise = np.random.default_rng([zlib.crc32(name.encode()), seed]).standard_normal(out[name].shape)
        drawn = base * np.exp(spread * noise) if base else spread * noise
        out[name] = jnp.asarray(drawn.astype(out[name].dtype))
    for name, factor in factors.items():
        out[name] = (out[name] * factor).astype(out[name].dtype)
    return out
```

```python
from contextlib import ExitStack

import numpy as np

import concourse.bass as bass
from concourse import mybir

F32 = mybir.dt.float32
I32 = mybir.dt.int32
ALU = mybir.AluOpType
ACT = mybir.ActivationFunctionType
AX = mybir.AxisListType.X

P = 128
SEG, STRIDE = 48, 24
BALL_EPS, MIN_NORM = 0.004, 1e-15
HEADS, DH = 8, 64
DE, DS, DHY = 64, 64, 32
FEAT = DE + DS + DHY
LN_EPS = 1e-5
TINY = 2.0 ** -60
SIM_MAX = float(np.float32(1.0 - 1e-6))
ARG_MIN_HALF = float((np.float32(1.0 + 1e-6) - np.float32(1.0)) / 2)
NORM_SHIFT = 20
TOP = 1024
TB = 384
SET_SQRT, SET_LN_EXP, SET_ATAN_TANH = "sqrt_and_others", "natural_log_exp_and_others", "sigmoid_and_others"


def tower(nc, x, tok_W, tok_b, effective_scale, w_qkv, w_proj, b_proj, w_e, b_e, w_s, b_s, w_h, b_h,
          alpha, beta, gamma, temperature, Wr, W1, b1, W2, b2, out):
    B, L = x.shape
    D = tok_W.shape[1]
    N = (L - SEG) // STRIDE + 1
    T = B * N
    E, _, F = W1.shape
    NT = T // P
    NB = T // TB
    TPB = TB // P
    FC = F // P
    PAIRS = B // 2
    W2N = 2 * N
    INNER = HEADS * DH
    assert D == P and T == NT * P and T == NB * TB and B % 8 == 0 and P % E == 0

    h2_dram = nc.dram_tensor("h2_scratch", (T, D), F32, kind="Internal").ap()

    with ExitStack() as ctx:
        banks = [ctx.enter_context(nc.psum_tensor(f"slot{k}", [P, 2, 512], F32)) for k in range(4)]
        h2 = ctx.enter_context(nc.sbuf_tensor("h2", [P, NT, D], F32))
        ident = ctx.enter_context(nc.sbuf_tensor("ident", [P, P], F32))
        h2_saved = ctx.enter_context(nc.semaphore("h2_saved"))
        embed_and_attend(nc, (B, L, D, N, PAIRS, W2N, INNER), banks, ident, h2_dram, h2_saved, x, tok_W, tok_b, effective_scale,
                         w_qkv, w_proj, b_proj, w_e, b_e, w_s, b_s, w_h, b_h, alpha, beta, gamma, temperature)
        experts(nc, (D, T, E, F, NT, NB, TPB, FC, PAIRS), banks, ident, h2, h2_dram, h2_saved, Wr, W1, b1, W2, b2, out)


def embed_and_attend(nc, dims, banks, ident, h2_dram, h2_saved, x, tok_W, tok_b, effective_scale,
                     w_qkv, w_proj, b_proj, w_e, b_e, w_s, b_s, w_h, b_h, alpha, beta, gamma, temperature):
    B, L, D, N, PAIRS, W2N, INNER = dims
    QT = HEADS // 2
    HT = HEADS // 4
    CH = 4
    with ExitStack() as ctx:
        def sb(name, shape, dt=F32):
            return ctx.enter_context(nc.sbuf_tensor(name, shape, dt))

        block64 = sb("block64", [P, P])
        block32 = sb("block32", [P, P])
        pick2 = sb("pick2", [P, 2, N])
        pick4 = sb("pick4", [P, 4, N])
        pick4_32nd = sb("pick4_32nd", [P, 4, W2N])
        quarter = sb("quarter", [P, N])
        shift_bias = sb("shift_bias", [P, 1])
        eps_bias = sb("eps_bias", [P, 1])
        seg_w = sb("seg_w", [SEG + 1, D])
        w_heads = sb("w_heads", [DH, 2 * HEADS, D])
        w_es = sb("w_es", [DE + DS, DH])
        w_hy = sb("w_hy", [DHY, DH])
        w_v = sb("w_v", [P, 4, D])
        w_p = sb("w_p", [P, INNER])
        featT = sb("featT", [DH, FEAT])
        comp_e = sb("comp_e", [P, 2 * HEADS * DE])
        comp_s = sb("comp_s", [P, 2 * HEADS * DS])
        comp_h = sb("comp_h", [P, 2 * HEADS * DHY])
        w_vT = sb("w_vT", [P, INNER])
        w_pT = sb("w_pT", [P, 4, D])
        be2 = sb("be2", [P, 1])
        bs2 = sb("bs2", [P, 1])
        bh4 = sb("bh4", [P, 1])
        bproj = sb("bproj", [P, D])
        raw5 = sb("raw5", [P, 5])
        sp_abs = sb("sp_abs", [P, 4])
        sp = sb("sp", [P, 4])
        scale_t = sb("scale_t", [P, 1])
        c_e2 = sb("c_e2", [P, 1])
        c_s = sb("c_s", [P, 1])
        c_h = sb("c_h", [P, 1])

        seg = [sb(f"seg{k}", [N, CH, SEG]) for k in range(2)]
        segT = [sb(f"segT{k}", [SEG + 1, CH * N]) for k in range(2)]
        u = sb("u", [N, B, D])
        stats = sb("stats", [N, B, 6])
        st = {n: sb(f"st_{n}", [N, B]) for n in ("sum", "mean", "diff", "m2", "sq", "norm", "unorm", "th",
                                                 "f", "yn", "clip", "var", "std", "gain", "shift")}

        xn = sb("xn", [N, 2, D])
        xT = sb("xT", [P, W2N])
        eq, eq_sq, ek_sq = (sb(n, [P, QT, W2N]) for n in ("eq", "eq_sq", "ek_sq"))
        ek_m2 = sb("ek_m2", [P, QT, 2, W2N])
        s_raw = sb("s_raw", [P, 2, QT, W2N])
        s_sq = sb("s_sq", [P, 2, QT, W2N])
        s_inv = sb("s_inv", [P, 2, QT, W2N])
        sq_n = sb("sq_n", [P, QT, W2N])
        sk_n = sb("sk_n", [P, QT, 2, W2N])
        hqk = sb("hqk", [P, 2, HT, W2N])
        hq_sq = sb("hq_sq", [P, HT, W2N])
        one_un = sb("one_un", [P, HT, W2N])
        hk_m2 = sb("hk_m2", [P, HT, 4, W2N])
        hk_sq4 = sb("hk_sq4", [P, HT, 4, W2N])
        hk_den = sb("hk_den", [P, HT, 4, W2N])
        v_aug = sb("v_aug", [N, 2, HEADS, DH + 1])
        esb, csb, den, mq, rden, dist, su, sh, hs, hr, attnT = (
            sb(n, [N, 2, HEADS * N]) for n in ("esb", "csb", "den", "mq", "rden", "dist", "su", "sh", "hs",
                                               "hr", "attnT"))
        dmin = sb("dmin", [N, 2 * HEADS])
        rsum = sb("rsum", [N, 2, HEADS])
        o_tok = [sb(f"o_tok{k}", [N, HEADS, DH]) for k in range(2)]
        oT = [sb(f"oT{k}", [P, 4, N]) for k in range(2)]
        hres = sb("hres", [N, 2, D])
        h2_out = sb("h2_out", [N, 2, D])

        def sem(name):
            return ctx.enter_context(nc.semaphore(name))

        (ident_zero, ident_ready, consts_set, picks_set, seg_w_loaded, weights_loaded, params_loaded, segT_ready,
         z_filled, u_ready, stats_ready, ones_set, stat_step, stat_root, softplus_step, c_ready, scale_ready,
         w_turned, featT_ready, wvp_turned, wvp_ready, comp_filled, comp_ready, xn_ready, xT_filled, xT_ready,
         eq_filled, eq_ready, eq_squared, ek_filled, ek_squared, ek_ready, sqf_filled, sqf_ready, skf_filled,
         skf_ready, s_squared, snq_filled, snk_filled, s_norm_ready, s_inv_step, s_inv_ready, sn_ready,
         hf_filled, hf_ready, hq_squared, un_filled, un_ready, hk_spread, hk_squared, hk_den_ready, v_filled,
         v_placed, e_filled, e_read, s_filled, s_read, hden_filled, den_ready, hdns_filled, mq_ready, rden_step,
         rden_ready, mq_scaled, q_ready, dist_rooted, su_rooted, sh_rooted, hs_rooted, hr_rooted, w_step,
         w_ready, t_ready, atan_ready, g_ready, log_ready, dist_h, dist_hs, dmin_ready, dist_shifted, exp_ready,
         attn_turned, attnT_ready, pv_filled, rsum_ready, o_ready, o_turned, oT_ready, proj_filled, hres_ready,
         h2_ready) = (
             sem(n) for n in """ident_zero ident_ready consts_set picks_set seg_w_loaded weights_loaded params_loaded segT_ready
                 z_filled u_ready stats_ready ones_set stat_step stat_root softplus_step c_ready scale_ready
                 w_turned featT_ready wvp_turned wvp_ready comp_filled comp_ready xn_ready xT_filled xT_ready
                 eq_filled eq_ready eq_squared ek_filled ek_squared ek_ready sqf_filled sqf_ready skf_filled
                 skf_ready s_squared snq_filled snk_filled s_norm_ready s_inv_step s_inv_ready sn_ready hf_filled
                 hf_ready hq_squared un_filled un_ready hk_spread hk_squared hk_den_ready v_filled v_placed
                 e_filled e_read s_filled s_read hden_filled den_ready hdns_filled mq_ready rden_step rden_ready
                 mq_scaled q_ready dist_rooted su_rooted sh_rooted hs_rooted hr_rooted w_step w_ready t_ready
                 atan_ready g_ready log_ready dist_h dist_hs dmin_ready dist_shifted exp_ready attn_turned
                 attnT_ready pv_filled rsum_ready o_ready o_turned oT_ready proj_filled hres_ready h2_ready""".split())
        seg_freed = [ctx.enter_context(nc.semaphore(f"seg_freed{k}")) for k in range(2)]
        seg_in = [ctx.enter_context(nc.semaphore(f"seg_in{k}")) for k in range(2)]
        block = ctx.enter_context(nc.Block())

        CHUNKS = B // CH
        COMP = [(g, min(3, 2 * HEADS - g)) for g in range(0, 2 * HEADS, 3)]
        COMP_AT = [(2, 0), (2, 1), (3, 0), (3, 1), (1, 1), (0, 0)]

        @block.sync
        def _(sp):
            def load_seg(c, k):
                src = bass.AP(x.tensor, c * (CH * L), [[STRIDE, N], [L, CH], [1, SEG]])
                sp.dma_start(seg[k][:], src).then_inc(seg_in[k], 16)

            load_seg(0, 0)
            load_seg(1, 1)
            sp.dma_start(seg_w[0:SEG, :], tok_W).then_inc(seg_w_loaded, 16)
            sp.dma_start(seg_w[SEG:SEG + 1, :], tok_b.unsqueeze(0)).then_inc(seg_w_loaded, 16)
            sp.dma_start(raw5[:, 4:5], effective_scale.unsqueeze(0).broadcast_to([P, 1])).then_inc(params_loaded, 16)
            for j, a in enumerate((alpha, beta, gamma, temperature)):
                sp.dma_start(raw5[:, j:j + 1], a.unsqueeze(0).broadcast_to([P, 1])).then_inc(params_loaded, 16)
            with sp.Fori(1, CHUNKS // 2) as i:
                for k in range(2):
                    sp.wait_ge(seg_freed[k], i)
                    load_seg(2 * i + k, k)
            sp.dma_start(w_heads[:], w_qkv[0:2 * INNER, :].rearrange("(g d) c -> d g c", d=DH)).then_inc(weights_loaded, 16)
            sp.dma_start(w_v[:], w_qkv[2 * INNER:3 * INNER, :].rearrange("(k p) c -> p k c", p=P)).then_inc(weights_loaded, 16)
            sp.dma_start(w_p[:], w_proj).then_inc(weights_loaded, 16)
            sp.dma_start(w_es[0:DE, :], w_e).then_inc(weights_loaded, 16)
            sp.dma_start(w_es[DE:DE + DS, :], w_s).then_inc(weights_loaded, 16)
            sp.dma_start(w_hy[:], w_h).then_inc(weights_loaded, 16)
            for k in range(2):
                sp.dma_start(be2[k * DE:(k + 1) * DE, :], b_e.unsqueeze(1)).then_inc(weights_loaded, 16)
                sp.dma_start(bs2[k * DS:(k + 1) * DS, :], b_s.unsqueeze(1)).then_inc(weights_loaded, 16)
            for k in range(4):
                sp.dma_start(bh4[k * DHY:(k + 1) * DHY, :], b_h.unsqueeze(1)).then_inc(weights_loaded, 16)
            sp.dma_start(bproj[:], b_proj.unsqueeze(0).broadcast_to([P, D])).then_inc(weights_loaded, 16)
            with sp.Fori(0, PAIRS) as p:
                sp.wait_ge(h2_ready, 2 * p + 2)
                dst = h2_dram[bass.ds(p * W2N, W2N), :].rearrange("(b n) c -> n b c", n=N)
                sp.dma_start(dst, h2_out[:]).then_inc(h2_saved, 16)
        WEIGHTS = 16 * 15
        PARAMS = 16 * 5

        @block.gpsimd
        def _(pool):
            pool.memset(ident[:], 0.0).then_inc(ident_zero, 1)
            pool.wait_ge(ident_zero, 1)
            pool.affine_select(out=ident[:], in_=ident[:], compare_op=ALU.not_equal, fill=1.0, base=0,
                               pattern=[[-1, P]], channel_multiplier=1).then_inc(ident_ready, 1)
            for t in (ek_m2, sk_n, hk_m2, block64, block32, pick2, pick4, pick4_32nd):
                last = pool.memset(t[:], 0.0)
            last.then_inc(consts_set, 1)
            pool.memset(quarter[:], 0.25).then_inc(consts_set, 1)
            pool.memset(v_aug[:, :, :, DH:DH + 1], 1.0).then_inc(consts_set, 1)
            pool.memset(shift_bias[:], float(NORM_SHIFT * np.log(2.0) / 2)).then_inc(consts_set, 1)

            def features(nxt):
                pool.wait_ge(eq_ready, nxt + 1)
                pool.wait_ge(e_filled, 2 * nxt)
                pool.tensor_tensor(eq_sq[:], eq[:], eq[:], ALU.mult).then_inc(eq_squared, 1)
                pool.wait_ge(sqf_ready, nxt + 1)
                pool.wait_ge(snq_filled, nxt)
                pool.tensor_tensor(s_sq[:, 0], s_raw[:, 0], s_raw[:, 0], ALU.mult).then_inc(s_squared, 1)
                pool.wait_ge(skf_ready, nxt + 1)
                pool.wait_ge(snk_filled, nxt)
                pool.tensor_tensor(s_sq[:, 1], s_raw[:, 1], s_raw[:, 1], ALU.mult).then_inc(s_squared, 1)

            def hyperbolic_features(nxt):
                pool.wait_ge(hk_spread, 4 * nxt + 4)
                pool.wait_ge(hdns_filled, 2 * nxt)
                pool.wait_ge(hk_den_ready, HT * nxt)
                pool.tensor_tensor(hk_sq4[:], hk_m2[:], hk_m2[:], ALU.mult).then_inc(hk_squared, 1)

            def scale_mq(nxt):
                pool.wait_ge(mq_ready, 2 * nxt + 2)
                pool.wait_ge(rden_ready, nxt + 1)
                pool.tensor_tensor(mq[:], mq[:], rden[:], ALU.mult).then_inc(mq_scaled, 1)

            def add_roots(cur):
                pool.wait_ge(hs_rooted, cur + 1)
                pool.wait_ge(hr_rooted, cur + 1)
                pool.tensor_tensor(hs[:], hs[:], hr[:], ALU.add).then_inc(g_ready, 1)

            def tangent(cur):
                pool.wait_ge(su_rooted, cur + 1)
                pool.wait_ge(w_ready, cur + 1)
                pool.tensor_tensor(su[:], su[:], sh[:], ALU.mult).then_inc(t_ready, 1)

            features(0)
            hyperbolic_features(0)
            scale_mq(0)
            with pool.Fori(0, PAIRS - 1) as p:
                add_roots(p)
                features(p + 1)
                tangent(p)
                hyperbolic_features(p + 1)
                scale_mq(p + 1)
            add_roots(PAIRS - 1)
            tangent(PAIRS - 1)

        @block.tensor
        def _(pe):
            pe.wait_ge(ident_ready, 1)
            pe.wait_ge(seg_w_loaded, 32)
            with pe.Fori(0, CHUNKS // 2) as i:
                for k in range(2):
                    pe.wait_ge(seg_in[k], 16 * i + 16)
                    pe.wait_ge(segT_ready, 2 * i + k)
                    for j in range(CH):
                        last = pe.matmul(banks[k][0:SEG, 0, j * N:(j + 1) * N], seg[k][:, j, :], ident[0:N, 0:N],
                                         start=True, stop=True)
                    last.then_inc(seg_freed[k], 1)
                    pe.wait_ge(segT_ready, 2 * i + k + 1)
                    pe.wait_ge(u_ready, 2 * i + k)
                    for j in range(CH):
                        last = pe.matmul(banks[2 + k][0:N, 0, j * D:(j + 1) * D], segT[k][:, j * N:(j + 1) * N],
                                         seg_w[:], start=True, stop=True)
                    last.then_inc(z_filled, 1)

            pe.wait_ge(weights_loaded, WEIGHTS)
            pe.wait_ge(segT_ready, CHUNKS)
            pe.wait_ge(u_ready, CHUNKS)
            pe.transpose(banks[0][0:DH, 0, 0:P], w_es[:], ident[:])
            pe.transpose(banks[0][0:DH, 0, P:FEAT], w_hy[:], ident[0:DHY, 0:DHY]).then_inc(w_turned, 1)
            for k in range(4):
                pe.transpose(banks[0][:, 1, k * P:(k + 1) * P], w_v[:, k, :], ident[:])
            for k in range(4):
                last = pe.transpose(banks[1][:, 0, k * P:(k + 1) * P], w_p[:, k * P:(k + 1) * P], ident[:])
            last.then_inc(wvp_turned, 1)
            pe.wait_ge(featT_ready, 1)
            for (g0, n), (sl, bk) in zip(COMP, COMP_AT):
                for j in range(n):
                    last = pe.matmul(banks[sl][:, bk, j * FEAT:(j + 1) * FEAT], w_heads[:, g0 + j, :], featT[:],
                                     start=True, stop=True)
                last.then_inc(comp_filled, 1)
            pe.wait_ge(comp_ready, len(COMP))
            pe.wait_ge(wvp_ready, 2)
            pe.wait_ge(picks_set, 16)

            def four(slot, comp, t0):
                for j in range(4):
                    last = pe.matmul(slot[:, j // 2, (j % 2) * W2N:(j % 2 + 1) * W2N],
                                     comp[:, (t0 + j) * P:(t0 + j + 1) * P], xT[:], start=True, stop=True)
                return last

            def features(nxt):
                sl = banks[0]
                pe.wait_ge(den_ready, 2 * nxt)
                pe.wait_ge(xn_ready, 2 * nxt + 2)
                for j in range(2):
                    last = pe.transpose(sl[:, 0, j * N:(j + 1) * N], xn[:, j, :], ident[0:N, 0:N])
                last.then_inc(xT_filled, 1)
                pe.wait_ge(xT_ready, nxt + 1)
                pe.wait_ge(mq_ready, 2 * nxt)
                four(banks[1], comp_e, 0).then_inc(eq_filled, 1)
                four(banks[2], comp_e, QT).then_inc(ek_filled, 1)
                four(banks[3], comp_s, 0).then_inc(sqf_filled, 1)
                four(banks[0], comp_s, QT).then_inc(skf_filled, 1)
                pe.wait_ge(ek_ready, 2 * nxt + 2)
                pe.wait_ge(sqf_ready, nxt + 1)
                for side, signal in enumerate((snq_filled, snk_filled)):
                    pe.wait_ge(s_squared, 2 * nxt + side + 1)
                    for j in range(2):
                        last = pe.matmul(banks[2 + side][:, j, 0:2 * W2N], block64[:], s_sq[:, side, 2 * j:2 * j + 2, :],
                                         start=True, stop=True)
                    last.then_inc(signal, 1)

            def values(nxt):
                pe.wait_ge(s_read, 2 * nxt + 1)
                pe.wait_ge(o_ready, 4 * nxt)
                for j in range(2):
                    last = pe.matmul(banks[2][0:N, j, 0:INNER], xT[:, j * N:(j + 1) * N], w_vT[:], start=True, stop=True)
                last.then_inc(v_filled, 1)

            def pair_out(sl, j, half):
                return sl[0:N, j, half * W2N:(half + 1) * W2N]

            def euclid_and_sphere(nxt):
                pe.wait_ge(eq_squared, nxt + 1)
                pe.wait_ge(ek_squared, nxt + 1)
                pe.wait_ge(skf_ready, nxt + 1)
                pe.wait_ge(eq_ready, nxt + 1)
                for b in range(2):
                    sl = banks[b]
                    tok = slice(b * N, (b + 1) * N)
                    for j in range(2):
                        for h in range(2):
                            o = sl[0:N, j, 0:4 * N].rearrange("p (t h m) -> p t h m", t=2, h=2)[:, :, h, :]
                            pe.matmul(o, pick2[:, h, :], ek_sq[:, 2 * j:2 * j + 2, tok], start=(h == 0),
                                      stop=False, skip_group_check=True)
                        for half in range(2):
                            t = 2 * j + half
                            pe.matmul(pair_out(sl, j, half), eq_sq[:, t, tok], pick2[:], start=False, stop=False,
                                      skip_group_check=True)
                            last = pe.matmul(pair_out(sl, j, half), eq[:, t, tok], ek_m2[:, t, :, tok],
                                             start=False, stop=(half == 1), skip_group_check=True)
                    last.then_inc(e_filled, 1)
                pe.wait_ge(sn_ready, 3 * nxt + 3)
                for b in range(2):
                    tok = slice(b * N, (b + 1) * N)
                    for t in range(QT):
                        last = pe.matmul(pair_out(banks[2 + b], t // 2, t % 2), sq_n[:, t, tok], sk_n[:, t, :, tok],
                                         start=True, stop=True)
                    last.then_inc(s_filled, 1)

            def hyperbolic_features(nxt):
                pe.wait_ge(e_read, 2 * nxt + 1)
                for side in range(2):
                    for j in range(HT):
                        t = side * HT + j
                        last = pe.matmul(banks[0][:, side, j * W2N:(j + 1) * W2N], comp_h[:, t * P:(t + 1) * P], xT[:],
                                         start=True, stop=True)
                last.then_inc(hf_filled, 1)
                pe.wait_ge(hq_squared, nxt + 1)
                pe.wait_ge(e_read, 2 * nxt + 2)
                pe.matmul(banks[1][:, 0, 0:HT * W2N], block32[:], hq_sq[:], start=True, stop=True).then_inc(un_filled, 1)

            def hyperbolic_scores(nxt):
                pe.wait_ge(un_ready, nxt + 1)
                pe.wait_ge(hk_den_ready, HT * nxt + HT)
                pe.wait_ge(s_read, 2 * nxt + 2)
                pe.wait_ge(v_placed, nxt + 1)
                pe.wait_ge(h2_ready, 2 * nxt)
                for b in range(2):
                    tok = slice(b * N, (b + 1) * N)
                    for t in range(HT):
                        last = pe.matmul(banks[2 * b][0:N, t, 0:4 * N], one_un[:, t, tok], hk_den[:, t, :, tok],
                                         start=True, stop=True)
                    last.then_inc(hden_filled, 1)
                    for t in range(HT):
                        o = banks[2 * b + 1][0:N, t, 0:4 * N]
                        pe.matmul(o, quarter[:], hk_sq4[:, t, :, tok], start=True, stop=False)
                        pe.matmul(o, hq_sq[:, t, tok], pick4[:], start=False, stop=False)
                        last = pe.matmul(o, hqk[:, 0, t, tok], hk_m2[:, t, :, tok], start=False, stop=True)
                    last.then_inc(hdns_filled, 1)

            def output(cur, last_pair=False):
                if last_pair:
                    pe.wait_ge(den_ready, 2 * cur + 2)
                    pe.wait_ge(mq_ready, 2 * cur + 2)
                else:
                    pe.wait_ge(s_read, 2 * cur + 4)
                    pe.wait_ge(hf_ready, cur + 2)
                    pe.wait_ge(un_ready, cur + 2)
                pe.wait_ge(exp_ready, cur + 1)
                pe.wait_ge(v_placed, cur + 1)
                for b, (kt, kp, kq) in enumerate(((2, 3, 0), (1, 2, 3))):
                    for h in range(HEADS):
                        last = pe.transpose(banks[kt][0:N, h // 4, (h % 4) * N:(h % 4 + 1) * N],
                                            dist[:, b, h * N:(h + 1) * N], ident[0:N, 0:N])
                    last.then_inc(attn_turned, 1)
                    pe.wait_ge(attnT_ready, 2 * cur + b + 1)
                    for h in range(HEADS):
                        last = pe.matmul(banks[kp][0:N, h // 4, (h % 4) * (DH + 1):(h % 4 + 1) * (DH + 1)],
                                         attnT[:, b, h * N:(h + 1) * N], v_aug[:, b, h, :], start=True, stop=True)
                    last.then_inc(pv_filled, 1)
                    pe.wait_ge(o_ready, 4 * cur + 2 * b + 2)
                    for k in range(4):
                        last = pe.transpose(banks[kq][:, 0, k * N:(k + 1) * N],
                                            o_tok[b][:, 2 * k:2 * k + 2, :].rearrange("p h d -> p (h d)"), ident[0:N, 0:N])
                    last.then_inc(o_turned, 1)
                    pe.wait_ge(oT_ready, 2 * cur + b + 1)
                    for k in range(4):
                        last = pe.matmul(banks[kq][0:N, 1, 0:D], oT[b][:, k, :], w_pT[:, k, :], start=(k == 0), stop=(k == 3))
                    last.then_inc(proj_filled, 1)

            features(0)
            euclid_and_sphere(0)
            hyperbolic_features(0)
            values(0)
            hyperbolic_scores(0)
            with pe.Fori(0, PAIRS - 1) as p:
                features(p + 1)
                euclid_and_sphere(p + 1)
                hyperbolic_features(p + 1)
                output(p)
                values(p + 1)
                hyperbolic_scores(p + 1)
            output(PAIRS - 1, last_pair=True)

        @block.scalar
        def _(act):
            act.wait_ge(params_loaded, PARAMS)
            act.activation(scale_t[:], raw5[:, 4:5], ACT.Tanh).then_inc(scale_ready, 1)
            act.activation(sp_abs[:], raw5[:, 0:4], ACT.Abs).then_inc(softplus_step, 1)
            act.wait_ge(softplus_step, 1)
            act.preload_act_table_set(SET_LN_EXP)
            act.activation(sp_abs[:], sp_abs[:], ACT.Exp, scale=-1.0).then_inc(softplus_step, 1)
            act.wait_ge(softplus_step, 2)
            act.activation(sp_abs[:], sp_abs[:], ACT.Ln, bias=1.0).then_inc(softplus_step, 1)
            act.wait_ge(scale_ready, 1)
            act.wait_ge(ones_set, 1)
            with act.Fori(0, CHUNKS // 2) as i:
                for k in range(2):
                    act.wait_ge(seg_freed[k], i + 1)
                    act.wait_ge(z_filled, 2 * i + k)
                    act.copy(segT[k][0:SEG, :], banks[k][0:SEG, 0, 0:CH * N]).then_inc(segT_ready, 1)
                    act.wait_ge(z_filled, 2 * i + k + 1)
                    act.activation(u[:, bass.ds((2 * i + k) * CH, CH), :].rearrange("n b d -> n (b d)"),
                                   banks[2 + k][0:N, 0, :], ACT.Copy, scale=scale_t[0:N, :]).then_inc(u_ready, 1)
            act.wait_ge(w_turned, 1)
            act.copy(featT[:], banks[0][0:DH, 0, 0:FEAT]).then_inc(featT_ready, 1)
            act.wait_ge(wvp_turned, 1)
            act.copy(w_vT[:], banks[0][:, 1, :]).then_inc(wvp_ready, 1)
            act.copy(w_pT[:].rearrange("p k c -> p (k c)"), banks[1][:, 0, :]).then_inc(wvp_ready, 1)
            for n, ((g0, m), (sl, bk)) in enumerate(zip(COMP, COMP_AT)):
                act.wait_ge(comp_filled, n + 1)
                src = banks[sl][:, bk, 0:m * FEAT].rearrange("p (g f) -> p g f", f=FEAT)
                for dst, a, w in ((comp_e, 0, DE), (comp_s, DE, DS), (comp_h, DE + DS, DHY)):
                    last = act.copy(dst[:, g0 * w:(g0 + m) * w].rearrange("p (g f) -> p g f", f=w), src[:, :, a:a + w])
                last.then_inc(comp_ready, 1)
            act.preload_act_table_set(SET_SQRT)
            act.wait_ge(stat_step, 8)
            act.activation(st["unorm"][:], st["norm"][:], ACT.Sqrt).then_inc(stat_root, 1)
            act.preload_act_table_set(SET_ATAN_TANH)
            act.wait_ge(stat_step, 9)
            act.activation(st["th"][:], st["norm"][:], ACT.Tanh).then_inc(stat_root, 1)
            act.preload_act_table_set(SET_SQRT)
            act.wait_ge(stat_step, 18)
            act.activation(st["std"][:], st["var"][:], ACT.Sqrt, bias=eps_bias[0:N, :]).then_inc(stat_root, 1)

            def flat(ap):
                return ap.rearrange("p a b -> p (a b)")

            def feature_evacuation(nxt):
                pe_out = [banks[k][:, :, 0:2 * W2N] for k in range(4)]

                def tiles(ap):
                    return ap.rearrange("p (j t) w -> p j (t w)", j=2)
                act.wait_ge(eq_filled, nxt + 1)
                act.wait_ge(e_filled, 2 * nxt)
                act.wait_ge(eq_squared, nxt)
                act.activation(tiles(eq[:]), pe_out[1], ACT.Identity, bias=be2[:]).then_inc(eq_ready, 1)
                act.wait_ge(ek_filled, nxt + 1)
                act.activation(tiles(ek_sq[:]), pe_out[2], ACT.Square, bias=be2[:]).then_inc(ek_squared, 1)
                act.wait_ge(sqf_filled, nxt + 1)
                act.wait_ge(sn_ready, 3 * nxt)
                act.activation(tiles(s_raw[:, 0]), pe_out[3], ACT.Identity, bias=bs2[:]).then_inc(sqf_ready, 1)
                act.wait_ge(skf_filled, nxt + 1)
                act.activation(tiles(s_raw[:, 1]), pe_out[0], ACT.Identity, bias=bs2[:]).then_inc(skf_ready, 1)

            def inverse_norms(nxt):
                f = s_inv[:].rearrange("p a b c -> p (a b c)")
                act.wait_ge(s_norm_ready, 2 * nxt + 2)
                act.activation(f, f, ACT.Ln).then_inc(s_inv_step, 1)
                act.wait_ge(s_inv_step, nxt + 1)
                act.activation(f, f, ACT.Exp, scale=-0.5, bias=shift_bias[:]).then_inc(s_inv_ready, 1)

            def hyperbolic_evacuation(nxt):
                act.wait_ge(hf_filled, nxt + 1)
                act.wait_ge(hdns_filled, 2 * nxt)
                act.activation(hqk[:].rearrange("p a b c -> p a (b c)"), banks[0][:, :, 0:HT * W2N], ACT.Tanh,
                               bias=bh4[:]).then_inc(hf_ready, 1)
                act.wait_ge(hf_ready, nxt + 1)
                act.activation(flat(hq_sq[:]), flat(hqk[:, 0]), ACT.Square).then_inc(hq_squared, 1)

            def inverse_denominators(nxt):
                act.wait_ge(den_ready, 2 * nxt + 2)
                act.wait_ge(mq_scaled, nxt)
                act.activation(flat(rden[:]), flat(den[:]), ACT.Ln).then_inc(rden_step, 1)
                act.wait_ge(rden_step, nxt + 1)
                act.activation(flat(rden[:]), flat(rden[:]), ACT.Exp, scale=-1.0).then_inc(rden_ready, 1)

            def roots(cur):
                act.wait_ge(e_read, 2 * cur + 2)
                act.wait_ge(attn_turned, 2 * cur)
                act.activation(flat(dist[:]), flat(esb[:]), ACT.Sqrt, scale=c_e2[0:N, :]).then_inc(dist_rooted, 1)
                act.wait_ge(s_read, 2 * cur + 2)
                act.wait_ge(dist_hs, cur)
                act.activation(flat(su[:]), flat(csb[:]), ACT.Sqrt, scale=-0.5, bias=0.5).then_inc(su_rooted, 1)
                act.activation(flat(sh[:]), flat(csb[:]), ACT.Sqrt, scale=0.5, bias=0.5).then_inc(sh_rooted, 1)
                act.wait_ge(q_ready, cur + 1)
                act.activation(flat(hs[:]), flat(mq[:]), ACT.Sqrt).then_inc(hs_rooted, 1)
                act.activation(flat(hr[:]), flat(mq[:]), ACT.Sqrt, bias=1.0).then_inc(hr_rooted, 1)

            def logs(cur):
                act.wait_ge(sh_rooted, cur + 1)
                act.activation(flat(sh[:]), flat(sh[:]), ACT.Ln, bias=1.0).then_inc(w_step, 1)
                act.wait_ge(w_step, cur + 1)
                act.activation(flat(sh[:]), flat(sh[:]), ACT.Exp, scale=-1.0).then_inc(w_ready, 1)
                act.wait_ge(g_ready, cur + 1)
                act.activation(flat(hs[:]), flat(hs[:]), ACT.Ln).then_inc(log_ready, 1)

            def arctangent(cur):
                act.wait_ge(t_ready, cur + 1)
                act.activation(flat(su[:]), flat(su[:]), ACT.Arctan).then_inc(atan_ready, 1)

            def exponent(cur):
                act.wait_ge(dist_shifted, cur + 1)
                act.activation(flat(dist[:]), flat(dist[:]), ACT.Exp).then_inc(exp_ready, 1)
                for b, k in enumerate((2, 1)):
                    act.wait_ge(attn_turned, 2 * cur + b + 1)
                    act.copy(attnT[:, b, :].rearrange("p (j w) -> p j w", j=2),
                             banks[k][0:N, :, 0:4 * N]).then_inc(attnT_ready, 1)

            act.wait_ge(weights_loaded, WEIGHTS)
            feature_evacuation(0)
            act.preload_act_table_set(SET_LN_EXP)
            inverse_norms(0)
            act.preload_act_table_set(SET_ATAN_TANH)
            hyperbolic_evacuation(0)
            act.preload_act_table_set(SET_LN_EXP)
            inverse_denominators(0)
            act.wait_ge(c_ready, 1)
            with act.Fori(0, PAIRS - 1) as p:
                act.preload_act_table_set(SET_SQRT)
                roots(p)
                feature_evacuation(p + 1)
                act.preload_act_table_set(SET_LN_EXP)
                logs(p)
                inverse_norms(p + 1)
                act.preload_act_table_set(SET_ATAN_TANH)
                arctangent(p)
                hyperbolic_evacuation(p + 1)
                act.preload_act_table_set(SET_LN_EXP)
                exponent(p)
                inverse_denominators(p + 1)
            act.preload_act_table_set(SET_SQRT)
            roots(PAIRS - 1)
            act.preload_act_table_set(SET_LN_EXP)
            logs(PAIRS - 1)
            act.preload_act_table_set(SET_ATAN_TANH)
            arctangent(PAIRS - 1)
            act.preload_act_table_set(SET_LN_EXP)
            exponent(PAIRS - 1)

        @block.vector
        def _(dve):
            dve.memset(eps_bias[:], LN_EPS)
            dve.wait_ge(consts_set, 4)
            for k in range(2):
                dve.memset(block64[64 * k:64 * k + 64, 64 * k:64 * k + 64], 1.0).then_inc(picks_set, 1)
                dve.memset(pick2[64 * k:64 * k + 64, k, :], 1.0).then_inc(picks_set, 1)
            for k in range(4):
                r = slice(32 * k, 32 * k + 32)
                dve.memset(block32[r, 32 * k:32 * k + 32], 1.0).then_inc(picks_set, 1)
                dve.memset(pick4[r, k, :], 1.0).then_inc(picks_set, 1)
                dve.memset(pick4_32nd[r, k, :], 1.0 / 32).then_inc(picks_set, 1)
            for k in range(2):
                last = dve.memset(segT[k][:], 1.0)
            last.then_inc(ones_set, 1)
            with dve.Fori(0, CHUNKS) as c:
                dve.wait_ge(u_ready, c + 1)
                for j in range(CH):
                    dve.bn_stats(stats[:, bass.ds(c * CH + j, 1), :].rearrange("n b k -> n (b k)"),
                                 u[:, bass.ds(c * CH + j, 1), :].rearrange("n b d -> n (b d)")).then_inc(stats_ready, 1)

            dve.wait_ge(softplus_step, 3)
            dve.scalar_tensor_tensor(sp[:], raw5[:, 0:4], 0.0, sp_abs[:], ALU.max, ALU.add).then_inc(softplus_step, 1)
            dve.wait_ge(softplus_step, 4)
            dve.reciprocal(sp_abs[:, 3:4], sp[:, 3:4]).then_inc(softplus_step, 1)
            dve.wait_ge(softplus_step, 5)
            dve.tensor_scalar(c_e2[:], sp[:, 0:1], sp_abs[:, 3:4], None, ALU.mult).then_inc(softplus_step, 1)
            dve.tensor_scalar(c_s[:], sp[:, 1:2], sp_abs[:, 3:4], 4.0, ALU.mult, ALU.mult).then_inc(softplus_step, 1)
            dve.tensor_scalar(c_h[:], sp[:, 2:3], sp_abs[:, 3:4], 2.0, ALU.mult, ALU.mult).then_inc(softplus_step, 1)
            dve.wait_ge(softplus_step, 8)
            dve.tensor_tensor(c_e2[:], c_e2[:], c_e2[:], ALU.mult).then_inc(c_ready, 1)

            half = D // 2
            step = [0]

            def done(ins):
                step[0] += 1
                ins.then_inc(stat_step, 1)
                dve.wait_ge(stat_step, step[0])

            dve.wait_ge(stats_ready, B)
            me, mo, ve, vo = stats[:, :, 1], stats[:, :, 4], stats[:, :, 2], stats[:, :, 5]
            done(dve.tensor_tensor(st["sum"][:], me, mo, ALU.add))
            done(dve.tensor_tensor(st["diff"][:], me, mo, ALU.subtract))
            done(dve.tensor_tensor(st["diff"][:], st["diff"][:], st["diff"][:], ALU.mult))
            done(dve.tensor_tensor(st["m2"][:], ve, vo, ALU.add))
            done(dve.scalar_tensor_tensor(st["m2"][:], st["diff"][:], half / 2.0, st["m2"][:], ALU.mult, ALU.add))
            done(dve.tensor_scalar(st["mean"][:], st["sum"][:], 0.5, None, ALU.mult))
            done(dve.tensor_tensor(st["sq"][:], st["mean"][:], st["mean"][:], ALU.mult))
            done(dve.scalar_tensor_tensor(st["norm"][:], st["sq"][:], float(D), st["m2"][:], ALU.mult, ALU.add))
            dve.wait_ge(stat_root, 1)
            done(dve.tensor_scalar(st["norm"][:], st["unorm"][:], MIN_NORM, None, ALU.max))
            done(dve.reciprocal(st["f"][:], st["norm"][:]))
            dve.wait_ge(stat_root, 2)
            done(dve.tensor_tensor(st["f"][:], st["f"][:], st["th"][:], ALU.mult))
            done(dve.tensor_tensor(st["yn"][:], st["f"][:], st["unorm"][:], ALU.mult))
            done(dve.tensor_scalar(st["yn"][:], st["yn"][:], MIN_NORM, None, ALU.max))
            done(dve.reciprocal(st["clip"][:], st["yn"][:]))
            done(dve.tensor_scalar(st["clip"][:], st["clip"][:], 1.0 - BALL_EPS, 1.0, ALU.mult, ALU.min))
            done(dve.tensor_tensor(st["f"][:], st["f"][:], st["clip"][:], ALU.mult))
            done(dve.tensor_tensor(st["var"][:], st["f"][:], st["f"][:], ALU.mult))
            done(dve.scalar_tensor_tensor(st["var"][:], st["var"][:], 1.0 / D, st["m2"][:], ALU.mult, ALU.mult))
            dve.wait_ge(stat_root, 3)
            done(dve.reciprocal(st["std"][:], st["std"][:]))
            done(dve.tensor_tensor(st["gain"][:], st["std"][:], st["f"][:], ALU.mult))
            done(dve.scalar_tensor_tensor(st["shift"][:], st["gain"][:], -1.0, st["mean"][:], ALU.mult, ALU.mult))

            def tiles(ap):
                return ap.rearrange("p (j t) w -> p j (t w)", j=2)

            def flat(ap):
                return ap.rearrange("p a b -> p (a b)")

            def normalise(nxt):
                dve.wait_ge(xT_filled, nxt)
                for j in range(2):
                    b = 2 * nxt + j
                    dve.tensor_scalar(xn[:, j, :], u[:, bass.ds(b, 1), :].rearrange("n b d -> n (b d)"), st["gain"][:, bass.ds(b, 1)],
                                      st["shift"][:, bass.ds(b, 1)], ALU.mult, ALU.add).then_inc(xn_ready, 1)
                dve.wait_ge(xT_filled, nxt + 1)
                dve.wait_ge(hf_filled, nxt)
                dve.wait_ge(v_filled, nxt)
                dve.tensor_copy(xT[:], banks[0][:, 0, 0:W2N]).then_inc(xT_ready, 1)

            def key_evacuation(nxt):
                dve.wait_ge(ek_squared, nxt + 1)
                dve.wait_ge(e_filled, 2 * nxt)
                for h in range(2):
                    r = slice(64 * h, 64 * h + 64)
                    dve.tensor_scalar(ek_m2[r, :, h, :].rearrange("p (j t) w -> p j t w", j=2),
                                      banks[2][r, :, 0:2 * W2N].rearrange("p j (t w) -> p j t w", t=2),
                                      be2[r, :], -2.0, ALU.add, ALU.mult).then_inc(ek_ready, 1)

            def guarded_norms(nxt):
                dve.wait_ge(sn_ready, 3 * nxt)
                for side, k, signal in ((0, 2, snq_filled), (1, 3, snk_filled)):
                    dve.wait_ge(signal, nxt + 1)
                    dve.tensor_scalar(tiles(s_inv[:, side]), banks[k][:, :, 0:2 * W2N], 1e-24,
                                      2.0 ** NORM_SHIFT, ALU.max, ALU.mult).then_inc(s_norm_ready, 1)

            def unit_features(nxt):
                dve.wait_ge(s_inv_ready, nxt + 1)
                dve.wait_ge(s_filled, 2 * nxt)
                dve.tensor_tensor(sq_n[:], s_raw[:, 0], s_inv[:, 0], ALU.mult).then_inc(sn_ready, 1)
                for h in range(2):
                    r = slice(64 * h, 64 * h + 64)
                    dve.tensor_tensor(sk_n[r, :, h, :], s_raw[r, 1], s_inv[r, 1], ALU.mult).then_inc(sn_ready, 1)

            def scores_to_sbuf(nxt):
                dve.wait_ge(dist_rooted, nxt)
                for b in range(2):
                    dve.wait_ge(e_filled, 2 * nxt + b + 1)
                    dve.tensor_scalar(esb[:, b, :].rearrange("p (j w) -> p j w", j=2), banks[b][0:N, :, 0:4 * N],
                                      1e-12, None, ALU.max).then_inc(e_read, 1)
                dve.wait_ge(sh_rooted, nxt)
                for b in range(2):
                    dve.wait_ge(s_filled, 2 * nxt + b + 1)
                    dve.tensor_scalar(csb[:, b, :].rearrange("p (j w) -> p j w", j=2), banks[2 + b][0:N, :, 0:4 * N],
                                      -SIM_MAX, SIM_MAX, ALU.max, ALU.min).then_inc(s_read, 1)

            def hyperbolic_features(nxt):
                dve.wait_ge(hf_ready, nxt + 1)
                dve.wait_ge(hdns_filled, 2 * nxt)
                dve.wait_ge(hk_squared, nxt)
                for h in range(4):
                    r = slice(32 * h, 32 * h + 32)
                    dve.tensor_scalar(hk_m2[r, :, h, :], hqk[r, 1], -2.0, None, ALU.mult).then_inc(hk_spread, 1)
                dve.wait_ge(un_filled, nxt + 1)
                dve.tensor_scalar(flat(one_un[:]), banks[1][:, 0, 0:HT * W2N], -1.0, 1.0, ALU.mult, ALU.add)\
                   .then_inc(un_ready, 1)
                dve.wait_ge(hk_squared, nxt + 1)
                for t in range(HT):
                    dve.scalar_tensor_tensor(flat(hk_den[:, t]), flat(hk_sq4[:, t]), -0.25, flat(pick4_32nd[:]),
                                             ALU.mult, ALU.add).then_inc(hk_den_ready, 1)

            def hyperbolic_scores(nxt):
                for b in range(2):
                    dve.wait_ge(hden_filled, 2 * nxt + b + 1)
                    if b == 0:
                        dve.wait_ge(rden_step, nxt)
                        dve.wait_ge(hr_rooted, nxt)
                    dve.tensor_scalar(den[:, b, :].rearrange("p (j w) -> p j w", j=2), banks[2 * b][0:N, :, 0:4 * N],
                                      1e-8, TINY, ALU.add, ALU.max).then_inc(den_ready, 1)
                    dve.wait_ge(hdns_filled, 2 * nxt + b + 1)
                    dve.wait_ge(den_ready, 2 * nxt + b + 1)
                    dve.scalar_tensor_tensor(mq[:, b, :].rearrange("p (j w) -> p j w", j=2),
                                             den[:, b, :].rearrange("p (j w) -> p j w", j=2), TINY,
                                             banks[2 * b + 1][0:N, :, 0:4 * N], ALU.is_gt, ALU.mult)\
                       .then_inc(mq_ready, 1)

            def place_values(nxt):
                dve.wait_ge(v_filled, nxt + 1)
                dve.wait_ge(pv_filled, 2 * nxt)
                dve.tensor_copy(v_aug[:, :, :, 0:DH], banks[2][0:N, :, :].rearrange("n b (h d) -> n b h d", d=DH))\
                   .then_inc(v_placed, 1)

            def clamp_q(cur):
                dve.wait_ge(mq_scaled, cur + 1)
                dve.tensor_scalar(flat(mq[:]), flat(mq[:]), ARG_MIN_HALF, None, ALU.max).then_inc(q_ready, 1)

            def add_hyperbolic(cur):
                dve.wait_ge(dist_rooted, cur + 1)
                dve.wait_ge(log_ready, cur + 1)
                dve.scalar_tensor_tensor(flat(dist[:]), flat(hs[:]), c_h[0:N, :], flat(dist[:]), ALU.mult,
                                         ALU.add).then_inc(dist_h, 1)

            def add_spherical(cur):
                dve.wait_ge(dist_h, cur + 1)
                dve.wait_ge(atan_ready, cur + 1)
                dve.scalar_tensor_tensor(flat(dist[:]), flat(su[:]), c_s[0:N, :], flat(dist[:]), ALU.mult,
                                         ALU.add).then_inc(dist_hs, 1)
                dve.wait_ge(dist_hs, cur + 1)
                dve.tensor_reduce(dmin[:], flat(dist[:]).rearrange("p (h m) -> p h m", m=N), AX, ALU.min)\
                   .then_inc(dmin_ready, 1)
                dve.wait_ge(dmin_ready, cur + 1)
                d3 = flat(dist[:]).rearrange("p (h m) -> p h m", m=N)
                dve.tensor_tensor(d3, dmin[:].unsqueeze(2).broadcast_to([N, 2 * HEADS, N]), d3, ALU.subtract)\
                   .then_inc(dist_shifted, 1)

            def output(cur):
                for b, (kp, kq) in enumerate(((3, 0), (2, 3))):
                    n = 2 * cur + b
                    dve.wait_ge(pv_filled, n + 1)
                    pv = banks[kp][0:N, :, 0:4 * (DH + 1)].rearrange("p j (h d) -> p j h d", h=4)
                    dve.reciprocal(rsum[:, b, :].rearrange("p (j h) -> p j h", j=2), pv[:, :, :, DH]).then_inc(rsum_ready, 1)
                    dve.wait_ge(rsum_ready, n + 1)
                    dve.wait_ge(o_turned, 2 * cur)
                    for j in range(2):
                        dve.tensor_tensor(o_tok[b][:, 4 * j:4 * j + 4, :], pv[:, j, :, 0:DH],
                                          rsum[:, b, 4 * j:4 * j + 4].unsqueeze(2).broadcast_to([N, 4, DH]),
                                          ALU.mult).then_inc(o_ready, 1)
                    dve.wait_ge(o_turned, n + 1)
                    dve.wait_ge(proj_filled, 2 * cur)
                    dve.tensor_copy(flat(oT[b][:]), banks[kq][:, 0, 0:4 * N]).then_inc(oT_ready, 1)
                    if b == 0:
                        dve.wait_ge(h2_saved, 16 * cur)
                    dve.scalar_tensor_tensor(hres[:, b, :], u[:, bass.ds(n, 1), :].rearrange("p a d -> p (a d)"),
                                             st["f"][:, bass.ds(n, 1)], bproj[0:N, :], ALU.mult, ALU.add)\
                       .then_inc(hres_ready, 1)
                    dve.wait_ge(hres_ready, n + 1)
                    dve.wait_ge(proj_filled, n + 1)
                    dve.tensor_tensor(h2_out[:, b, :], banks[kq][0:N, 1, 0:D], hres[:, b, :], ALU.add)\
                       .then_inc(h2_ready, 1)

            normalise(0)
            key_evacuation(0)
            guarded_norms(0)
            unit_features(0)
            scores_to_sbuf(0)
            hyperbolic_features(0)
            place_values(0)
            hyperbolic_scores(0)
            with dve.Fori(0, PAIRS - 1) as p:
                clamp_q(p)
                normalise(p + 1)
                key_evacuation(p + 1)
                guarded_norms(p + 1)
                add_hyperbolic(p)
                unit_features(p + 1)
                add_spherical(p)
                scores_to_sbuf(p + 1)
                hyperbolic_features(p + 1)
                output(p)
                place_values(p + 1)
                hyperbolic_scores(p + 1)
            clamp_q(PAIRS - 1)
            add_hyperbolic(PAIRS - 1)
            add_spherical(PAIRS - 1)
            output(PAIRS - 1)


def experts(nc, dims, banks, ident, h2, h2_dram, h2_saved, Wr, W1, b1, W2, b2, out):
    D, T, E, F, NT, NB, TPB, FC, PAIRS = dims
    REPS = P // E
    AHEAD = 2
    SHIFTS = [26, 22, 18, 14, 10, 6, 2, 0]
    ROUNDS = len(SHIFTS)
    THIRD = NT // 3
    with ExitStack() as ctx:
        def sb(name, shape, dt=F32):
            return ctx.enter_context(nc.sbuf_tensor(name, shape, dt))

        x2 = sb("x2", [P, NT, D])
        x2T = sb("x2T", [P, T])
        w1 = [sb(f"w1_{k}", [D, F]) for k in range(2)]
        w2 = [sb(f"w2_{k}", [P, FC, D]) for k in range(2)]
        b1_rows = sb("b1_rows", [E * FC, P])
        b1T = sb("b1T", [P, E * FC])
        b2_sb = sb("b2_sb", [E, D])
        wr = sb("wr", [D, E])
        wr_reps = sb("wr_reps", [D, REPS, E])
        hid = [sb(f"hid{c}", [P, TB]) for c in range(FC)]
        ahead = sb("ahead", [P, AHEAD, NT, D])
        acc = sb("acc", [P, NT, D])
        stats = sb("stats2", [P, NT, 6])
        st = {n: sb(f"st2_{n}", [P, NT]) for n in ("sum", "diff", "m2", "mean", "std", "shift")}
        eps2 = sb("eps2", [P, 1])
        probs = sb("probs", [P, T])
        above = sb("above", [P, T])
        ties = sb("ties", [E, T])
        ranks = sb("ranks", [E, T])
        gate = sb("gate", [P, NT, E])
        bmax = sb("bmax", [P, NB])
        nmax = sb("nmax", [P, 1])
        bsum = sb("bsum", [P, NB])
        psum_inv = sb("psum_inv", [P, 1])
        same = sb("same", [P, P])
        iota = sb("iota", [P, P], I32)
        rep = sb("rep", [P, 1], I32)
        trial = sb("trial", [P, ROUNDS], I32)
        low = sb("low", [P, 1], I32)
        thr = sb("thr", [P, 1], I32)
        count = sb("count", [P, 1])
        enough = sb("enough", [P, 1])
        digit = sb("digit", [P, 1], I32)
        need = sb("need", [P, 1])

        def sem(name):
            return ctx.enter_context(nc.semaphore(name + "2"))

        (h2_loaded, router_loaded, bias_loaded, iota_set, eps_set, sel_const, stats_ready, stat_step, std_rooted,
         x2_ready, x2_turned, x2T_ready, b1_turned, b1T_ready, logits_filled, bmax_ready, nmax_ready, exp_ready,
         psum_step, probs_ready, thr_ready, counted, enough_ready, digits_filled, digit_ready, low_ready,
         gate_step, gates_ready, gates_turned, gate_ready, bias_filled, hid_filled, hid_ready, y_filled, y_kept,
         acc_ready, y_added, out_stored) = (
             sem(n) for n in """h2_loaded router_loaded bias_loaded iota_set eps_set sel_const stats_ready stat_step std_rooted
                 x2_ready x2_turned x2T_ready b1_turned b1T_ready logits_filled bmax_ready nmax_ready exp_ready
                 psum_step probs_ready thr_ready counted enough_ready digits_filled digit_ready low_ready
                 gate_step gates_ready gates_turned gate_ready bias_filled hid_filled hid_ready y_filled y_kept
                 acc_ready y_added out_stored""".split())
        w_in = [ctx.enter_context(nc.semaphore(f"experts_in{k}")) for k in range(2)]
        block = ctx.enter_context(nc.Block())
        hid_bank = [banks[c // 2][:, c % 2, 0:TB] for c in range(FC)]
        y_bank = banks[2][:, 0, :]
        count_bank = banks[2][:, 1, :]
        gate_bank = banks[3][:, 0, 0:NT * E]
        seven = [banks[k // 2][:, k % 2, :] for k in range(8)]
        h2_rows = h2_dram.rearrange("(t p) c -> p t c", p=P)

        @block.sync
        def _(sp):
            sp.dma_start(wr[:], Wr).then_inc(router_loaded, 16)
            sp.dma_start(b1_rows[:], b1.rearrange("e (c p) -> (e c) p", p=P)).then_inc(bias_loaded, 16)
            sp.dma_start(b2_sb[:], b2).then_inc(bias_loaded, 16)
            for e in range(2):
                sp.dma_start(w1[e][:], W1[e]).then_inc(w_in[e], 16)
                sp.dma_start(w2[e][:], W2[e].rearrange("(c p) d -> p c d", p=P)).then_inc(w_in[e], 16)
            sp.wait_ge(h2_saved, 16 * PAIRS)
            for c in range(3):
                sp.dma_start(h2[:, c * THIRD:(c + 1) * THIRD, :], h2_rows[:, c * THIRD:(c + 1) * THIRD, :])\
                  .then_inc(h2_loaded, 16)
            with sp.Fori(1, E // 2) as i:
                for k in range(2):
                    sp.wait_ge(y_filled, (2 * i + k - 1) * NB)
                    sp.dma_start(w1[k][:], W1[bass.ds(2 * i + k, 1)].rearrange("e d f -> d (e f)")).then_inc(w_in[k], 16)
                    sp.dma_start(w2[k][:], W2[bass.ds(2 * i + k, 1)].rearrange("e (c p) d -> p (e c) d", p=P))\
                      .then_inc(w_in[k], 16)
            sp.wait_ge(y_added, (E - AHEAD) * NT)
            sp.dma_start(out.rearrange("b n c -> (b n) c").rearrange("(t p) c -> p t c", p=P), acc[:]).then_inc(out_stored, 16)
            sp.wait_ge(out_stored, 16)

        @block.gpsimd
        def _(pool):
            pool.iota(iota[:], [[1, P]], base=P, channel_multiplier=-1).then_inc(iota_set, 1)
            pool.iota(rep[:], [[0, 1]], base=0, channel_multiplier=1).then_inc(iota_set, 1)

        @block.tensor
        def _(pe):
            pe.wait_ge(bias_loaded, 32)
            pe.transpose(seven[7][:, 0:E * FC], b1_rows[:], ident[0:E * FC, 0:E * FC]).then_inc(b1_turned, 1)
            for t in range(NT):
                pe.wait_ge(x2_ready, t + 1)
                last = pe.transpose(seven[t // 4][:, (t % 4) * P:(t % 4 + 1) * P], x2[:, t, :], ident[:])
                if t % 4 == 3 or t == NT - 1:
                    last.then_inc(x2_turned, 1)
            for n in range(NB):
                pe.wait_ge(x2T_ready, (NT + 3) // 4)
                pe.matmul(seven[n][:, 0:TB], wr_reps[:].rearrange("p r e -> p (r e)"), x2T[:, n * TB:(n + 1) * TB],
                          start=True, stop=True).then_inc(logits_filled, 1)

            def ffn_block(n, e_blocks, w1e, w2e):
                for c in range(FC):
                    pe.matmul(hid_bank[c], w1e[:, c * P:(c + 1) * P], x2T[:, bass.ds(n * TB, TB)], start=True,
                              stop=True).then_inc(hid_filled, 1)
                for c in range(FC):
                    pe.wait_ge(hid_ready, FC * e_blocks + c + 1)
                    for t in range(TPB):
                        last = pe.matmul(y_bank[:, t * D:(t + 1) * D], hid[c][:, t * P:(t + 1) * P], w2e[:, c, :],
                                         start=(c == 0 and t == 0), stop=(c == FC - 1), skip_group_check=True)
                last.then_inc(y_filled, 1)

            pe.wait_ge(exp_ready, NB)
            pe.wait_ge(b1T_ready, 1)
            for e in range(AHEAD):
                pe.wait_ge(w_in[e], 32)
                with pe.Fori(0, NB) as n:
                    if e == 0:
                        pe.wait_ge(y_kept, n)
                        ffn_block(n, n, w1[e], w2[e])
                        pe.wait_ge(enough_ready, n + 1)
                        pe.matmul(count_bank[:, 0:1], same[:], enough[:], start=True, stop=True).then_inc(digits_filled, 1)
                    else:
                        pe.wait_ge(y_kept, NB * e + n)
                        ffn_block(n, NB * e + n, w1[e], w2[e])
                if e == 0:
                    for r in range(NB, ROUNDS):
                        pe.wait_ge(enough_ready, r + 1)
                        pe.matmul(count_bank[:, 0:1], same[:], enough[:], start=True, stop=True).then_inc(digits_filled, 1)
            pe.wait_ge(gates_ready, 1)
            for t in range(NT):
                last = pe.transpose(gate_bank[:, t * E:(t + 1) * E], above[0:E, t * P:(t + 1) * P], ident[0:E, 0:E])
            last.then_inc(gates_turned, 1)
            pe.wait_ge(y_kept, AHEAD * NB)
            free = [banks[3][:, 1, :], banks[2][:, 1, :]]
            for g in range((NT + 3) // 4):
                if g >= 2:
                    pe.wait_ge(acc_ready, g - 1)
                for t in range(4 * g, min(4 * g + 4, NT)):
                    last = pe.matmul(free[g % 2][:, (t % 4) * D:(t % 4 + 1) * D], above[0:E, t * P:(t + 1) * P], b2_sb[:],
                                     start=True, stop=True)
                last.then_inc(bias_filled, 1)
            with pe.Fori(AHEAD // 2, E // 2) as i:
                for k in range(2):
                    with pe.Fori(0, NB) as n:
                        pe.wait_ge(w_in[k], 32 * i + 32)
                        before = i * (2 * NB) + k * NB + n
                        pe.wait_ge(y_added, (before - AHEAD * NB) * TPB)
                        ffn_block(n, before, w1[k], w2[k])

        @block.scalar
        def _(act):
            act.preload_act_table_set(SET_SQRT)
            act.wait_ge(b1_turned, 1)
            act.copy(b1T[:], seven[7][:, 0:E * FC]).then_inc(b1T_ready, 1)
            act.wait_ge(stat_step, 5)
            act.wait_ge(eps_set, 1)
            act.activation(st["std"][:], st["m2"][:], ACT.Sqrt, scale=1.0 / D, bias=eps2[:]).then_inc(std_rooted, 1)
            for g in range((NT + 3) // 4):
                n = min(4, NT - 4 * g)
                act.wait_ge(x2_turned, g + 1)
                act.copy(x2T[:, 4 * g * P:(4 * g + n) * P], seven[g][:, 0:n * P]).then_inc(x2T_ready, 1)
            act.preload_act_table_set("exp_and_others")
            act.wait_ge(nmax_ready, 1)
            for n in range(NB):
                act.activation(probs[:, n * TB:(n + 1) * TB], seven[n][:, 0:TB], ACT.Exp, bias=nmax[:],
                               accum_out=bsum[:, n:n + 1]).then_inc(exp_ready, 1)
            act.preload_act_table_set("gelu_and_others")

            def gelus(e, before):
                for c in range(FC):
                    act.wait_ge(hid_filled, FC * before + c + 1)
                    if c == 0:
                        act.wait_ge(y_filled, before)
                    act.activation(hid[c][:], hid_bank[c], ACT.Gelu, bias=b1T[:, bass.ds(e * FC + c, 1)])\
                       .then_inc(hid_ready, 1)

            for e in range(AHEAD):
                with act.Fori(0, NB) as n:
                    gelus(e, NB * e + n)
                    act.wait_ge(y_filled, NB * e + n + 1)
                    act.copy(ahead[:, e, bass.ds(n * TPB, TPB), :].rearrange("p t d -> p (t d)"),
                             y_bank[:, 0:TB]).then_inc(y_kept, 1)
            with act.Fori(AHEAD, E) as e:
                with act.Fori(0, NB) as n:
                    gelus(e, e * NB + n)

        @block.vector
        def _(dve):
            dve.memset(eps2[:], LN_EPS).then_inc(eps_set, 1)
            consts = [0]

            def const(ins):
                consts[0] += 1
                ins.then_inc(sel_const, 1)
                dve.wait_ge(sel_const, consts[0])

            dve.wait_ge(iota_set, 2)
            const(dve.tensor_scalar(iota[:], iota[:], E - 1, None, ALU.bitwise_and))
            const(dve.tensor_scalar(same[:], iota[:], 0.0, None, ALU.is_equal))
            const(dve.tensor_scalar(rep[:], rep[:], int(np.log2(E)), None, ALU.logical_shift_right))
            for r, shift in enumerate(SHIFTS[:-1]):
                dve.tensor_scalar(trial[:, r:r + 1], rep[:], shift, None, ALU.logical_shift_left)
            dve.tensor_scalar(trial[:, ROUNDS - 1:ROUNDS], rep[:], 2, None, ALU.logical_shift_right)
            const(dve.memset(low[:], 0))
            dve.wait_ge(router_loaded, 16)
            const(dve.tensor_copy(wr_reps[:], wr[:].unsqueeze(1).broadcast_to([D, REPS, E])))

            step = [0]

            def done(ins):
                step[0] += 1
                ins.then_inc(stat_step, 1)
                dve.wait_ge(stat_step, step[0])

            for c in range(3):
                dve.wait_ge(h2_loaded, 48)
                for t in range(c * THIRD, (c + 1) * THIRD):
                    dve.bn_stats(stats[:, t, :], h2[:, t, :]).then_inc(stats_ready, 1)
            dve.wait_ge(stats_ready, NT)
            me, mo, ve, vo = stats[:, :, 1], stats[:, :, 4], stats[:, :, 2], stats[:, :, 5]
            done(dve.tensor_tensor(st["sum"][:], me, mo, ALU.add))
            done(dve.tensor_tensor(st["diff"][:], me, mo, ALU.subtract))
            done(dve.tensor_tensor(st["diff"][:], st["diff"][:], st["diff"][:], ALU.mult))
            done(dve.tensor_tensor(st["m2"][:], ve, vo, ALU.add))
            done(dve.scalar_tensor_tensor(st["m2"][:], st["diff"][:], D / 4.0, st["m2"][:], ALU.mult, ALU.add))
            dve.wait_ge(std_rooted, 1)
            done(dve.reciprocal(st["std"][:], st["std"][:]))
            done(dve.scalar_tensor_tensor(st["shift"][:], st["sum"][:], -0.5, st["std"][:], ALU.mult, ALU.mult))
            for t in range(NT):
                dve.tensor_scalar(x2[:, t, :], h2[:, t, :], st["std"][:, t:t + 1], st["shift"][:, t:t + 1], ALU.mult,
                                  ALU.add).then_inc(x2_ready, 1)

            for n in range(NB):
                dve.wait_ge(logits_filled, n + 1)
                dve.tensor_reduce(bmax[:, n:n + 1], seven[n][:, 0:TB], AX, ALU.max).then_inc(bmax_ready, 1)
            dve.wait_ge(bmax_ready, NB)
            dve.tensor_reduce(nmax[:], bmax[:], AX, ALU.max).then_inc(psum_step, 1)
            dve.wait_ge(psum_step, 1)
            dve.tensor_scalar(nmax[:], nmax[:], -1.0, None, ALU.mult).then_inc(nmax_ready, 1)
            dve.wait_ge(exp_ready, NB)
            dve.tensor_reduce(psum_inv[:], bsum[:], AX, ALU.add).then_inc(psum_step, 1)
            dve.wait_ge(psum_step, 2)
            dve.reciprocal(psum_inv[:], psum_inv[:]).then_inc(psum_step, 1)
            dve.wait_ge(psum_step, 3)
            dve.tensor_scalar(probs[:], probs[:], psum_inv[:], None, ALU.mult).then_inc(probs_ready, 1)
            dve.wait_ge(probs_ready, 1)

            for r, shift in enumerate(SHIFTS):
                dve.tensor_tensor(thr[:], low[:], trial[:, r:r + 1], ALU.bitwise_or).then_inc(thr_ready, 1)
                dve.wait_ge(thr_ready, r + 1)
                dve.tensor_scalar(above[:], probs[:], thr[:].bitcast(F32), 0.0, ALU.is_ge, ALU.add,
                                  accum_out=count[:]).then_inc(counted, 1)
                dve.wait_ge(counted, r + 1)
                dve.tensor_scalar(enough[:], count[:], float(TOP), None, ALU.is_ge).then_inc(enough_ready, 1)
                dve.wait_ge(digits_filled, r + 1)
                share = 1.0 if r < ROUNDS - 1 else 4.0 / REPS
                dve.tensor_scalar(digit[:], count_bank[:, 0:1], share, -1.0, ALU.mult, ALU.add).then_inc(digit_ready, 1)
                dve.wait_ge(digit_ready, 2 * r + 1)
                dve.tensor_scalar(digit[:], digit[:], shift, None, ALU.logical_shift_left).then_inc(digit_ready, 1)
                dve.wait_ge(digit_ready, 2 * r + 2)
                dve.tensor_tensor(low[:], low[:], digit[:], ALU.bitwise_or).then_inc(low_ready, 1)
                dve.wait_ge(low_ready, r + 1)

            at = low[0:E, :].bitcast(F32)
            dve.tensor_scalar(above[0:E, :], probs[0:E, :], at, 0.0, ALU.is_gt, ALU.add,
                              accum_out=count[0:E, :]).then_inc(gate_step, 1)
            dve.tensor_scalar(ties[:], probs[0:E, :], at, None, ALU.is_equal).then_inc(gate_step, 1)
            dve.wait_ge(gate_step, 2)
            dve.tensor_tensor_scan(ranks[:], ties[:], ties[:], 0.0, ALU.add, ALU.max).then_inc(gate_step, 1)
            dve.tensor_scalar(need[0:E, :], count[0:E, :], -1.0, float(TOP), ALU.mult, ALU.add).then_inc(gate_step, 1)
            dve.wait_ge(gate_step, 4)
            dve.scalar_tensor_tensor(ties[:], ranks[:], need[0:E, :], ties[:], ALU.is_le, ALU.mult).then_inc(gate_step, 1)
            dve.wait_ge(gate_step, 5)
            dve.tensor_tensor(above[0:E, :], above[0:E, :], ties[:], ALU.add).then_inc(gate_step, 1)
            dve.wait_ge(gate_step, 6)
            dve.tensor_tensor(above[0:E, :], above[0:E, :], probs[0:E, :], ALU.mult).then_inc(gates_ready, 1)
            dve.wait_ge(gates_turned, 1)
            dve.tensor_copy(gate[:].rearrange("p t e -> p (t e)"), gate_bank).then_inc(gate_ready, 1)
            dve.wait_ge(gate_ready, 1)

            free = [banks[3][:, 1, :], banks[2][:, 1, :]]
            for g in range((NT + 3) // 4):
                n = min(4, NT - 4 * g)
                dve.wait_ge(bias_filled, g + 1)
                dve.tensor_tensor(acc[:, 4 * g:4 * g + n, :].rearrange("p t d -> p (t d)"), free[g % 2][:, 0:n * D],
                                  h2[:, 4 * g:4 * g + n, :].rearrange("p t d -> p (t d)"), ALU.add).then_inc(acc_ready, 1)
            groups = (NT + 3) // 4
            dve.wait_ge(y_kept, AHEAD * NB)
            dve.wait_ge(acc_ready, groups)
            for e in range(AHEAD):
                with dve.Fori(0, NT) as t:
                    if e:
                        dve.wait_ge(acc_ready, t + (groups + 1))
                    tile = acc[:, bass.ds(t, 1), :].rearrange("p t d -> p (t d)")
                    dve.scalar_tensor_tensor(tile, ahead[:, e, bass.ds(t, 1), :].rearrange("p t d -> p (t d)"),
                                             gate[:, bass.ds(t, 1), e:e + 1].rearrange("p t e -> p (t e)"), tile,
                                             ALU.mult, ALU.add).then_inc(acc_ready, 1)
            dve.wait_ge(acc_ready, groups + AHEAD * NT)
            with dve.Fori(AHEAD, E) as e:
                with dve.Fori(0, NB) as n:
                    dve.wait_ge(y_filled, e * NB + n + 1)
                    for k in range(TPB):
                        t = n * TPB + k
                        tile = acc[:, bass.ds(t, 1), :].rearrange("p t d -> p (t d)")
                        dve.scalar_tensor_tensor(tile, y_bank[:, k * D:(k + 1) * D],
                                                 gate[:, bass.ds(t, 1), bass.ds(e, 1)].rearrange("p t e -> p (t e)"), tile,
                                                 ALU.mult, ALU.add).then_inc(y_added, 1)


_INS = ['x', 'L0_tok_W', 'L0_tok_b', 'L0_tok_effective_scale', 'L0_attn_w_qkv', 'L0_attn_w_proj', 'L0_attn_b_proj',
        'L0_attn_w_e', 'L0_attn_b_e', 'L0_attn_w_s', 'L0_attn_b_s', 'L0_attn_w_h', 'L0_attn_b_h', 'L0_attn_alpha',
        'L0_attn_beta', 'L0_attn_gamma', 'L0_attn_temperature', 'L0_ffn_Wr', 'L0_ffn_W1', 'L0_ffn_b1', 'L0_ffn_W2',
        'L0_ffn_b2']
_OUTS = [((32, 84, 128), 'float32')]


def kernel(**inputs):
    import numpy as _np
    import concourse.bacc as _bacc
    from concourse import mybir as _mybir
    from concourse.bass_utils import run_bass_kernel_spmd as _run

    nc = _bacc.Bacc("TRN2", target_bir_lowering=False, num_devices=1)
    arrays, args = {}, []
    for name in _INS:
        a = _np.ascontiguousarray(inputs[name])
        if a.ndim == 0:
            a = a.reshape(1)
        arrays[f"in_{name}_dram"] = a
        args.append(nc.dram_tensor(f"in_{name}_dram", a.shape, _mybir.dt.from_np(a.dtype), kind="ExternalInput").ap())
    for i, (shape, dtype) in enumerate(_OUTS):
        dt = _mybir.dt.from_np(_np.dtype(dtype))
        args.append(nc.dram_tensor(f"out_{i}_dram", shape, dt, kind="ExternalOutput").ap())
    tower(nc, *args)
    r = _run(nc, [arrays], core_ids=[0])
    got = tuple(r.results[0][f"out_{i}_dram"] for i in range(len(_OUTS)))
    return got[0]
```

```python
from contextlib import ExitStack

import numpy as np

import concourse.bass as bass
from concourse import mybir

F32 = mybir.dt.float32
I32 = mybir.dt.int32
ALU = mybir.AluOpType
ACT = mybir.ActivationFunctionType
AX = mybir.AxisListType.X

P = 128
SEG, STRIDE = 48, 24
BALL_EPS, MIN_NORM = 0.004, 1e-15
HEADS, DH = 8, 64
DE, DS, DHY = 64, 64, 32
FEAT = DE + DS + DHY
LN_EPS = 1e-5
TINY = 2.0 ** -60
SIM_MAX = float(np.float32(1.0 - 1e-6))
ARG_MIN_HALF = float((np.float32(1.0 + 1e-6) - np.float32(1.0)) / 2)
NORM_SHIFT = 20
TOP = 1024
TB = 384
SET_SQRT, SET_LN_EXP, SET_ATAN_TANH = "sqrt_and_others", "natural_log_exp_and_others", "sigmoid_and_others"


def tower(nc, x, tok_W, tok_b, effective_scale, w_qkv, w_proj, b_proj, w_e, b_e, w_s, b_s, w_h, b_h,
          alpha, beta, gamma, temperature, Wr, W1, b1, W2, b2, out):
    B, L = x.shape
    D = tok_W.shape[1]
    N = (L - SEG) // STRIDE + 1
    T = B * N
    E, _, F = W1.shape
    NT = T // P
    NB = T // TB
    TPB = TB // P
    FC = F // P
    PAIRS = B // 2
    W2N = 2 * N
    INNER = HEADS * DH
    assert D == P and T == NT * P and T == NB * TB and B % 8 == 0 and P % E == 0

    h2_dram = nc.dram_tensor("h2_scratch", (T, D), F32, kind="Internal").ap()

    with ExitStack() as ctx:
        banks = [ctx.enter_context(nc.psum_tensor(f"slot{k}", [P, 2, 512], F32)) for k in range(4)]
        ident = ctx.enter_context(nc.sbuf_tensor("ident", [P, P], F32))
        h2_saved = ctx.enter_context(nc.semaphore("h2_saved"))
        embed_and_attend(nc, (B, L, D, N, PAIRS, W2N, INNER), banks, ident, h2_dram, h2_saved, x, tok_W, tok_b, effective_scale,
                         w_qkv, w_proj, b_proj, w_e, b_e, w_s, b_s, w_h, b_h, alpha, beta, gamma, temperature)
        experts(nc, (D, T, E, F, NT, NB, TPB, FC, PAIRS), banks, ident, h2_dram, h2_saved, Wr, W1, b1, W2, b2, out)


def embed_and_attend(nc, dims, banks, ident, h2_dram, h2_saved, x, tok_W, tok_b, effective_scale,
                     w_qkv, w_proj, b_proj, w_e, b_e, w_s, b_s, w_h, b_h, alpha, beta, gamma, temperature):
    B, L, D, N, PAIRS, W2N, INNER = dims
    QT = HEADS // 2
    HT = HEADS // 4
    CH = 4
    with ExitStack() as ctx:
        def sb(name, shape, dt=F32):
            return ctx.enter_context(nc.sbuf_tensor(name, shape, dt))

        block64 = sb("block64", [P, P])
        block32 = sb("block32", [P, P])
        pick2 = sb("pick2", [P, 2, N])
        pick4 = sb("pick4", [P, 4, N])
        pick4_32nd = sb("pick4_32nd", [P, 4, W2N])
        quarter = sb("quarter", [P, N])
        shift_bias = sb("shift_bias", [P, 1])
        eps_bias = sb("eps_bias", [P, 1])
        seg_w = sb("seg_w", [SEG + 1, D])
        w_heads = sb("w_heads", [DH, 2 * HEADS, D])
        w_es = sb("w_es", [DE + DS, DH])
        w_hy = sb("w_hy", [DHY, DH])
        w_v = sb("w_v", [P, 4, D])
        w_p = sb("w_p", [P, INNER])
        featT = sb("featT", [DH, FEAT])
        comp_e = sb("comp_e", [P, 2 * HEADS * DE])
        comp_s = sb("comp_s", [P, 2 * HEADS * DS])
        comp_h = sb("comp_h", [P, 2 * HEADS * DHY])
        w_vT = sb("w_vT", [P, INNER])
        w_pT = sb("w_pT", [P, 4, D])
        be2 = sb("be2", [P, 1])
        bs2 = sb("bs2", [P, 1])
        bh4 = sb("bh4", [P, 1])
        bproj = sb("bproj", [P, D])
        raw5 = sb("raw5", [P, 5])
        sp_abs = sb("sp_abs", [P, 4])
        sp = sb("sp", [P, 4])
        scale_t = sb("scale_t", [P, 1])
        c_e2 = sb("c_e2", [P, 1])
        c_s = sb("c_s", [P, 1])
        c_h = sb("c_h", [P, 1])

        seg = [sb(f"seg{k}", [N, CH, SEG]) for k in range(2)]
        segT = [sb(f"segT{k}", [SEG + 1, CH * N]) for k in range(2)]
        u = sb("u", [N, B, D])
        stats = sb("stats", [N, B, 6])
        st = {n: sb(f"st_{n}", [N, B]) for n in ("sum", "mean", "diff", "m2", "sq", "norm", "unorm", "th",
                                                 "f", "yn", "clip", "var", "std", "gain", "shift")}

        xn = sb("xn", [N, 2, D])
        xT = sb("xT", [P, PAIRS, W2N])
        xT_old = sb("xT_old", [P, W2N])
        eq, eq_sq, ek_sq = (sb(n, [P, QT, W2N]) for n in ("eq", "eq_sq", "ek_sq"))
        ek_m2 = sb("ek_m2", [P, QT, 2, W2N])
        s_raw = sb("s_raw", [P, 2, QT, W2N])
        s_sq = sb("s_sq", [P, 2, QT, W2N])
        s_inv = sb("s_inv", [P, 2, QT, W2N])
        sq_n = sb("sq_n", [P, QT, W2N])
        sk_n = sb("sk_n", [P, QT, 2, W2N])
        hqk = sb("hqk", [P, 2, HT, W2N])
        hq_sq = sb("hq_sq", [P, HT, W2N])
        one_un = sb("one_un", [P, HT, W2N])
        hk_m2 = sb("hk_m2", [P, HT, 4, W2N])
        hk_sq4 = sb("hk_sq4", [P, HT, 4, W2N])
        hk_den = sb("hk_den", [P, HT, 4, W2N])
        v_aug = sb("v_aug", [N, 2, HEADS, DH + 1])
        esb, csb, den, mq, rden, droot, dist, su, sh, hs, hr, attnT = (
            sb(n, [N, 2, HEADS * N]) for n in ("esb", "csb", "den", "mq", "rden", "droot", "dist", "su", "sh", "hs",
                                               "hr", "attnT"))
        dmin = sb("dmin", [N, 2 * HEADS])
        rsum = sb("rsum", [N, 2, HEADS])
        o_tok = [sb(f"o_tok{k}", [N, HEADS, DH]) for k in range(2)]
        oT = [sb(f"oT{k}", [P, 4, N]) for k in range(2)]
        hres = sb("hres", [N, 2, D])
        h2_out = sb("h2_out", [N, 2, D])

        def sem(name):
            return ctx.enter_context(nc.semaphore(name))

        (ident_zero, ident_ready, consts_set, picks_set, seg_w_loaded, weights_loaded, params_loaded, segT_ready,
         z_filled, u_ready, stats_ready, ones_set, stat_step, stat_root, softplus_step, c_ready, scale_ready,
         w_turned, featT_ready, wvp_turned, wvp_ready, comp_filled, comp_ready, xn_ready, xT_filled, xT_ready,
         eq_filled, eq_ready, eq_squared, ek_filled, ek_squared, ek_ready, sqf_filled, sqf_ready, skf_filled,
         skf_ready, s_squared, snq_filled, snk_filled, s_norm_ready, s_inv_step, s_inv_ready, sn_ready,
         hf_filled, hf_ready, hq_squared, un_filled, un_ready, hk_spread, hk_squared, hk_den_ready, v_filled,
         v_placed, e_filled, e_read, s_filled, s_read, hden_filled, den_ready, hdns_filled, mq_ready, rden_step,
         rden_ready, mq_scaled, q_ready, dist_rooted, su_rooted, sh_rooted, hs_rooted, hr_rooted, w_step,
         w_ready, t_ready, atan_ready, g_ready, log_ready, dmin_ready, dist_shifted, exp_ready, attn_turned,
         attnT_ready, pv_filled, rsum_ready, o_ready, o_turned, oT_ready, proj_filled, hres_ready, h2_ready,
         dist_es, dist_whole, xT_old_ready) = (
             sem(n) for n in """ident_zero ident_ready consts_set picks_set seg_w_loaded weights_loaded params_loaded segT_ready
                 z_filled u_ready stats_ready ones_set stat_step stat_root softplus_step c_ready scale_ready
                 w_turned featT_ready wvp_turned wvp_ready comp_filled comp_ready xn_ready xT_filled xT_ready
                 eq_filled eq_ready eq_squared ek_filled ek_squared ek_ready sqf_filled sqf_ready skf_filled
                 skf_ready s_squared snq_filled snk_filled s_norm_ready s_inv_step s_inv_ready sn_ready hf_filled
                 hf_ready hq_squared un_filled un_ready hk_spread hk_squared hk_den_ready v_filled v_placed
                 e_filled e_read s_filled s_read hden_filled den_ready hdns_filled mq_ready rden_step rden_ready
                 mq_scaled q_ready dist_rooted su_rooted sh_rooted hs_rooted hr_rooted w_step w_ready t_ready
                 atan_ready g_ready log_ready dmin_ready dist_shifted exp_ready attn_turned attnT_ready pv_filled
                 rsum_ready o_ready o_turned oT_ready proj_filled hres_ready h2_ready dist_es dist_whole
                 xT_old_ready""".split())
        seg_freed = [ctx.enter_context(nc.semaphore(f"seg_freed{k}")) for k in range(2)]
        seg_in = [ctx.enter_context(nc.semaphore(f"seg_in{k}")) for k in range(2)]
        block = ctx.enter_context(nc.Block())

        CHUNKS = B // CH
        COMP = [(g, min(3, 2 * HEADS - g)) for g in range(0, 2 * HEADS, 3)]
        COMP_AT = [(2, 0), (2, 1), (3, 0), (3, 1), (1, 1), (0, 0)]

        @block.sync
        def _(sp):
            def load_seg(c, k):
                src = bass.AP(x.tensor, c * (CH * L), [[STRIDE, N], [L, CH], [1, SEG]])
                sp.dma_start(seg[k][:], src).then_inc(seg_in[k], 16)

            load_seg(0, 0)
            load_seg(1, 1)
            sp.dma_start(seg_w[0:SEG, :], tok_W).then_inc(seg_w_loaded, 16)
            sp.dma_start(seg_w[SEG:SEG + 1, :], tok_b.unsqueeze(0)).then_inc(seg_w_loaded, 16)
            sp.dma_start(raw5[:, 4:5], effective_scale.unsqueeze(0).broadcast_to([P, 1])).then_inc(params_loaded, 16)
            for j, a in enumerate((alpha, beta, gamma, temperature)):
                sp.dma_start(raw5[:, j:j + 1], a.unsqueeze(0).broadcast_to([P, 1])).then_inc(params_loaded, 16)
            with sp.Fori(1, CHUNKS // 2) as i:
                for k in range(2):
                    sp.wait_ge(seg_freed[k], i)
                    load_seg(2 * i + k, k)
            sp.dma_start(w_heads[:], w_qkv[0:2 * INNER, :].rearrange("(g d) c -> d g c", d=DH)).then_inc(weights_loaded, 16)
            sp.dma_start(w_v[:], w_qkv[2 * INNER:3 * INNER, :].rearrange("(k p) c -> p k c", p=P)).then_inc(weights_loaded, 16)
            sp.dma_start(w_p[:], w_proj).then_inc(weights_loaded, 16)
            sp.dma_start(w_es[0:DE, :], w_e).then_inc(weights_loaded, 16)
            sp.dma_start(w_es[DE:DE + DS, :], w_s).then_inc(weights_loaded, 16)
            sp.dma_start(w_hy[:], w_h).then_inc(weights_loaded, 16)
            for k in range(2):
                sp.dma_start(be2[k * DE:(k + 1) * DE, :], b_e.unsqueeze(1)).then_inc(weights_loaded, 16)
                sp.dma_start(bs2[k * DS:(k + 1) * DS, :], b_s.unsqueeze(1)).then_inc(weights_loaded, 16)
            for k in range(4):
                sp.dma_start(bh4[k * DHY:(k + 1) * DHY, :], b_h.unsqueeze(1)).then_inc(weights_loaded, 16)
            sp.dma_start(bproj[:], b_proj.unsqueeze(0).broadcast_to([P, D])).then_inc(weights_loaded, 16)
            with sp.Fori(0, PAIRS) as p:
                sp.wait_ge(h2_ready, 2 * p + 2)
                dst = h2_dram[bass.ds(p * W2N, W2N), :].rearrange("(b n) c -> n b c", n=N)
                sp.dma_start(dst, h2_out[:]).then_inc(h2_saved, 16)
        WEIGHTS = 16 * 15
        PARAMS = 16 * 5

        @block.gpsimd
        def _(pool):
            pool.memset(ident[:], 0.0).then_inc(ident_zero, 1)
            pool.wait_ge(ident_zero, 1)
            pool.affine_select(out=ident[:], in_=ident[:], compare_op=ALU.not_equal, fill=1.0, base=0,
                               pattern=[[-1, P]], channel_multiplier=1).then_inc(ident_ready, 1)
            for t in (ek_m2, sk_n, hk_m2, block64, block32, pick2, pick4, pick4_32nd):
                last = pool.memset(t[:], 0.0)
            last.then_inc(consts_set, 1)
            pool.memset(quarter[:], 0.25).then_inc(consts_set, 1)
            pool.memset(v_aug[:, :, :, DH:DH + 1], 1.0).then_inc(consts_set, 1)
            pool.memset(shift_bias[:], float(NORM_SHIFT * np.log(2.0) / 2)).then_inc(consts_set, 1)

            def features(nxt):
                pool.wait_ge(eq_ready, nxt + 1)
                pool.tensor_tensor(eq_sq[:], eq[:], eq[:], ALU.mult).then_inc(eq_squared, 1)
                pool.wait_ge(sqf_ready, nxt + 1)
                pool.tensor_tensor(s_sq[:, 0], s_raw[:, 0], s_raw[:, 0], ALU.mult).then_inc(s_squared, 1)
                pool.wait_ge(skf_ready, nxt + 1)
                pool.tensor_tensor(s_sq[:, 1], s_raw[:, 1], s_raw[:, 1], ALU.mult).then_inc(s_squared, 1)

            def hyperbolic_features(nxt):
                pool.wait_ge(hk_spread, 4 * nxt + 4)
                pool.wait_ge(hdns_filled, 2 * nxt)
                pool.wait_ge(hk_den_ready, HT * nxt)
                pool.tensor_tensor(hk_sq4[:], hk_m2[:], hk_m2[:], ALU.mult).then_inc(hk_squared, 1)

            def scale_mq(nxt):
                pool.wait_ge(mq_ready, 2 * nxt + 2)
                pool.wait_ge(rden_ready, nxt + 1)
                pool.tensor_tensor(mq[:], mq[:], rden[:], ALU.mult).then_inc(mq_scaled, 1)

            def add_roots(cur):
                pool.wait_ge(hs_rooted, cur + 1)
                pool.wait_ge(hr_rooted, cur + 1)
                pool.tensor_tensor(hs[:], hs[:], hr[:], ALU.add).then_inc(g_ready, 1)

            def tangent(cur):
                pool.wait_ge(su_rooted, cur + 1)
                pool.wait_ge(w_ready, cur + 1)
                pool.tensor_tensor(su[:], su[:], sh[:], ALU.mult).then_inc(t_ready, 1)

            def cycle(i, new=True, mid=True, old=True):
                if old:
                    add_roots(i - 2)
                if new:
                    features(i)
                if mid:
                    tangent(i - 1)
                    scale_mq(i - 1)
                if new:
                    hyperbolic_features(i)

            cycle(0, mid=False, old=False)
            cycle(1, old=False)
            cycle(2)
            with pool.Fori(3, PAIRS - 1) as i:
                cycle(i)
            cycle(PAIRS - 1)
            cycle(PAIRS, new=False)
            cycle(PAIRS + 1, new=False, mid=False)

        @block.tensor
        def _(pe):
            pe.wait_ge(ident_ready, 1)
            pe.wait_ge(seg_w_loaded, 32)
            with pe.Fori(0, CHUNKS // 2) as i:
                for k in range(2):
                    pe.wait_ge(seg_in[k], 16 * i + 16)
                    pe.wait_ge(segT_ready, 2 * i + k)
                    for j in range(CH):
                        last = pe.matmul(banks[k][0:SEG, 0, j * N:(j + 1) * N], seg[k][:, j, :], ident[0:N, 0:N],
                                         start=True, stop=True)
                    last.then_inc(seg_freed[k], 1)
                    pe.wait_ge(segT_ready, 2 * i + k + 1)
                    pe.wait_ge(u_ready, 2 * i + k)
                    for j in range(CH):
                        last = pe.matmul(banks[2 + k][0:N, 0, j * D:(j + 1) * D], segT[k][:, j * N:(j + 1) * N],
                                         seg_w[:], start=True, stop=True)
                    last.then_inc(z_filled, 1)

            pe.wait_ge(weights_loaded, WEIGHTS)
            pe.wait_ge(segT_ready, CHUNKS)
            pe.wait_ge(u_ready, CHUNKS)
            pe.transpose(banks[0][0:DH, 0, 0:P], w_es[:], ident[:])
            pe.transpose(banks[0][0:DH, 0, P:FEAT], w_hy[:], ident[0:DHY, 0:DHY]).then_inc(w_turned, 1)
            for k in range(4):
                pe.transpose(banks[0][:, 1, k * P:(k + 1) * P], w_v[:, k, :], ident[:])
            for k in range(4):
                last = pe.transpose(banks[1][:, 0, k * P:(k + 1) * P], w_p[:, k * P:(k + 1) * P], ident[:])
            last.then_inc(wvp_turned, 1)
            pe.wait_ge(featT_ready, 1)
            for (g0, n), (sl, bk) in zip(COMP, COMP_AT):
                for j in range(n):
                    last = pe.matmul(banks[sl][:, bk, j * FEAT:(j + 1) * FEAT], w_heads[:, g0 + j, :], featT[:],
                                     start=True, stop=True)
                last.then_inc(comp_filled, 1)
            pe.wait_ge(comp_ready, len(COMP))
            pe.wait_ge(wvp_ready, 2)
            pe.wait_ge(picks_set, 16)

            def four(slot, comp, t0, nxt):
                for j in range(4):
                    last = pe.matmul(slot[:, j // 2, (j % 2) * W2N:(j % 2 + 1) * W2N],
                                     comp[:, (t0 + j) * P:(t0 + j + 1) * P],
                                     xT[:, bass.ds(nxt, 1), :].rearrange("p a w -> p (a w)"), start=True, stop=True)
                return last

            slot0, slot1, slot2, slot3 = banks

            def hyperbolic_scores(mid, more_tokens, first_cycles):
                pe.wait_ge(un_ready, mid + 1)
                pe.wait_ge(hk_den_ready, HT * mid + HT)
                for b, (den_slot, dist_slot) in enumerate(((slot0, slot1), (slot2, slot3))):
                    tok = slice(b * N, (b + 1) * N)
                    if b == 1:
                        if more_tokens:
                            pe.wait_ge(xT_ready, mid + 2)
                        if not first_cycles:
                            pe.wait_ge(h2_ready, 2 * (mid - 1))
                    for t in range(HT):
                        last = pe.matmul(den_slot[0:N, t, 0:4 * N], one_un[:, t, tok], hk_den[:, t, :, tok],
                                         start=True, stop=True)
                    last.then_inc(hden_filled, 1)
                    for t in range(HT):
                        o = dist_slot[0:N, t, 0:4 * N]
                        pe.matmul(o, quarter[:], hk_sq4[:, t, :, tok], start=True, stop=False)
                        pe.matmul(o, hq_sq[:, t, tok], pick4[:], start=False, stop=False)
                        last = pe.matmul(o, hqk[:, 0, t, tok], hk_m2[:, t, :, tok], start=False, stop=True)
                    last.then_inc(hdns_filled, 1)

            def features(nxt, with_mid):
                pe.wait_ge(xT_ready, nxt + 1)
                for slot, comp, t0, filled, read, count in ((slot0, comp_e, 0, eq_filled, den_ready, 2 * nxt - 1),
                                                            (slot1, comp_e, QT, ek_filled, mq_ready, 2 * nxt - 1),
                                                            (slot2, comp_s, 0, sqf_filled, den_ready, 2 * nxt),
                                                            (slot3, comp_s, QT, skf_filled, mq_ready, 2 * nxt)):
                    if with_mid:
                        pe.wait_ge(read, count)
                    four(slot, comp, t0, nxt).then_inc(filled, 1)

            def pair_out(sl, j, half):
                return sl[0:N, j, half * W2N:(half + 1) * W2N]

            def euclid(nxt):
                pe.wait_ge(ek_ready, 2 * nxt + 2)
                pe.wait_ge(eq_squared, nxt + 1)
                for b, sl in enumerate((slot0, slot1)):
                    tok = slice(b * N, (b + 1) * N)
                    for j in range(2):
                        for h in range(2):
                            o = sl[0:N, j, 0:4 * N].rearrange("p (t h m) -> p t h m", t=2, h=2)[:, :, h, :]
                            pe.matmul(o, pick2[:, h, :], ek_sq[:, 2 * j:2 * j + 2, tok], start=(h == 0),
                                      stop=False, skip_group_check=True)
                        for half in range(2):
                            t = 2 * j + half
                            pe.matmul(pair_out(sl, j, half), eq_sq[:, t, tok], pick2[:], start=False, stop=False,
                                      skip_group_check=True)
                            last = pe.matmul(pair_out(sl, j, half), eq[:, t, tok], ek_m2[:, t, :, tok],
                                             start=False, stop=(half == 1), skip_group_check=True)
                    last.then_inc(e_filled, 1)

            def spherical_norms(nxt):
                for side, (sl, signal) in enumerate(((slot2, snq_filled), (slot3, snk_filled))):
                    pe.wait_ge(s_squared, 2 * nxt + side + 1)
                    for j in range(2):
                        last = pe.matmul(sl[:, j, 0:2 * W2N], block64[:], s_sq[:, side, 2 * j:2 * j + 2, :],
                                         start=True, stop=True)
                    last.then_inc(signal, 1)

            def values(old, with_new):
                if with_new:
                    pe.wait_ge(e_read, 2 * old + 5)
                else:
                    pe.wait_ge(den_ready, 2 * PAIRS)
                    pe.wait_ge(mq_ready, 2 * PAIRS)
                    pe.wait_ge(h2_ready, 2 * old)
                pe.wait_ge(xT_old_ready, old + 1)
                for j in range(2):
                    last = pe.matmul(slot0[0:N, j, 0:INNER], xT_old[:, j * N:(j + 1) * N], w_vT[:], start=True, stop=True)
                last.then_inc(v_filled, 1)

            def hyperbolic_features(nxt):
                pe.wait_ge(e_read, 2 * nxt + 2)
                for side in range(2):
                    for j in range(HT):
                        t = side * HT + j
                        last = pe.matmul(slot1[:, side, j * W2N:(j + 1) * W2N], comp_h[:, t * P:(t + 1) * P],
                                         xT[:, bass.ds(nxt, 1), :].rearrange("p a w -> p (a w)"), start=True, stop=True)
                last.then_inc(hf_filled, 1)

            def attention_turned(old, with_new):
                if with_new:
                    pe.wait_ge(s_norm_ready, 2 * old + 6)
                pe.wait_ge(exp_ready, old + 1)
                for b, sl in enumerate((slot2, slot3)):
                    for h in range(HEADS):
                        last = pe.transpose(sl[0:N, h // 4, (h % 4) * N:(h % 4 + 1) * N],
                                            dist[:, b, h * N:(h + 1) * N], ident[0:N, 0:N])
                    last.then_inc(attn_turned, 1)

            def sphere(nxt, with_old):
                pe.wait_ge(sn_ready, 3 * nxt + 3)
                for b, sl in enumerate((slot0, slot1)):
                    if b == 0 and with_old:
                        pe.wait_ge(v_placed, nxt - 1)
                    elif b == 1:
                        pe.wait_ge(hf_ready, nxt + 1)
                    tok = slice(b * N, (b + 1) * N)
                    for t in range(QT):
                        last = pe.matmul(pair_out(sl, t // 2, t % 2), sq_n[:, t, tok], sk_n[:, t, :, tok],
                                         start=True, stop=True)
                    last.then_inc(s_filled, 1)

            def tokens_turned(nxt, with_old):
                if with_old:
                    pe.wait_ge(attnT_ready, 2 * nxt - 5)
                pe.wait_ge(xn_ready, 2 * nxt + 2)
                for j in range(2):
                    last = pe.transpose(slot2[:, 0, j * N:(j + 1) * N], xn[:, j, :], ident[0:N, 0:N])
                last.then_inc(xT_filled, 1)

            def hyperbolic_norms(nxt, with_old):
                pe.wait_ge(hq_squared, nxt + 1)
                if with_old:
                    pe.wait_ge(attnT_ready, 2 * nxt - 2)
                pe.matmul(slot3[:, 0, 0:HT * W2N], block32[:], hq_sq[:], start=True, stop=True).then_inc(un_filled, 1)

            def output(old, with_new, with_next):
                pe.wait_ge(v_placed, old + 1)
                for b, sl in enumerate((slot0, slot1)):
                    if with_new:
                        pe.wait_ge(s_read, 2 * old + 5 + b)
                    pe.wait_ge(attnT_ready, 2 * old + b + 1)
                    for h in range(HEADS):
                        last = pe.matmul(sl[0:N, h // 4, (h % 4) * (DH + 1):(h % 4 + 1) * (DH + 1)],
                                         attnT[:, b, h * N:(h + 1) * N], v_aug[:, b, h, :], start=True, stop=True)
                    last.then_inc(pv_filled, 1)
                for b, sl in enumerate((slot2, slot3)):
                    if b == 0 and with_next:
                        pe.wait_ge(xT_ready, old + 4)
                    if b == 1 and with_new:
                        pe.wait_ge(un_ready, old + 3)
                    pe.wait_ge(o_ready, 4 * old + 2 * b + 2)
                    for k in range(4):
                        last = pe.transpose(sl[:, 0, k * N:(k + 1) * N],
                                            o_tok[b][:, 2 * k:2 * k + 2, :].rearrange("p h d -> p (h d)"), ident[0:N, 0:N])
                    last.then_inc(o_turned, 1)
                for b, sl in enumerate((slot2, slot3)):
                    pe.wait_ge(oT_ready, 2 * old + b + 1)
                    for k in range(4):
                        last = pe.matmul(sl[0:N, 1, 0:D], oT[b][:, k, :], w_pT[:, k, :], start=(k == 0), stop=(k == 3))
                    last.then_inc(proj_filled, 1)

            def cycle(i, new=True, mid=True, old=True, more=True, first_cycles=False):
                if mid:
                    hyperbolic_scores(i - 1, new, first_cycles)
                if new:
                    features(i, mid)
                    euclid(i)
                    spherical_norms(i)
                if old:
                    values(i - 2, new)
                if new:
                    hyperbolic_features(i)
                if old:
                    attention_turned(i - 2, new)
                if new:
                    sphere(i, old)
                    if more:
                        tokens_turned(i + 1, old)
                    hyperbolic_norms(i, old)
                if old:
                    output(i - 2, new, new and more)

            tokens_turned(0, False)
            cycle(0, mid=False, old=False)
            cycle(1, old=False, first_cycles=True)
            cycle(2, first_cycles=True)
            with pe.Fori(3, PAIRS - 1) as i:
                cycle(i)
            cycle(PAIRS - 1, more=False)
            cycle(PAIRS, new=False)
            cycle(PAIRS + 1, new=False, mid=False)

        @block.scalar
        def _(act):
            act.wait_ge(params_loaded, PARAMS)
            act.activation(scale_t[:], raw5[:, 4:5], ACT.Tanh).then_inc(scale_ready, 1)
            act.activation(sp_abs[:], raw5[:, 0:4], ACT.Abs).then_inc(softplus_step, 1)
            act.wait_ge(softplus_step, 1)
            act.preload_act_table_set(SET_LN_EXP)
            act.activation(sp_abs[:], sp_abs[:], ACT.Exp, scale=-1.0).then_inc(softplus_step, 1)
            act.wait_ge(softplus_step, 2)
            act.activation(sp_abs[:], sp_abs[:], ACT.Ln, bias=1.0).then_inc(softplus_step, 1)
            act.wait_ge(scale_ready, 1)
            act.wait_ge(ones_set, 1)
            with act.Fori(0, CHUNKS // 2) as i:
                for k in range(2):
                    act.wait_ge(seg_freed[k], i + 1)
                    act.wait_ge(z_filled, 2 * i + k)
                    act.copy(segT[k][0:SEG, :], banks[k][0:SEG, 0, 0:CH * N]).then_inc(segT_ready, 1)
                    act.wait_ge(z_filled, 2 * i + k + 1)
                    act.activation(u[:, bass.ds((2 * i + k) * CH, CH), :].rearrange("n b d -> n (b d)"),
                                   banks[2 + k][0:N, 0, :], ACT.Copy, scale=scale_t[0:N, :]).then_inc(u_ready, 1)
            act.wait_ge(w_turned, 1)
            act.copy(featT[:], banks[0][0:DH, 0, 0:FEAT]).then_inc(featT_ready, 1)
            act.wait_ge(wvp_turned, 1)
            act.copy(w_vT[:], banks[0][:, 1, :]).then_inc(wvp_ready, 1)
            act.copy(w_pT[:].rearrange("p k c -> p (k c)"), banks[1][:, 0, :]).then_inc(wvp_ready, 1)
            for n, ((g0, m), (sl, bk)) in enumerate(zip(COMP, COMP_AT)):
                act.wait_ge(comp_filled, n + 1)
                src = banks[sl][:, bk, 0:m * FEAT].rearrange("p (g f) -> p g f", f=FEAT)
                for dst, a, w in ((comp_e, 0, DE), (comp_s, DE, DS), (comp_h, DE + DS, DHY)):
                    last = act.copy(dst[:, g0 * w:(g0 + m) * w].rearrange("p (g f) -> p g f", f=w), src[:, :, a:a + w])
                last.then_inc(comp_ready, 1)
            act.preload_act_table_set(SET_SQRT)
            act.wait_ge(stat_step, 8)
            act.activation(st["unorm"][:], st["norm"][:], ACT.Sqrt).then_inc(stat_root, 1)
            act.preload_act_table_set(SET_ATAN_TANH)
            act.wait_ge(stat_step, 9)
            act.activation(st["th"][:], st["norm"][:], ACT.Tanh).then_inc(stat_root, 1)
            act.preload_act_table_set(SET_SQRT)
            act.wait_ge(stat_step, 18)
            act.activation(st["std"][:], st["var"][:], ACT.Sqrt, bias=eps_bias[0:N, :]).then_inc(stat_root, 1)

            def flat(ap):
                return ap.rearrange("p a b -> p (a b)")

            def feature_evacuation(nxt):
                slots = [banks[k][:, :, 0:2 * W2N] for k in range(4)]

                def tiles(ap):
                    return ap.rearrange("p (j t) w -> p j (t w)", j=2)
                act.wait_ge(eq_filled, nxt + 1)
                act.activation(tiles(eq[:]), slots[0], ACT.Identity, bias=be2[:]).then_inc(eq_ready, 1)
                act.wait_ge(ek_filled, nxt + 1)
                act.activation(tiles(ek_sq[:]), slots[1], ACT.Square, bias=be2[:]).then_inc(ek_squared, 1)
                act.wait_ge(sqf_filled, nxt + 1)
                act.activation(tiles(s_raw[:, 0]), slots[2], ACT.Identity, bias=bs2[:]).then_inc(sqf_ready, 1)
                act.wait_ge(skf_filled, nxt + 1)
                act.activation(tiles(s_raw[:, 1]), slots[3], ACT.Identity, bias=bs2[:]).then_inc(skf_ready, 1)

            def inverse_norms(nxt):
                f = s_inv[:].rearrange("p a b c -> p (a b c)")
                act.wait_ge(s_norm_ready, 2 * nxt + 2)
                act.activation(f, f, ACT.Ln).then_inc(s_inv_step, 1)
                act.wait_ge(s_inv_step, nxt + 1)
                act.activation(f, f, ACT.Exp, scale=-0.5, bias=shift_bias[:]).then_inc(s_inv_ready, 1)

            def hyperbolic_evacuation(nxt):
                act.wait_ge(hf_filled, nxt + 1)
                act.activation(hqk[:].rearrange("p a b c -> p a (b c)"), banks[1][:, :, 0:HT * W2N], ACT.Tanh,
                               bias=bh4[:]).then_inc(hf_ready, 1)

            def hyperbolic_squares(nxt):
                act.wait_ge(hf_ready, nxt + 1)
                act.activation(flat(hq_sq[:]), flat(hqk[:, 0]), ACT.Square).then_inc(hq_squared, 1)

            def inverse_denominators(nxt):
                act.wait_ge(den_ready, 2 * nxt + 2)
                act.activation(flat(rden[:]), flat(den[:]), ACT.Ln).then_inc(rden_step, 1)
                act.wait_ge(rden_step, nxt + 1)
                act.activation(flat(rden[:]), flat(rden[:]), ACT.Exp, scale=-1.0).then_inc(rden_ready, 1)

            def roots_of_q(cur):
                act.wait_ge(q_ready, cur + 1)
                act.activation(flat(hs[:]), flat(mq[:]), ACT.Sqrt).then_inc(hs_rooted, 1)
                act.activation(flat(hr[:]), flat(mq[:]), ACT.Sqrt, bias=1.0).then_inc(hr_rooted, 1)

            def roots(cur, first):
                act.wait_ge(e_read, 2 * cur + 2)
                if not first:
                    act.wait_ge(dist_es, cur)
                act.activation(flat(droot[:]), flat(esb[:]), ACT.Sqrt, scale=c_e2[0:N, :]).then_inc(dist_rooted, 1)
                act.wait_ge(s_read, 2 * cur + 2)
                act.activation(flat(su[:]), flat(csb[:]), ACT.Sqrt, scale=-0.5, bias=0.5).then_inc(su_rooted, 1)
                act.activation(flat(sh[:]), flat(csb[:]), ACT.Sqrt, scale=0.5, bias=0.5).then_inc(sh_rooted, 1)

            def log_of_g(cur):
                act.wait_ge(g_ready, cur + 1)
                act.activation(flat(hs[:]), flat(hs[:]), ACT.Ln).then_inc(log_ready, 1)

            def logs(cur):
                act.wait_ge(sh_rooted, cur + 1)
                act.activation(flat(sh[:]), flat(sh[:]), ACT.Ln, bias=1.0).then_inc(w_step, 1)
                act.wait_ge(w_step, cur + 1)
                act.activation(flat(sh[:]), flat(sh[:]), ACT.Exp, scale=-1.0).then_inc(w_ready, 1)

            def arctangent(cur):
                act.wait_ge(t_ready, cur + 1)
                act.activation(flat(su[:]), flat(su[:]), ACT.Arctan).then_inc(atan_ready, 1)

            def exponent(cur):
                act.wait_ge(dist_shifted, cur + 1)
                act.activation(flat(dist[:]), flat(dist[:]), ACT.Exp).then_inc(exp_ready, 1)

            def attention_copy(cur, b):
                act.wait_ge(attn_turned, 2 * cur + b + 1)
                act.copy(attnT[:, b, :].rearrange("p (j w) -> p j w", j=2),
                         banks[2 + b][0:N, :, 0:4 * N]).then_inc(attnT_ready, 1)

            def cycle(i, new=True, mid=True, old=True, first=False):
                act.preload_act_table_set(SET_SQRT)
                if old:
                    roots_of_q(i - 2)
                if mid:
                    roots(i - 1, first)
                if new:
                    feature_evacuation(i)
                act.preload_act_table_set(SET_LN_EXP)
                if old:
                    log_of_g(i - 2)
                if mid:
                    logs(i - 1)
                    inverse_denominators(i - 1)
                if old:
                    exponent(i - 2)
                if new:
                    inverse_norms(i)
                if old:
                    attention_copy(i - 2, 0)
                act.preload_act_table_set(SET_ATAN_TANH)
                if new:
                    hyperbolic_evacuation(i)
                if old:
                    attention_copy(i - 2, 1)
                if new:
                    hyperbolic_squares(i)
                if mid:
                    arctangent(i - 1)

            act.wait_ge(weights_loaded, WEIGHTS)
            act.wait_ge(c_ready, 1)
            cycle(0, mid=False, old=False)
            cycle(1, old=False, first=True)
            cycle(2)
            with act.Fori(3, PAIRS - 1) as i:
                cycle(i)
            cycle(PAIRS - 1)
            cycle(PAIRS, new=False)
            cycle(PAIRS + 1, new=False, mid=False)

        @block.vector
        def _(dve):
            dve.memset(eps_bias[:], LN_EPS)
            dve.wait_ge(consts_set, 4)
            for k in range(2):
                dve.memset(block64[64 * k:64 * k + 64, 64 * k:64 * k + 64], 1.0).then_inc(picks_set, 1)
                dve.memset(pick2[64 * k:64 * k + 64, k, :], 1.0).then_inc(picks_set, 1)
            for k in range(4):
                r = slice(32 * k, 32 * k + 32)
                dve.memset(block32[r, 32 * k:32 * k + 32], 1.0).then_inc(picks_set, 1)
                dve.memset(pick4[r, k, :], 1.0).then_inc(picks_set, 1)
                dve.memset(pick4_32nd[r, k, :], 1.0 / 32).then_inc(picks_set, 1)
            for k in range(2):
                last = dve.memset(segT[k][:], 1.0)
            last.then_inc(ones_set, 1)
            with dve.Fori(0, CHUNKS) as c:
                dve.wait_ge(u_ready, c + 1)
                for j in range(CH):
                    dve.bn_stats(stats[:, bass.ds(c * CH + j, 1), :].rearrange("n b k -> n (b k)"),
                                 u[:, bass.ds(c * CH + j, 1), :].rearrange("n b d -> n (b d)")).then_inc(stats_ready, 1)

            dve.wait_ge(softplus_step, 3)
            dve.scalar_tensor_tensor(sp[:], raw5[:, 0:4], 0.0, sp_abs[:], ALU.max, ALU.add).then_inc(softplus_step, 1)
            dve.wait_ge(softplus_step, 4)
            dve.reciprocal(sp_abs[:, 3:4], sp[:, 3:4]).then_inc(softplus_step, 1)
            dve.wait_ge(softplus_step, 5)
            dve.tensor_scalar(c_e2[:], sp[:, 0:1], sp_abs[:, 3:4], None, ALU.mult).then_inc(softplus_step, 1)
            dve.tensor_scalar(c_s[:], sp[:, 1:2], sp_abs[:, 3:4], 4.0, ALU.mult, ALU.mult).then_inc(softplus_step, 1)
            dve.tensor_scalar(c_h[:], sp[:, 2:3], sp_abs[:, 3:4], 2.0, ALU.mult, ALU.mult).then_inc(softplus_step, 1)
            dve.wait_ge(softplus_step, 8)
            dve.tensor_tensor(c_e2[:], c_e2[:], c_e2[:], ALU.mult).then_inc(c_ready, 1)

            half = D // 2
            step = [0]

            def done(ins):
                step[0] += 1
                ins.then_inc(stat_step, 1)
                dve.wait_ge(stat_step, step[0])

            dve.wait_ge(stats_ready, B)
            me, mo, ve, vo = stats[:, :, 1], stats[:, :, 4], stats[:, :, 2], stats[:, :, 5]
            done(dve.tensor_tensor(st["sum"][:], me, mo, ALU.add))
            done(dve.tensor_tensor(st["diff"][:], me, mo, ALU.subtract))
            done(dve.tensor_tensor(st["diff"][:], st["diff"][:], st["diff"][:], ALU.mult))
            done(dve.tensor_tensor(st["m2"][:], ve, vo, ALU.add))
            done(dve.scalar_tensor_tensor(st["m2"][:], st["diff"][:], half / 2.0, st["m2"][:], ALU.mult, ALU.add))
            done(dve.tensor_scalar(st["mean"][:], st["sum"][:], 0.5, None, ALU.mult))
            done(dve.tensor_tensor(st["sq"][:], st["mean"][:], st["mean"][:], ALU.mult))
            done(dve.scalar_tensor_tensor(st["norm"][:], st["sq"][:], float(D), st["m2"][:], ALU.mult, ALU.add))
            dve.wait_ge(stat_root, 1)
            done(dve.tensor_scalar(st["norm"][:], st["unorm"][:], MIN_NORM, None, ALU.max))
            done(dve.reciprocal(st["f"][:], st["norm"][:]))
            dve.wait_ge(stat_root, 2)
            done(dve.tensor_tensor(st["f"][:], st["f"][:], st["th"][:], ALU.mult))
            done(dve.tensor_tensor(st["yn"][:], st["f"][:], st["unorm"][:], ALU.mult))
            done(dve.tensor_scalar(st["yn"][:], st["yn"][:], MIN_NORM, None, ALU.max))
            done(dve.reciprocal(st["clip"][:], st["yn"][:]))
            done(dve.tensor_scalar(st["clip"][:], st["clip"][:], 1.0 - BALL_EPS, 1.0, ALU.mult, ALU.min))
            done(dve.tensor_tensor(st["f"][:], st["f"][:], st["clip"][:], ALU.mult))
            done(dve.tensor_tensor(st["var"][:], st["f"][:], st["f"][:], ALU.mult))
            done(dve.scalar_tensor_tensor(st["var"][:], st["var"][:], 1.0 / D, st["m2"][:], ALU.mult, ALU.mult))
            dve.wait_ge(stat_root, 3)
            done(dve.reciprocal(st["std"][:], st["std"][:]))
            done(dve.tensor_tensor(st["gain"][:], st["std"][:], st["f"][:], ALU.mult))
            done(dve.scalar_tensor_tensor(st["shift"][:], st["gain"][:], -1.0, st["mean"][:], ALU.mult, ALU.mult))

            def tiles(ap):
                return ap.rearrange("p (j t) w -> p j (t w)", j=2)

            def flat(ap):
                return ap.rearrange("p a b -> p (a b)")

            def normalise(nxt):
                for j in range(2):
                    b = 2 * nxt + j
                    dve.tensor_scalar(xn[:, j, :], u[:, bass.ds(b, 1), :].rearrange("n b d -> n (b d)"), st["gain"][:, bass.ds(b, 1)],
                                      st["shift"][:, bass.ds(b, 1)], ALU.mult, ALU.add).then_inc(xn_ready, 1)

            def keep_turned_tokens(nxt):
                dve.wait_ge(xT_filled, nxt + 1)
                dve.tensor_scalar(xT[:, bass.ds(nxt, 1), :].rearrange("p a w -> p (a w)"), banks[2][:, 0, 0:W2N], 1.0, None,
                                  ALU.mult).then_inc(xT_ready, 1)

            def fetch_turned_tokens(old, first):
                dve.wait_ge(xT_ready, old + 1)
                if not first:
                    dve.wait_ge(v_filled, old)
                dve.tensor_scalar(xT_old[:], xT[:, bass.ds(old, 1), :].rearrange("p a w -> p (a w)"), 1.0, None,
                                  ALU.mult).then_inc(xT_old_ready, 1)

            def key_evacuation(nxt):
                dve.wait_ge(ek_squared, nxt + 1)
                for h in range(2):
                    r = slice(64 * h, 64 * h + 64)
                    dve.tensor_scalar(ek_m2[r, :, h, :].rearrange("p (j t) w -> p j t w", j=2),
                                      banks[1][r, :, 0:2 * W2N].rearrange("p j (t w) -> p j t w", t=2),
                                      be2[r, :], -2.0, ALU.add, ALU.mult).then_inc(ek_ready, 1)

            def guarded_norms(nxt):
                for side, k, signal in ((0, 2, snq_filled), (1, 3, snk_filled)):
                    dve.wait_ge(signal, nxt + 1)
                    dve.tensor_scalar(tiles(s_inv[:, side]), banks[k][:, :, 0:2 * W2N], 1e-24,
                                      2.0 ** NORM_SHIFT, ALU.max, ALU.mult).then_inc(s_norm_ready, 1)

            def unit_features(nxt):
                dve.wait_ge(s_inv_ready, nxt + 1)
                dve.tensor_tensor(sq_n[:], s_raw[:, 0], s_inv[:, 0], ALU.mult).then_inc(sn_ready, 1)
                for h in range(2):
                    r = slice(64 * h, 64 * h + 64)
                    dve.tensor_tensor(sk_n[r, :, h, :], s_raw[r, 1], s_inv[r, 1], ALU.mult).then_inc(sn_ready, 1)

            def euclid_to_sbuf(nxt, b, first):
                if b == 0 and not first:
                    dve.wait_ge(dist_rooted, nxt)
                dve.wait_ge(e_filled, 2 * nxt + b + 1)
                dve.tensor_scalar(esb[:, b, :].rearrange("p (j w) -> p j w", j=2), banks[b][0:N, :, 0:4 * N],
                                  1e-12, None, ALU.max).then_inc(e_read, 1)

            def sphere_to_sbuf(nxt, first):
                if not first:
                    dve.wait_ge(sh_rooted, nxt)
                for b in range(2):
                    dve.wait_ge(s_filled, 2 * nxt + b + 1)
                    dve.tensor_scalar(csb[:, b, :].rearrange("p (j w) -> p j w", j=2), banks[b][0:N, :, 0:4 * N],
                                      -SIM_MAX, SIM_MAX, ALU.max, ALU.min).then_inc(s_read, 1)

            def spread_keys(nxt):
                dve.wait_ge(hf_ready, nxt + 1)
                for h in range(4):
                    r = slice(32 * h, 32 * h + 32)
                    dve.tensor_scalar(hk_m2[r, :, h, :], hqk[r, 1], -2.0, None, ALU.mult).then_inc(hk_spread, 1)

            def query_norms(nxt):
                dve.wait_ge(un_filled, nxt + 1)
                dve.tensor_scalar(flat(one_un[:]), banks[3][:, 0, 0:HT * W2N], -1.0, 1.0, ALU.mult, ALU.add)\
                   .then_inc(un_ready, 1)

            def key_denominators(nxt):
                dve.wait_ge(hk_squared, nxt + 1)
                for t in range(HT):
                    dve.scalar_tensor_tensor(flat(hk_den[:, t]), flat(hk_sq4[:, t]), -0.25, flat(pick4_32nd[:]),
                                             ALU.mult, ALU.add).then_inc(hk_den_ready, 1)

            def hyperbolic_scores(mid, first):
                for b in range(2):
                    dve.wait_ge(hden_filled, 2 * mid + b + 1)
                    if b == 0 and not first:
                        dve.wait_ge(rden_step, mid)
                    dve.tensor_scalar(den[:, b, :].rearrange("p (j w) -> p j w", j=2), banks[2 * b][0:N, :, 0:4 * N],
                                      1e-8, TINY, ALU.add, ALU.max).then_inc(den_ready, 1)
                    dve.wait_ge(hdns_filled, 2 * mid + b + 1)
                    dve.wait_ge(den_ready, 2 * mid + b + 1)
                    if b == 0 and not first:
                        dve.wait_ge(hr_rooted, mid)
                    dve.scalar_tensor_tensor(mq[:, b, :].rearrange("p (j w) -> p j w", j=2),
                                             den[:, b, :].rearrange("p (j w) -> p j w", j=2), TINY,
                                             banks[2 * b + 1][0:N, :, 0:4 * N], ALU.is_gt, ALU.mult)\
                       .then_inc(mq_ready, 1)

            def place_values(old, first):
                dve.wait_ge(v_filled, old + 1)
                if not first:
                    dve.wait_ge(pv_filled, 2 * old)
                dve.tensor_copy(v_aug[:, :, :, 0:DH], banks[0][0:N, :, :].rearrange("n b (h d) -> n b h d", d=DH))\
                   .then_inc(v_placed, 1)

            def clamp_q(mid):
                dve.wait_ge(mq_scaled, mid + 1)
                dve.tensor_scalar(flat(mq[:]), flat(mq[:]), ARG_MIN_HALF, None, ALU.max).then_inc(q_ready, 1)

            def add_spherical(mid, first):
                if not first:
                    dve.wait_ge(attn_turned, 2 * mid)
                dve.wait_ge(atan_ready, mid + 1)
                dve.scalar_tensor_tensor(flat(dist[:]), flat(su[:]), c_s[0:N, :], flat(droot[:]), ALU.mult,
                                         ALU.add).then_inc(dist_es, 1)

            def add_hyperbolic(old):
                dve.wait_ge(dist_es, old + 1)
                dve.wait_ge(log_ready, old + 1)
                dve.scalar_tensor_tensor(flat(dist[:]), flat(hs[:]), c_h[0:N, :], flat(dist[:]), ALU.mult,
                                         ALU.add).then_inc(dist_whole, 1)
                dve.wait_ge(dist_whole, old + 1)
                dve.tensor_reduce(dmin[:], flat(dist[:]).rearrange("p (h m) -> p h m", m=N), AX, ALU.min)\
                   .then_inc(dmin_ready, 1)

            def shift_distance(old):
                dve.wait_ge(dmin_ready, old + 1)
                d3 = flat(dist[:]).rearrange("p (h m) -> p h m", m=N)
                dve.tensor_tensor(d3, dmin[:].unsqueeze(2).broadcast_to([N, 2 * HEADS, N]), d3, ALU.subtract)\
                   .then_inc(dist_shifted, 1)

            def divide_by_sum(old, b, first):
                n = 2 * old + b
                dve.wait_ge(pv_filled, n + 1)
                pv = banks[b][0:N, :, 0:4 * (DH + 1)].rearrange("p j (h d) -> p j h d", h=4)
                dve.reciprocal(rsum[:, b, :].rearrange("p (j h) -> p j h", j=2), pv[:, :, :, DH]).then_inc(rsum_ready, 1)
                dve.wait_ge(rsum_ready, n + 1)
                for j in range(2):
                    dve.tensor_tensor(o_tok[b][:, 4 * j:4 * j + 4, :], pv[:, j, :, 0:DH],
                                      rsum[:, b, 4 * j:4 * j + 4].unsqueeze(2).broadcast_to([N, 4, DH]),
                                      ALU.mult).then_inc(o_ready, 1)

            def residual(old, b, first):
                n = 2 * old + b
                if b == 0 and not first:
                    dve.wait_ge(h2_saved, 16 * old)
                dve.scalar_tensor_tensor(hres[:, b, :], u[:, bass.ds(n, 1), :].rearrange("p a d -> p (a d)"),
                                         st["f"][:, bass.ds(n, 1)], bproj[0:N, :], ALU.mult, ALU.add)\
                   .then_inc(hres_ready, 1)

            def turned_output(old, b):
                dve.wait_ge(o_turned, 2 * old + b + 1)
                dve.tensor_copy(flat(oT[b][:]), banks[2 + b][:, 0, 0:4 * N]).then_inc(oT_ready, 1)

            def add_residual(old, b):
                n = 2 * old + b
                dve.wait_ge(hres_ready, n + 1)
                dve.wait_ge(proj_filled, n + 1)
                dve.tensor_tensor(h2_out[:, b, :], banks[2 + b][0:N, 1, 0:D], hres[:, b, :], ALU.add)\
                   .then_inc(h2_ready, 1)

            def cycle(i, new=True, mid=True, old=True, more=True, first_new=False, first_mid=False, first_old=False):
                if mid:
                    hyperbolic_scores(i - 1, first_mid)
                if old:
                    fetch_turned_tokens(i - 2, first_old)
                if new:
                    key_evacuation(i)
                    euclid_to_sbuf(i, 0, first_new)
                if old:
                    add_hyperbolic(i - 2)
                if new:
                    euclid_to_sbuf(i, 1, first_new)
                if old:
                    shift_distance(i - 2)
                if new:
                    guarded_norms(i)
                    if more:
                        normalise(i + 1)
                if old:
                    place_values(i - 2, first_old)
                if mid:
                    clamp_q(i - 1)
                if new:
                    unit_features(i)
                    sphere_to_sbuf(i, first_new)
                    spread_keys(i)
                    if more:
                        keep_turned_tokens(i + 1)
                    query_norms(i)
                if old:
                    divide_by_sum(i - 2, 0, first_old)
                    residual(i - 2, 0, first_old)
                    divide_by_sum(i - 2, 1, first_old)
                    residual(i - 2, 1, first_old)
                    turned_output(i - 2, 0)
                    turned_output(i - 2, 1)
                if new:
                    key_denominators(i)
                if mid:
                    add_spherical(i - 1, first_mid)
                if old:
                    add_residual(i - 2, 0)
                    add_residual(i - 2, 1)

            normalise(0)
            keep_turned_tokens(0)
            cycle(0, mid=False, old=False, first_new=True)
            cycle(1, old=False, first_mid=True)
            cycle(2, first_old=True)
            with dve.Fori(3, PAIRS - 1) as i:
                cycle(i)
            cycle(PAIRS - 1, more=False)
            cycle(PAIRS, new=False)
            cycle(PAIRS + 1, new=False, mid=False)


def experts(nc, dims, banks, ident, h2_dram, h2_saved, Wr, W1, b1, W2, b2, out):
    D, T, E, F, NT, NB, TPB, FC, PAIRS = dims
    REPS = P // E
    AHEAD = 2
    SHIFTS = [26, 22, 18, 14, 10, 6, 2, 0]
    ROUNDS = len(SHIFTS)
    THIRD = NT // 3
    with ExitStack() as ctx:
        def sb(name, shape, dt=F32):
            return ctx.enter_context(nc.sbuf_tensor(name, shape, dt))

        h2 = sb("h2", [P, NT, D])
        x2 = sb("x2", [P, NT, D])
        x2T = sb("x2T", [P, T])
        w1 = [sb(f"w1_{k}", [D, F]) for k in range(2)]
        w2 = [sb(f"w2_{k}", [P, FC, D]) for k in range(2)]
        b1_rows = sb("b1_rows", [E * FC, P])
        b1T = sb("b1T", [P, E * FC])
        b2_sb = sb("b2_sb", [E, D])
        wr = sb("wr", [D, E])
        wr_reps = sb("wr_reps", [D, REPS, E])
        hid = [sb(f"hid{c}", [P, TB]) for c in range(FC)]
        ahead = sb("ahead", [P, AHEAD, NT, D])
        acc = sb("acc", [P, NT, D])
        stats = sb("stats2", [P, NT, 6])
        st = {n: sb(f"st2_{n}", [P, NT]) for n in ("sum", "diff", "m2", "mean", "std", "shift")}
        eps2 = sb("eps2", [P, 1])
        probs = sb("probs", [P, T])
        above = sb("above", [P, T])
        ties = sb("ties", [E, T])
        ranks = sb("ranks", [E, T])
        gate = sb("gate", [P, NT, E])
        bmax = sb("bmax", [P, NB])
        nmax = sb("nmax", [P, 1])
        bsum = sb("bsum", [P, NB])
        psum_inv = sb("psum_inv", [P, 1])
        same = sb("same", [P, P])
        iota = sb("iota", [P, P], I32)
        rep = sb("rep", [P, 1], I32)
        trial = sb("trial", [P, ROUNDS], I32)
        low = sb("low", [P, 1], I32)
        thr = sb("thr", [P, 1], I32)
        count = sb("count", [P, 1])
        enough = sb("enough", [P, 1])
        digit = sb("digit", [P, 1], I32)
        need = sb("need", [P, 1])

        def sem(name):
            return ctx.enter_context(nc.semaphore(name + "2"))

        (h2_loaded, router_loaded, bias_loaded, iota_set, eps_set, sel_const, stats_ready, stat_step, std_rooted,
         x2_ready, x2_turned, x2T_ready, b1_turned, b1T_ready, logits_filled, bmax_ready, nmax_ready, exp_ready,
         psum_step, probs_ready, thr_ready, counted, enough_ready, digits_filled, digit_ready, low_ready,
         gate_step, gates_ready, gates_turned, gate_ready, bias_filled, hid_filled, hid_ready, y_filled, y_kept,
         acc_ready, y_added, out_stored) = (
             sem(n) for n in """h2_loaded router_loaded bias_loaded iota_set eps_set sel_const stats_ready stat_step std_rooted
                 x2_ready x2_turned x2T_ready b1_turned b1T_ready logits_filled bmax_ready nmax_ready exp_ready
                 psum_step probs_ready thr_ready counted enough_ready digits_filled digit_ready low_ready
                 gate_step gates_ready gates_turned gate_ready bias_filled hid_filled hid_ready y_filled y_kept
                 acc_ready y_added out_stored""".split())
        w_in = [ctx.enter_context(nc.semaphore(f"experts_in{k}")) for k in range(2)]
        block = ctx.enter_context(nc.Block())
        hid_bank = [banks[c // 2][:, c % 2, 0:TB] for c in range(FC)]
        y_bank = banks[2][:, 0, :]
        count_bank = banks[2][:, 1, :]
        gate_bank = banks[3][:, 0, 0:NT * E]
        seven = [banks[k // 2][:, k % 2, :] for k in range(8)]
        h2_rows = h2_dram.rearrange("(t p) c -> p t c", p=P)

        @block.sync
        def _(sp):
            sp.dma_start(wr[:], Wr).then_inc(router_loaded, 16)
            sp.dma_start(b1_rows[:], b1.rearrange("e (c p) -> (e c) p", p=P)).then_inc(bias_loaded, 16)
            sp.dma_start(b2_sb[:], b2).then_inc(bias_loaded, 16)
            for e in range(2):
                sp.dma_start(w1[e][:], W1[e]).then_inc(w_in[e], 16)
                sp.dma_start(w2[e][:], W2[e].rearrange("(c p) d -> p c d", p=P)).then_inc(w_in[e], 16)
            sp.wait_ge(h2_saved, 16 * PAIRS)
            for c in range(3):
                sp.dma_start(h2[:, c * THIRD:(c + 1) * THIRD, :], h2_rows[:, c * THIRD:(c + 1) * THIRD, :])\
                  .then_inc(h2_loaded, 16)
            with sp.Fori(1, E // 2) as i:
                for k in range(2):
                    sp.wait_ge(y_filled, (2 * i + k - 1) * NB)
                    sp.dma_start(w1[k][:], W1[bass.ds(2 * i + k, 1)].rearrange("e d f -> d (e f)")).then_inc(w_in[k], 16)
                    sp.dma_start(w2[k][:], W2[bass.ds(2 * i + k, 1)].rearrange("e (c p) d -> p (e c) d", p=P))\
                      .then_inc(w_in[k], 16)
            sp.wait_ge(y_added, (E - AHEAD) * NT)
            sp.dma_start(out.rearrange("b n c -> (b n) c").rearrange("(t p) c -> p t c", p=P), acc[:]).then_inc(out_stored, 16)
            sp.wait_ge(out_stored, 16)

        @block.gpsimd
        def _(pool):
            pool.iota(iota[:], [[1, P]], base=P, channel_multiplier=-1).then_inc(iota_set, 1)
            pool.iota(rep[:], [[0, 1]], base=0, channel_multiplier=1).then_inc(iota_set, 1)

        @block.tensor
        def _(pe):
            pe.wait_ge(bias_loaded, 32)
            pe.transpose(seven[7][:, 0:E * FC], b1_rows[:], ident[0:E * FC, 0:E * FC]).then_inc(b1_turned, 1)
            for t in range(NT):
                pe.wait_ge(x2_ready, t + 1)
                last = pe.transpose(seven[t // 4][:, (t % 4) * P:(t % 4 + 1) * P], x2[:, t, :], ident[:])
                if t % 4 == 3 or t == NT - 1:
                    last.then_inc(x2_turned, 1)
            for n in range(NB):
                pe.wait_ge(x2T_ready, (NT + 3) // 4)
                pe.matmul(seven[n][:, 0:TB], wr_reps[:].rearrange("p r e -> p (r e)"), x2T[:, n * TB:(n + 1) * TB],
                          start=True, stop=True).then_inc(logits_filled, 1)

            def ffn_block(n, e_blocks, w1e, w2e):
                for c in range(FC):
                    pe.matmul(hid_bank[c], w1e[:, c * P:(c + 1) * P], x2T[:, bass.ds(n * TB, TB)], start=True,
                              stop=True).then_inc(hid_filled, 1)
                for c in range(FC):
                    pe.wait_ge(hid_ready, FC * e_blocks + c + 1)
                    for t in range(TPB):
                        last = pe.matmul(y_bank[:, t * D:(t + 1) * D], hid[c][:, t * P:(t + 1) * P], w2e[:, c, :],
                                         start=(c == 0 and t == 0), stop=(c == FC - 1), skip_group_check=True)
                last.then_inc(y_filled, 1)

            pe.wait_ge(exp_ready, NB)
            pe.wait_ge(b1T_ready, 1)
            for e in range(AHEAD):
                pe.wait_ge(w_in[e], 32)
                with pe.Fori(0, NB) as n:
                    if e == 0:
                        pe.wait_ge(y_kept, n)
                        ffn_block(n, n, w1[e], w2[e])
                        pe.wait_ge(enough_ready, n + 1)
                        pe.matmul(count_bank[:, 0:1], same[:], enough[:], start=True, stop=True).then_inc(digits_filled, 1)
                    else:
                        pe.wait_ge(y_kept, NB * e + n)
                        ffn_block(n, NB * e + n, w1[e], w2[e])
                if e == 0:
                    for r in range(NB, ROUNDS):
                        pe.wait_ge(enough_ready, r + 1)
                        pe.matmul(count_bank[:, 0:1], same[:], enough[:], start=True, stop=True).then_inc(digits_filled, 1)
            pe.wait_ge(gates_ready, 1)
            for t in range(NT):
                last = pe.transpose(gate_bank[:, t * E:(t + 1) * E], above[0:E, t * P:(t + 1) * P], ident[0:E, 0:E])
            last.then_inc(gates_turned, 1)
            pe.wait_ge(y_kept, AHEAD * NB)
            free = [banks[3][:, 1, :], banks[2][:, 1, :]]
            for g in range((NT + 3) // 4):
                if g >= 2:
                    pe.wait_ge(acc_ready, g - 1)
                for t in range(4 * g, min(4 * g + 4, NT)):
                    last = pe.matmul(free[g % 2][:, (t % 4) * D:(t % 4 + 1) * D], above[0:E, t * P:(t + 1) * P], b2_sb[:],
                                     start=True, stop=True)
                last.then_inc(bias_filled, 1)
            with pe.Fori(AHEAD // 2, E // 2) as i:
                for k in range(2):
                    with pe.Fori(0, NB) as n:
                        pe.wait_ge(w_in[k], 32 * i + 32)
                        before = i * (2 * NB) + k * NB + n
                        pe.wait_ge(y_added, (before - AHEAD * NB) * TPB)
                        ffn_block(n, before, w1[k], w2[k])

        @block.scalar
        def _(act):
            act.preload_act_table_set(SET_SQRT)
            act.wait_ge(b1_turned, 1)
            act.copy(b1T[:], seven[7][:, 0:E * FC]).then_inc(b1T_ready, 1)
            act.wait_ge(stat_step, 5)
            act.wait_ge(eps_set, 1)
            act.activation(st["std"][:], st["m2"][:], ACT.Sqrt, scale=1.0 / D, bias=eps2[:]).then_inc(std_rooted, 1)
            for g in range((NT + 3) // 4):
                n = min(4, NT - 4 * g)
                act.wait_ge(x2_turned, g + 1)
                act.copy(x2T[:, 4 * g * P:(4 * g + n) * P], seven[g][:, 0:n * P]).then_inc(x2T_ready, 1)
            act.preload_act_table_set("exp_and_others")
            act.wait_ge(nmax_ready, 1)
            for n in range(NB):
                act.activation(probs[:, n * TB:(n + 1) * TB], seven[n][:, 0:TB], ACT.Exp, bias=nmax[:],
                               accum_out=bsum[:, n:n + 1]).then_inc(exp_ready, 1)
            act.preload_act_table_set("gelu_and_others")

            def gelus(e, before):
                for c in range(FC):
                    act.wait_ge(hid_filled, FC * before + c + 1)
                    if c == 0:
                        act.wait_ge(y_filled, before)
                    act.activation(hid[c][:], hid_bank[c], ACT.Gelu, bias=b1T[:, bass.ds(e * FC + c, 1)])\
                       .then_inc(hid_ready, 1)

            for e in range(AHEAD):
                with act.Fori(0, NB) as n:
                    gelus(e, NB * e + n)
                    act.wait_ge(y_filled, NB * e + n + 1)
                    act.copy(ahead[:, e, bass.ds(n * TPB, TPB), :].rearrange("p t d -> p (t d)"),
                             y_bank[:, 0:TB]).then_inc(y_kept, 1)
            with act.Fori(AHEAD, E) as e:
                with act.Fori(0, NB) as n:
                    gelus(e, e * NB + n)

        @block.vector
        def _(dve):
            dve.memset(eps2[:], LN_EPS).then_inc(eps_set, 1)
            consts = [0]

            def const(ins):
                consts[0] += 1
                ins.then_inc(sel_const, 1)
                dve.wait_ge(sel_const, consts[0])

            dve.wait_ge(iota_set, 2)
            const(dve.tensor_scalar(iota[:], iota[:], E - 1, None, ALU.bitwise_and))
            const(dve.tensor_scalar(same[:], iota[:], 0.0, None, ALU.is_equal))
            const(dve.tensor_scalar(rep[:], rep[:], int(np.log2(E)), None, ALU.logical_shift_right))
            for r, shift in enumerate(SHIFTS[:-1]):
                dve.tensor_scalar(trial[:, r:r + 1], rep[:], shift, None, ALU.logical_shift_left)
            dve.tensor_scalar(trial[:, ROUNDS - 1:ROUNDS], rep[:], 2, None, ALU.logical_shift_right)
            const(dve.memset(low[:], 0))
            dve.wait_ge(router_loaded, 16)
            const(dve.tensor_copy(wr_reps[:], wr[:].unsqueeze(1).broadcast_to([D, REPS, E])))

            step = [0]

            def done(ins):
                step[0] += 1
                ins.then_inc(stat_step, 1)
                dve.wait_ge(stat_step, step[0])

            for c in range(3):
                dve.wait_ge(h2_loaded, 48)
                for t in range(c * THIRD, (c + 1) * THIRD):
                    dve.bn_stats(stats[:, t, :], h2[:, t, :]).then_inc(stats_ready, 1)
            dve.wait_ge(stats_ready, NT)
            me, mo, ve, vo = stats[:, :, 1], stats[:, :, 4], stats[:, :, 2], stats[:, :, 5]
            done(dve.tensor_tensor(st["sum"][:], me, mo, ALU.add))
            done(dve.tensor_tensor(st["diff"][:], me, mo, ALU.subtract))
            done(dve.tensor_tensor(st["diff"][:], st["diff"][:], st["diff"][:], ALU.mult))
            done(dve.tensor_tensor(st["m2"][:], ve, vo, ALU.add))
            done(dve.scalar_tensor_tensor(st["m2"][:], st["diff"][:], D / 4.0, st["m2"][:], ALU.mult, ALU.add))
            dve.wait_ge(std_rooted, 1)
            done(dve.reciprocal(st["std"][:], st["std"][:]))
            done(dve.scalar_tensor_tensor(st["shift"][:], st["sum"][:], -0.5, st["std"][:], ALU.mult, ALU.mult))
            for t in range(NT):
                dve.tensor_scalar(x2[:, t, :], h2[:, t, :], st["std"][:, t:t + 1], st["shift"][:, t:t + 1], ALU.mult,
                                  ALU.add).then_inc(x2_ready, 1)

            for n in range(NB):
                dve.wait_ge(logits_filled, n + 1)
                dve.tensor_reduce(bmax[:, n:n + 1], seven[n][:, 0:TB], AX, ALU.max).then_inc(bmax_ready, 1)
            dve.wait_ge(bmax_ready, NB)
            dve.tensor_reduce(nmax[:], bmax[:], AX, ALU.max).then_inc(psum_step, 1)
            dve.wait_ge(psum_step, 1)
            dve.tensor_scalar(nmax[:], nmax[:], -1.0, None, ALU.mult).then_inc(nmax_ready, 1)
            dve.wait_ge(exp_ready, NB)
            dve.tensor_reduce(psum_inv[:], bsum[:], AX, ALU.add).then_inc(psum_step, 1)
            dve.wait_ge(psum_step, 2)
            dve.reciprocal(psum_inv[:], psum_inv[:]).then_inc(psum_step, 1)
            dve.wait_ge(psum_step, 3)
            dve.tensor_scalar(probs[:], probs[:], psum_inv[:], None, ALU.mult).then_inc(probs_ready, 1)
            dve.wait_ge(probs_ready, 1)

            for r, shift in enumerate(SHIFTS):
                dve.tensor_tensor(thr[:], low[:], trial[:, r:r + 1], ALU.bitwise_or).then_inc(thr_ready, 1)
                dve.wait_ge(thr_ready, r + 1)
                dve.tensor_scalar(above[:], probs[:], thr[:].bitcast(F32), 0.0, ALU.is_ge, ALU.add,
                                  accum_out=count[:]).then_inc(counted, 1)
                dve.wait_ge(counted, r + 1)
                dve.tensor_scalar(enough[:], count[:], float(TOP), None, ALU.is_ge).then_inc(enough_ready, 1)
                dve.wait_ge(digits_filled, r + 1)
                share = 1.0 if r < ROUNDS - 1 else 4.0 / REPS
                dve.tensor_scalar(digit[:], count_bank[:, 0:1], share, -1.0, ALU.mult, ALU.add).then_inc(digit_ready, 1)
                dve.wait_ge(digit_ready, 2 * r + 1)
                dve.tensor_scalar(digit[:], digit[:], shift, None, ALU.logical_shift_left).then_inc(digit_ready, 1)
                dve.wait_ge(digit_ready, 2 * r + 2)
                dve.tensor_tensor(low[:], low[:], digit[:], ALU.bitwise_or).then_inc(low_ready, 1)
                dve.wait_ge(low_ready, r + 1)

            at = low[0:E, :].bitcast(F32)
            dve.tensor_scalar(above[0:E, :], probs[0:E, :], at, 0.0, ALU.is_gt, ALU.add,
                              accum_out=count[0:E, :]).then_inc(gate_step, 1)
            dve.tensor_scalar(ties[:], probs[0:E, :], at, None, ALU.is_equal).then_inc(gate_step, 1)
            dve.wait_ge(gate_step, 2)
            dve.tensor_tensor_scan(ranks[:], ties[:], ties[:], 0.0, ALU.add, ALU.max).then_inc(gate_step, 1)
            dve.tensor_scalar(need[0:E, :], count[0:E, :], -1.0, float(TOP), ALU.mult, ALU.add).then_inc(gate_step, 1)
            dve.wait_ge(gate_step, 4)
            dve.scalar_tensor_tensor(ties[:], ranks[:], need[0:E, :], ties[:], ALU.is_le, ALU.mult).then_inc(gate_step, 1)
            dve.wait_ge(gate_step, 5)
            dve.tensor_tensor(above[0:E, :], above[0:E, :], ties[:], ALU.add).then_inc(gate_step, 1)
            dve.wait_ge(gate_step, 6)
            dve.tensor_tensor(above[0:E, :], above[0:E, :], probs[0:E, :], ALU.mult).then_inc(gates_ready, 1)
            dve.wait_ge(gates_turned, 1)
            dve.tensor_copy(gate[:].rearrange("p t e -> p (t e)"), gate_bank).then_inc(gate_ready, 1)
            dve.wait_ge(gate_ready, 1)

            free = [banks[3][:, 1, :], banks[2][:, 1, :]]
            for g in range((NT + 3) // 4):
                n = min(4, NT - 4 * g)
                dve.wait_ge(bias_filled, g + 1)
                dve.tensor_tensor(acc[:, 4 * g:4 * g + n, :].rearrange("p t d -> p (t d)"), free[g % 2][:, 0:n * D],
                                  h2[:, 4 * g:4 * g + n, :].rearrange("p t d -> p (t d)"), ALU.add).then_inc(acc_ready, 1)
            groups = (NT + 3) // 4
            dve.wait_ge(y_kept, AHEAD * NB)
            dve.wait_ge(acc_ready, groups)
            for e in range(AHEAD):
                with dve.Fori(0, NT) as t:
                    if e:
                        dve.wait_ge(acc_ready, t + (groups + 1))
                    tile = acc[:, bass.ds(t, 1), :].rearrange("p t d -> p (t d)")
                    dve.scalar_tensor_tensor(tile, ahead[:, e, bass.ds(t, 1), :].rearrange("p t d -> p (t d)"),
                                             gate[:, bass.ds(t, 1), e:e + 1].rearrange("p t e -> p (t e)"), tile,
                                             ALU.mult, ALU.add).then_inc(acc_ready, 1)
            dve.wait_ge(acc_ready, groups + AHEAD * NT)
            with dve.Fori(AHEAD, E) as e:
                with dve.Fori(0, NB) as n:
                    dve.wait_ge(y_filled, e * NB + n + 1)
                    for k in range(TPB):
                        t = n * TPB + k
                        tile = acc[:, bass.ds(t, 1), :].rearrange("p t d -> p (t d)")
                        dve.scalar_tensor_tensor(tile, y_bank[:, k * D:(k + 1) * D],
                                                 gate[:, bass.ds(t, 1), bass.ds(e, 1)].rearrange("p t e -> p (t e)"), tile,
                                                 ALU.mult, ALU.add).then_inc(y_added, 1)


_INS = ['x', 'L0_tok_W', 'L0_tok_b', 'L0_tok_effective_scale', 'L0_attn_w_qkv', 'L0_attn_w_proj', 'L0_attn_b_proj',
        'L0_attn_w_e', 'L0_attn_b_e', 'L0_attn_w_s', 'L0_attn_b_s', 'L0_attn_w_h', 'L0_attn_b_h', 'L0_attn_alpha',
        'L0_attn_beta', 'L0_attn_gamma', 'L0_attn_temperature', 'L0_ffn_Wr', 'L0_ffn_W1', 'L0_ffn_b1', 'L0_ffn_W2',
        'L0_ffn_b2']
_OUTS = [((32, 84, 128), 'float32')]


def kernel(**inputs):
    import numpy as _np
    import concourse.bacc as _bacc
    from concourse import mybir as _mybir
    from concourse.bass_utils import run_bass_kernel_spmd as _run

    nc = _bacc.Bacc("TRN2", target_bir_lowering=False, num_devices=1)
    arrays, args = {}, []
    for name in _INS:
        a = _np.ascontiguousarray(inputs[name])
        if a.ndim == 0:
            a = a.reshape(1)
        arrays[f"in_{name}_dram"] = a
        args.append(nc.dram_tensor(f"in_{name}_dram", a.shape, _mybir.dt.from_np(a.dtype), kind="ExternalInput").ap())
    for i, (shape, dtype) in enumerate(_OUTS):
        dt = _mybir.dt.from_np(_np.dtype(dtype))
        args.append(nc.dram_tensor(f"out_{i}_dram", shape, dt, kind="ExternalOutput").ap())
    tower(nc, *args)
    r = _run(nc, [arrays], core_ids=[0])
    got = tuple(r.results[0][f"out_{i}_dram"] for i in range(len(_OUTS)))
    return got[0]
```

```python
from contextlib import ExitStack

import numpy as np

import concourse.bass as bass
from concourse import mybir

F32 = mybir.dt.float32
F32R = mybir.dt.float32r
I32 = mybir.dt.int32
ALU = mybir.AluOpType
ACT = mybir.ActivationFunctionType
AX = mybir.AxisListType.X

P = 128
SEG, STRIDE = 48, 24
BALL_EPS, MIN_NORM = 0.004, 1e-15
HEADS, DH = 8, 64
DE, DS, DHY = 64, 64, 32
FEAT = DE + DS + DHY
LN_EPS = 1e-5
TINY = 2.0 ** -60
SIM_MAX = float(np.float32(1.0 - 1e-6))
ARG_MIN_HALF = float((np.float32(1.0 + 1e-6) - np.float32(1.0)) / 2)
NORM_SHIFT = 20
TOP = 1024
TB = 384
SET_SQRT, SET_LN_EXP, SET_ATAN_TANH = "sqrt_and_others", "natural_log_exp_and_others", "sigmoid_and_others"


def tower(nc, x, tok_W, tok_b, effective_scale, w_qkv, w_proj, b_proj, w_e, b_e, w_s, b_s, w_h, b_h,
          alpha, beta, gamma, temperature, Wr, W1, b1, W2, b2, out):
    B, L = x.shape
    D = tok_W.shape[1]
    N = (L - SEG) // STRIDE + 1
    T = B * N
    E, _, F = W1.shape
    NT = T // P
    NB = T // TB
    TPB = TB // P
    FC = F // P
    PAIRS = B // 2
    W2N = 2 * N
    INNER = HEADS * DH
    assert D == P and T == NT * P and T == NB * TB and B % 8 == 0 and P % E == 0

    h2_dram = nc.dram_tensor("h2_scratch", (T, D), F32, kind="Internal").ap()

    with ExitStack() as ctx:
        banks = [ctx.enter_context(nc.psum_tensor(f"slot{k}", [P, 2, 512], F32)) for k in range(4)]
        ident = ctx.enter_context(nc.sbuf_tensor("ident", [P, P], F32))
        h2 = ctx.enter_context(nc.sbuf_tensor("h2", [P, NT, D], F32))
        h2_stats = ctx.enter_context(nc.sbuf_tensor("h2_stats", [P, NT, 6], F32))
        h2_saved = ctx.enter_context(nc.semaphore("h2_saved"))
        early_loaded = ctx.enter_context(nc.semaphore("early_loaded"))
        early_stats = ctx.enter_context(nc.semaphore("early_stats"))
        early = (PAIRS - 1) * W2N // P
        handover = (h2, h2_stats, h2_dram, h2_saved, early_loaded, early_stats, early)
        embed_and_attend(nc, (B, L, D, N, PAIRS, W2N, INNER), banks, ident, handover, x, tok_W, tok_b, effective_scale,
                         w_qkv, w_proj, b_proj, w_e, b_e, w_s, b_s, w_h, b_h, alpha, beta, gamma, temperature)
        experts(nc, (D, T, E, F, NT, NB, TPB, FC, PAIRS), banks, ident, handover, Wr, W1, b1, W2, b2, out)


def embed_and_attend(nc, dims, banks, ident, handover, x, tok_W, tok_b, effective_scale,
                     w_qkv, w_proj, b_proj, w_e, b_e, w_s, b_s, w_h, b_h, alpha, beta, gamma, temperature):
    B, L, D, N, PAIRS, W2N, INNER = dims
    h2, h2_stats, h2_dram, h2_saved, early_loaded, early_stats, early = handover
    QT = HEADS // 2
    HT = HEADS // 4
    CH = 4
    with ExitStack() as ctx:
        def sb(name, shape, dt=F32):
            return ctx.enter_context(nc.sbuf_tensor(name, shape, dt))

        block64 = sb("block64", [P, P])
        block32 = sb("block32", [P, P])
        pick2 = sb("pick2", [P, 2, N])
        pick4 = sb("pick4", [P, 4, N])
        shift_bias = sb("shift_bias", [P, 1])
        eps_bias = sb("eps_bias", [P, 1])
        seg_w = sb("seg_w", [SEG + 1, D])
        w_heads = sb("w_heads", [DH, 2 * HEADS, D])
        w_es = sb("w_es", [DE + DS, DH])
        w_hy = sb("w_hy", [DHY, DH])
        w_v = sb("w_v", [P, 4, D])
        w_p = sb("w_p", [P, INNER])
        featT = sb("featT", [DH, FEAT])
        comp_e = sb("comp_e", [P, 2 * HEADS * DE])
        comp_s = sb("comp_s", [P, 2 * HEADS * DS])
        comp_h = sb("comp_h", [P, 2 * HEADS * DHY])
        w_vT = sb("w_vT", [P, INNER])
        w_pT = sb("w_pT", [P, 4, D])
        be2 = sb("be2", [P, 1])
        bs2 = sb("bs2", [P, 1])
        bh4 = sb("bh4", [P, 1])
        bproj = sb("bproj", [P, D])
        raw5 = sb("raw5", [P, 5])
        sp_abs = sb("sp_abs", [P, 4])
        sp = sb("sp", [P, 4])
        scale_t = sb("scale_t", [P, 1])
        c_e2 = sb("c_e2", [P, 1])
        c_s = sb("c_s", [P, 1])
        c_h = sb("c_h", [P, 1])

        seg = [sb(f"seg{k}", [N, CH, SEG]) for k in range(2)]
        segT = [sb(f"segT{k}", [SEG + 1, CH * N]) for k in range(2)]
        u = sb("u", [N, B, D])
        stats = sb("stats", [N, B, 6])
        st = {n: sb(f"st_{n}", [N, B]) for n in ("sum", "mean", "diff", "m2", "sq", "norm", "unorm", "th",
                                                 "f", "yn", "clip", "var", "std", "gain", "shift")}

        xn = sb("xn", [N, 2, D])
        xT = sb("xT", [P, PAIRS, W2N])
        xT_old = sb("xT_old", [P, W2N])
        eq, eq_sq, ek_sq = (sb(n, [P, QT, W2N]) for n in ("eq", "eq_sq", "ek_sq"))
        ek_m2 = sb("ek_m2", [P, QT, 2, W2N])
        s_raw = sb("s_raw", [P, 2, QT, W2N])
        s_sq = sb("s_sq", [P, 2, QT, W2N])
        s_inv = sb("s_inv", [P, 2, QT, W2N])
        sq_n = sb("sq_n", [P, QT, W2N])
        sk_n = sb("sk_n", [P, QT, 2, W2N])
        hqk = sb("hqk", [P, 2, HT, W2N])
        hqk_sq = sb("hqk_sq", [P, 2, HT, W2N])
        one_un = sb("one_un", [P, HT, W2N])
        hk_m2 = sb("hk_m2", [P, HT, 4, W2N])
        hk_den = sb("hk_den", [P, HT, 4, W2N])
        v_aug = sb("v_aug", [N, 2, HEADS, DH + 1])
        esb, csb, den, mq, rden, droot, dist, su, sh, hs, hr, attnT = (
            sb(n, [N, 2, HEADS * N]) for n in ("esb", "csb", "den", "mq", "rden", "droot", "dist", "su", "sh", "hs",
                                               "hr", "attnT"))
        eq_norm = sb("eq_norm", [N, 2, 2, 4])
        hq_norm = sb("hq_norm", [N, 2, 2, 4])
        dmin = sb("dmin", [N, 2 * HEADS])
        rsum = sb("rsum", [N, 2, HEADS])
        o_tok = [sb(f"o_tok{k}", [N, HEADS, DH]) for k in range(2)]
        oT = [sb(f"oT{k}", [P, 4, N]) for k in range(2)]
        hres = sb("hres", [N, 2, D])
        h2_out = sb("h2_out", [N, 2, D])

        def sem(name):
            return ctx.enter_context(nc.semaphore(name))

        (ident_zero, ident_ready, consts_set, picks_set, seg_w_loaded, weights_loaded, params_loaded, segT_ready,
         z_filled, u_ready, stats_ready, ones_set, stat_step, stat_root, softplus_step, c_ready, scale_ready,
         w_turned, featT_ready, wvp_turned, wvp_ready, comp_filled, comp_ready, xn_ready, xT_filled, xT_ready,
         eq_filled, eq_ready, eq_squared, ek_filled, ek_squared, ek_ready, sqf_filled, sqf_ready, skf_filled,
         skf_ready, sq_squared, sk_squared, snq_filled, snk_filled, s_norm_ready, s_inv_step, s_inv_ready, sn_ready,
         hf_filled, hf_ready, h_squared, un_filled, un_ready, hk_den_ready, sq_unit, v_filled,
         v_placed, e_filled, e_read, s_filled, s_read, hden_filled, den_ready, hdns_filled, mq_ready, rden_step,
         rden_ready, mq_scaled, q_ready, dist_rooted, su_rooted, sh_rooted, hs_rooted, hr_rooted, w_step,
         w_ready, t_ready, atan_ready, g_ready, log_ready, dmin_ready, dist_shifted, exp_ready, attn_turned,
         attnT_ready, pv_filled, rsum_ready, o_ready, o_turned, oT_ready, proj_filled, hres_ready, h2_ready,
         q_masked, esb_ready, eq_norm_ready, hq_norm_ready, dist_es, dist_whole, xT_old_ready) = (
             sem(n) for n in """ident_zero ident_ready consts_set picks_set seg_w_loaded weights_loaded params_loaded segT_ready
                 z_filled u_ready stats_ready ones_set stat_step stat_root softplus_step c_ready scale_ready
                 w_turned featT_ready wvp_turned wvp_ready comp_filled comp_ready xn_ready xT_filled xT_ready
                 eq_filled eq_ready eq_squared ek_filled ek_squared ek_ready sqf_filled sqf_ready skf_filled
                 skf_ready sq_squared sk_squared snq_filled snk_filled s_norm_ready s_inv_step s_inv_ready sn_ready hf_filled
                 hf_ready h_squared un_filled un_ready hk_den_ready sq_unit v_filled v_placed
                 e_filled e_read s_filled s_read hden_filled den_ready hdns_filled mq_ready rden_step rden_ready
                 mq_scaled q_ready dist_rooted su_rooted sh_rooted hs_rooted hr_rooted w_step w_ready t_ready
                 atan_ready g_ready log_ready dmin_ready dist_shifted exp_ready attn_turned attnT_ready pv_filled
                 rsum_ready o_ready o_turned oT_ready proj_filled hres_ready h2_ready q_masked esb_ready eq_norm_ready hq_norm_ready dist_es dist_whole
                 xT_old_ready""".split())
        seg_freed = [ctx.enter_context(nc.semaphore(f"seg_freed{k}")) for k in range(2)]
        seg_in = [ctx.enter_context(nc.semaphore(f"seg_in{k}")) for k in range(2)]
        block = ctx.enter_context(nc.Block())

        CHUNKS = B // CH
        COMP = [(g, min(3, 2 * HEADS - g)) for g in range(0, 2 * HEADS, 3)]
        COMP_AT = [(2, 0), (2, 1), (3, 0), (3, 1), (1, 1), (0, 0)]

        @block.sync
        def _(sp):
            def load_seg(c, k):
                src = bass.AP(x.tensor, c * (CH * L), [[STRIDE, N], [L, CH], [1, SEG]])
                sp.dma_start(seg[k][:], src).then_inc(seg_in[k], 16)

            load_seg(0, 0)
            load_seg(1, 1)
            sp.dma_start(seg_w[0:SEG, :], tok_W).then_inc(seg_w_loaded, 16)
            sp.dma_start(seg_w[SEG:SEG + 1, :], tok_b.unsqueeze(0)).then_inc(seg_w_loaded, 16)
            sp.dma_start(raw5[:, 4:5], effective_scale.unsqueeze(0).broadcast_to([P, 1])).then_inc(params_loaded, 16)
            for j, a in enumerate((alpha, beta, gamma, temperature)):
                sp.dma_start(raw5[:, j:j + 1], a.unsqueeze(0).broadcast_to([P, 1])).then_inc(params_loaded, 16)
            with sp.Fori(1, CHUNKS // 2) as i:
                for k in range(2):
                    sp.wait_ge(seg_freed[k], i)
                    load_seg(2 * i + k, k)
            sp.dma_start(w_heads[:], w_qkv[0:2 * INNER, :].rearrange("(g d) c -> d g c", d=DH)).then_inc(weights_loaded, 16)
            sp.dma_start(w_v[:], w_qkv[2 * INNER:3 * INNER, :].rearrange("(k p) c -> p k c", p=P)).then_inc(weights_loaded, 16)
            sp.dma_start(w_p[:], w_proj).then_inc(weights_loaded, 16)
            sp.dma_start(w_es[0:DE, :], w_e).then_inc(weights_loaded, 16)
            sp.dma_start(w_es[DE:DE + DS, :], w_s).then_inc(weights_loaded, 16)
            sp.dma_start(w_hy[:], w_h).then_inc(weights_loaded, 16)
            for k in range(2):
                sp.dma_start(be2[k * DE:(k + 1) * DE, :], b_e.unsqueeze(1)).then_inc(weights_loaded, 16)
                sp.dma_start(bs2[k * DS:(k + 1) * DS, :], b_s.unsqueeze(1)).then_inc(weights_loaded, 16)
            for k in range(4):
                sp.dma_start(bh4[k * DHY:(k + 1) * DHY, :], b_h.unsqueeze(1)).then_inc(weights_loaded, 16)
            sp.dma_start(bproj[:], b_proj.unsqueeze(0).broadcast_to([P, D])).then_inc(weights_loaded, 16)

            def save_pair(p):
                sp.wait_ge(h2_ready, 2 * p + 2)
                dst = h2_dram[bass.ds(p * W2N, W2N), :].rearrange("(b n) c -> n b c", n=N)
                sp.dma_start(dst, h2_out[:]).then_inc(h2_saved, 16)

            with sp.Fori(0, PAIRS - 1) as p:
                save_pair(p)
            sp.wait_ge(h2_saved, 16 * (PAIRS - 1))
            sp.dma_start(h2[:, 0:early, :], h2_dram[0:early * P, :].rearrange("(t p) c -> p t c", p=P))\
              .then_inc(early_loaded, 16)
            save_pair(PAIRS - 1)
        WEIGHTS = 16 * 15
        PARAMS = 16 * 5

        @block.gpsimd
        def _(pool):
            pool.memset(ident[:], 0.0).then_inc(ident_zero, 1)
            pool.wait_ge(ident_zero, 1)
            pool.affine_select(out=ident[:], in_=ident[:], compare_op=ALU.not_equal, fill=1.0, base=0,
                               pattern=[[-1, P]], channel_multiplier=1).then_inc(ident_ready, 1)
            for t in (ek_m2, sk_n, hk_m2, hk_den, block64, block32, pick2, pick4):
                last = pool.memset(t[:], 0.0)
            last.then_inc(consts_set, 1)
            pool.memset(v_aug[:, :, :, DH:DH + 1], 1.0).then_inc(consts_set, 1)
            pool.memset(shift_bias[:], float(NORM_SHIFT * np.log(2.0) / 2)).then_inc(consts_set, 1)

            def features(nxt):
                pool.wait_ge(sqf_ready, nxt + 1)
                pool.tensor_tensor(s_sq[:, 0], s_raw[:, 0], s_raw[:, 0], ALU.mult).then_inc(sq_squared, 1)
                pool.wait_ge(eq_ready, nxt + 1)
                pool.tensor_tensor(eq_sq[:], eq[:], eq[:], ALU.mult).then_inc(eq_squared, 1)

            def unit_queries(nxt):
                pool.wait_ge(s_inv_ready, nxt + 1)
                pool.tensor_tensor(sq_n[:], s_raw[:, 0], s_inv[:, 0], ALU.mult).then_inc(sq_unit, 1)

            def scale_mq(nxt):
                pool.wait_ge(mq_ready, 2 * nxt + 2)
                pool.wait_ge(rden_ready, nxt + 1)
                pool.tensor_tensor(mq[:], mq[:], rden[:], ALU.mult).then_inc(mq_scaled, 1)

            def add_roots(cur):
                pool.wait_ge(hs_rooted, cur + 1)
                pool.wait_ge(hr_rooted, cur + 1)
                pool.tensor_tensor(hs[:], hs[:], hr[:], ALU.add).then_inc(g_ready, 1)

            def tangent(cur):
                pool.wait_ge(su_rooted, cur + 1)
                pool.wait_ge(w_ready, cur + 1)
                pool.tensor_tensor(su[:], su[:], sh[:], ALU.mult).then_inc(t_ready, 1)

            def cycle(i, new=True, mid=True, old=True):
                if old:
                    add_roots(i - 2)
                if new:
                    features(i)
                    unit_queries(i)
                if mid:
                    tangent(i - 1)
                    scale_mq(i - 1)

            cycle(0, mid=False, old=False)
            cycle(1, old=False)
            cycle(2)
            with pool.Fori(3, PAIRS - 1) as i:
                cycle(i)
            cycle(PAIRS - 1)
            cycle(PAIRS, new=False)

        @block.tensor
        def _(pe):
            pe.wait_ge(ident_ready, 1)
            pe.wait_ge(seg_w_loaded, 32)
            def turn_segments(k, loaded):
                pe.wait_ge(seg_in[k], loaded)
                for j in range(CH):
                    last = pe.matmul(banks[k][0:SEG, 0, j * N:(j + 1) * N], seg[k][:, j, :], ident[0:N, 0:N],
                                     start=True, stop=True)
                last.then_inc(seg_freed[k], 1)

            def embed(c, k, first=False):
                pe.wait_ge(segT_ready, c + 1)
                if not first:
                    pe.wait_ge(u_ready, c - 1)
                for j in range(CH):
                    last = pe.matmul(banks[2 + k][0:N, 0, j * D:(j + 1) * D], segT[k][:, j * N:(j + 1) * N],
                                     seg_w[:], start=True, stop=True)
                last.then_inc(z_filled, 1)

            for k in range(2):
                turn_segments(k, 16)
            for k in range(2):
                embed(k, k, first=True)
                turn_segments(k, 32)
            with pe.Fori(1, CHUNKS // 2 - 1) as i:
                for k in range(2):
                    embed(2 * i + k, k)
                    turn_segments(k, 16 * i + 32)
            for k in range(2):
                embed(CHUNKS - 2 + k, k)

            pe.wait_ge(weights_loaded, WEIGHTS)
            pe.wait_ge(segT_ready, CHUNKS)
            pe.wait_ge(u_ready, CHUNKS)
            pe.transpose(banks[0][0:DH, 0, 0:P], w_es[:], ident[:])
            pe.transpose(banks[0][0:DH, 0, P:FEAT], w_hy[:], ident[0:DHY, 0:DHY]).then_inc(w_turned, 1)
            for k in range(4):
                pe.transpose(banks[0][:, 1, k * P:(k + 1) * P], w_v[:, k, :], ident[:])
            for k in range(4):
                last = pe.transpose(banks[1][:, 0, k * P:(k + 1) * P], w_p[:, k * P:(k + 1) * P], ident[:])
            last.then_inc(wvp_turned, 1)
            pe.wait_ge(featT_ready, 1)
            for (g0, n), (sl, bk) in zip(COMP, COMP_AT):
                for j in range(n):
                    last = pe.matmul(banks[sl][:, bk, j * FEAT:(j + 1) * FEAT], w_heads[:, g0 + j, :], featT[:],
                                     start=True, stop=True)
                last.then_inc(comp_filled, 1)
            pe.wait_ge(comp_ready, len(COMP))
            pe.wait_ge(wvp_ready, 2)
            pe.wait_ge(picks_set, 12)

            def four(slot, comp, t0, nxt):
                for j in range(4):
                    last = pe.matmul(slot[:, j // 2, (j % 2) * W2N:(j % 2 + 1) * W2N],
                                     comp[:, (t0 + j) * P:(t0 + j + 1) * P],
                                     xT[:, bass.ds(nxt, 1), :].rearrange("p a w -> p (a w)"), start=True, stop=True)
                return last

            slot0, slot1, slot2, slot3 = banks

            def tokens_turned(nxt, first=False):
                if not first:
                    pe.wait_ge(v_placed, nxt - 1)
                pe.wait_ge(xn_ready, 2 * nxt + 2)
                for j in range(2):
                    last = pe.transpose(slot0[:, 0, j * N:(j + 1) * N], xn[:, j, :], ident[0:N, 0:N])
                last.then_inc(xT_filled, 1)

            def hyperbolic_scores(mid, first_cycles, with_new):
                pe.wait_ge(un_ready, mid + 1)
                pe.wait_ge(hk_den_ready, 4 * mid + 4)
                for b, (den_slot, dist_slot) in enumerate(((slot1, slot2), (slot3, slot0))):
                    tok = slice(b * N, (b + 1) * N)
                    if b == 1 and not first_cycles:
                        pe.wait_ge(h2_ready, 2 * mid - 2)
                    for t in range(HT):
                        last = pe.matmul(den_slot[0:N, t, 0:4 * N], one_un[:, t, tok], hk_den[:, t, :, tok],
                                         start=True, stop=True)
                    last.then_inc(hden_filled, 1)
                    if b == 0 and with_new:
                        tokens_turned(mid + 1, first_cycles and mid == 0)
                    if b == 0 and not first_cycles:
                        pe.wait_ge(h2_ready, 2 * mid - 3)
                    elif b == 1 and with_new:
                        pe.wait_ge(xT_ready, mid + 2)
                    elif b == 1:
                        pe.wait_ge(v_placed, mid)
                    for t in range(HT):
                        o = dist_slot[0:N, t, 0:4 * N]
                        for h in range(4):
                            pe.matmul(dist_slot[0:N, t, h * N:(h + 1) * N], pick4[:, h, :], hqk_sq[:, 1, t, tok],
                                      start=(h == 0), stop=False, skip_group_check=True)
                        pe.matmul(dist_slot[0:N, t, 4 * N:4 * N + 4], hqk_sq[:, 0, t, tok], pick4[:, :, 0], start=False,
                                  stop=True, skip_group_check=True)
                        last = pe.matmul(o, hqk[:, 0, t, tok], hk_m2[:, t, :, tok], start=False, stop=True,
                                         skip_group_check=True)
                    last.then_inc(hdns_filled, 1)

            def features(nxt, with_mid):
                pe.wait_ge(xT_ready, nxt + 1)
                for slot, comp, t0, filled, read, count in ((slot1, comp_e, QT, ek_filled, den_ready, 2 * nxt - 1),
                                                            (slot2, comp_s, 0, sqf_filled, mq_ready, 2 * nxt - 1),
                                                            (slot3, comp_s, QT, skf_filled, den_ready, 2 * nxt),
                                                            (slot0, comp_e, 0, eq_filled, mq_ready, 2 * nxt)):
                    if with_mid:
                        pe.wait_ge(read, count)
                    four(slot, comp, t0, nxt).then_inc(filled, 1)

            def pair_out(sl, j, half):
                return sl[0:N, j, half * W2N:(half + 1) * W2N]

            def euclid(nxt):
                pe.wait_ge(eq_squared, nxt + 1)
                for b, sl in enumerate((slot3, slot0)):
                    tok = slice(b * N, (b + 1) * N)
                    for j in range(2):
                        for h in range(2):
                            o = sl[0:N, j, 0:4 * N].rearrange("p (t h m) -> p t h m", t=2, h=2)[:, :, h, :]
                            pe.matmul(o, pick2[:, h, :], ek_sq[:, 2 * j:2 * j + 2, tok], start=(h == 0),
                                      stop=False, skip_group_check=True)
                        for half in range(2):
                            t = 2 * j + half
                            pe.matmul(sl[0:N, j, 4 * N + 2 * half:4 * N + 2 * half + 2], eq_sq[:, t, tok], pick2[:, :, 0],
                                      start=False, stop=True, skip_group_check=True)
                            last = pe.matmul(pair_out(sl, j, half), eq[:, t, tok], ek_m2[:, t, :, tok],
                                             start=False, stop=(half == 1), skip_group_check=True)
                    last.then_inc(e_filled, 1)

            def spherical_norms(nxt):
                pe.wait_ge(ek_ready, 2 * nxt + 2)
                for side, (sl, squared, signal) in enumerate(((slot1, sq_squared, snq_filled),
                                                              (slot2, sk_squared, snk_filled))):
                    pe.wait_ge(squared, nxt + 1)
                    for j in range(2):
                        last = pe.matmul(sl[:, j, 0:2 * W2N], block64[:], s_sq[:, side, 2 * j:2 * j + 2, :],
                                         start=True, stop=True)
                    last.then_inc(signal, 1)

            def values(mid, with_new):
                if with_new:
                    pe.wait_ge(s_read, 2 * mid + 3)
                else:
                    pe.wait_ge(mq_ready, 2 * PAIRS)
                pe.wait_ge(xT_old_ready, mid + 1)
                for j in range(2):
                    last = pe.matmul(slot0[0:N, j, 0:INNER], xT_old[:, j * N:(j + 1) * N], w_vT[:], start=True, stop=True)
                last.then_inc(v_filled, 1)

            def hyperbolic_features(nxt):
                pe.wait_ge(s_norm_ready, 2 * nxt + 1)
                for side in range(2):
                    for j in range(HT):
                        t = side * HT + j
                        last = pe.matmul(slot1[:, side, j * W2N:(j + 1) * W2N], comp_h[:, t * P:(t + 1) * P],
                                         xT[:, bass.ds(nxt, 1), :].rearrange("p a w -> p (a w)"), start=True, stop=True)
                last.then_inc(hf_filled, 1)

            def attention_turned(old, with_new, with_mid):
                pe.wait_ge(exp_ready, old + 1)
                if not with_new and with_mid:
                    pe.wait_ge(mq_ready, 2 * PAIRS - 1)
                    pe.wait_ge(den_ready, 2 * PAIRS)
                elif not with_new:
                    pe.wait_ge(h2_ready, 2 * old)
                for b, sl in enumerate((slot2, slot3)):
                    if with_new and b == 0:
                        pe.wait_ge(s_norm_ready, 2 * old + 6)
                    elif with_new:
                        pe.wait_ge(e_read, 2 * old + 5)
                    for h in range(HEADS):
                        last = pe.transpose(sl[0:N, h // 4, (h % 4) * N:(h % 4 + 1) * N],
                                            dist[:, b, h * N:(h + 1) * N], ident[0:N, 0:N])
                    last.then_inc(attn_turned, 1)

            def sphere(nxt):
                pe.wait_ge(sq_unit, nxt + 1)
                pe.wait_ge(sn_ready, 2 * nxt + 2)
                for b, sl in enumerate((slot0, slot1)):
                    if b == 0:
                        pe.wait_ge(e_read, 2 * nxt + 2)
                    else:
                        pe.wait_ge(hf_ready, nxt + 1)
                    tok = slice(b * N, (b + 1) * N)
                    for t in range(QT):
                        last = pe.matmul(pair_out(sl, t // 2, t % 2), sq_n[:, t, tok], sk_n[:, t, :, tok],
                                         start=True, stop=True)
                    last.then_inc(s_filled, 1)

            def hyperbolic_norms(nxt):
                pe.wait_ge(h_squared, nxt + 1)
                pe.wait_ge(s_read, 2 * nxt + 2)
                pe.matmul(slot1[:, 0, 0:HT * W2N], block32[:], hqk_sq[:, 0], start=True, stop=True).then_inc(un_filled, 1)

            def attention_times_values(old):
                pe.wait_ge(v_placed, old + 1)
                for b, sl in enumerate((slot2, slot3)):
                    pe.wait_ge(attnT_ready, 2 * old + b + 1)
                    for h in range(HEADS):
                        last = pe.matmul(sl[0:N, h // 4, (h % 4) * (DH + 1):(h % 4 + 1) * (DH + 1)],
                                         attnT[:, b, h * N:(h + 1) * N], v_aug[:, b, h, :], start=True, stop=True)
                    last.then_inc(pv_filled, 1)

            def output_turned(old):
                for b, sl in enumerate((slot2, slot3)):
                    pe.wait_ge(o_ready, 4 * old + 2 * b + 2)
                    for k in range(4):
                        last = pe.transpose(sl[:, 0, k * N:(k + 1) * N],
                                            o_tok[b][:, 2 * k:2 * k + 2, :].rearrange("p h d -> p (h d)"), ident[0:N, 0:N])
                    last.then_inc(o_turned, 1)

            def output(old):
                for b, sl in enumerate((slot2, slot3)):
                    pe.wait_ge(oT_ready, 2 * old + b + 1)
                    for k in range(4):
                        last = pe.matmul(sl[0:N, 1, 0:D], oT[b][:, k, :], w_pT[:, k, :], start=(k == 0), stop=(k == 3))
                    last.then_inc(proj_filled, 1)

            def cycle(i, new=True, mid=True, old=True, first_cycles=False):
                if mid:
                    hyperbolic_scores(i - 1, first_cycles, new)
                if new:
                    features(i, mid)
                    spherical_norms(i)
                    euclid(i)
                    hyperbolic_features(i)
                if old:
                    attention_turned(i - 2, new, mid)
                if new:
                    sphere(i)
                if old:
                    attention_times_values(i - 2)
                    output_turned(i - 2)
                if mid:
                    values(i - 1, new)
                if new:
                    hyperbolic_norms(i)
                if old:
                    output(i - 2)

            tokens_turned(0, first=True)
            cycle(0, mid=False, old=False)
            cycle(1, old=False, first_cycles=True)
            cycle(2, first_cycles=True)
            with pe.Fori(3, PAIRS - 1) as i:
                cycle(i)
            cycle(PAIRS - 1)
            cycle(PAIRS, new=False)
            cycle(PAIRS + 1, new=False, mid=False)

        @block.scalar
        def _(act):
            act.wait_ge(params_loaded, PARAMS)
            act.activation(scale_t[:], raw5[:, 4:5], ACT.Tanh).then_inc(scale_ready, 1)
            act.activation(sp_abs[:], raw5[:, 0:4], ACT.Abs).then_inc(softplus_step, 1)
            act.wait_ge(softplus_step, 1)
            act.preload_act_table_set(SET_LN_EXP)
            act.activation(sp_abs[:], sp_abs[:], ACT.Exp, scale=-1.0).then_inc(softplus_step, 1)
            act.wait_ge(softplus_step, 2)
            act.activation(sp_abs[:], sp_abs[:], ACT.Ln, bias=1.0).then_inc(softplus_step, 1)
            act.wait_ge(scale_ready, 1)
            act.wait_ge(ones_set, 1)
            act.preload_act_table_set(SET_SQRT)

            def keep_turned_segments(k, turned):
                act.wait_ge(seg_freed[k], turned)
                act.copy(segT[k][0:SEG, :], banks[k][0:SEG, 0, 0:CH * N]).then_inc(segT_ready, 1)

            def scale_embedding(c, k):
                act.wait_ge(z_filled, c + 1)
                act.activation(u[:, bass.ds(c * CH, CH), :].rearrange("n b d -> n (b d)"),
                               banks[2 + k][0:N, 0, :], ACT.Copy, scale=scale_t[0:N, :]).then_inc(u_ready, 1)

            for k in range(2):
                keep_turned_segments(k, 1)
            with act.Fori(0, CHUNKS // 2 - 1) as i:
                for k in range(2):
                    scale_embedding(2 * i + k, k)
                    keep_turned_segments(k, i + 2)
            for k in range(2):
                scale_embedding(CHUNKS - 2 + k, k)
            act.wait_ge(w_turned, 1)
            act.copy(featT[:], banks[0][0:DH, 0, 0:FEAT]).then_inc(featT_ready, 1)

            def composites_to_sbuf(n):
                g0, m = COMP[n]
                sl, bk = COMP_AT[n]
                act.wait_ge(comp_filled, n + 1)
                src = banks[sl][:, bk, 0:m * FEAT].rearrange("p (g f) -> p g f", f=FEAT)
                for dst, a, w in ((comp_e, 0, DE), (comp_s, DE, DS), (comp_h, DE + DS, DHY)):
                    last = act.copy(dst[:, g0 * w:(g0 + m) * w].rearrange("p (g f) -> p g f", f=w), src[:, :, a:a + w])
                last.then_inc(comp_ready, 1)

            act.wait_ge(stat_step, 8)
            act.activation(st["unorm"][:], st["norm"][:], ACT.Sqrt).then_inc(stat_root, 1)
            act.preload_act_table_set(SET_ATAN_TANH)
            act.wait_ge(stat_step, 9)
            act.activation(st["th"][:], st["norm"][:], ACT.Tanh).then_inc(stat_root, 1)
            act.preload_act_table_set(SET_SQRT)
            act.wait_ge(wvp_turned, 1)
            act.copy(w_vT[:], banks[0][:, 1, :]).then_inc(wvp_ready, 1)
            act.wait_ge(stat_step, 18)
            act.activation(st["std"][:], st["var"][:], ACT.Sqrt, bias=eps_bias[0:N, :]).then_inc(stat_root, 1)
            act.copy(w_pT[:].rearrange("p k c -> p (k c)"), banks[1][:, 0, :]).then_inc(wvp_ready, 1)
            for n in range(len(COMP)):
                composites_to_sbuf(n)

            def flat(ap):
                return ap.rearrange("p a b -> p (a b)")

            def feature_evacuation(nxt):
                slots = [banks[k][:, :, 0:2 * W2N] for k in range(4)]

                def tiles(ap):
                    return ap.rearrange("p (j t) w -> p j (t w)", j=2)
                act.wait_ge(ek_filled, nxt + 1)
                act.activation(tiles(ek_sq[:]), slots[1], ACT.Square, bias=be2[:]).then_inc(ek_squared, 1)
                act.wait_ge(sqf_filled, nxt + 1)
                act.activation(tiles(s_raw[:, 0]), slots[2], ACT.Identity, bias=bs2[:]).then_inc(sqf_ready, 1)
                act.wait_ge(skf_filled, nxt + 1)
                act.activation(tiles(s_raw[:, 1]), slots[3], ACT.Identity, bias=bs2[:]).then_inc(skf_ready, 1)
                act.wait_ge(eq_filled, nxt + 1)
                act.activation(tiles(eq[:]), slots[0], ACT.Identity, bias=be2[:]).then_inc(eq_ready, 1)

            def inverse_norms(nxt):
                f = s_inv[:].rearrange("p a b c -> p (a b c)")
                act.wait_ge(s_norm_ready, 2 * nxt + 2)
                act.activation(f, f, ACT.Ln).then_inc(s_inv_step, 1)
                act.wait_ge(s_inv_step, nxt + 1)
                act.activation(f, f, ACT.Exp, scale=-0.5, bias=shift_bias[:]).then_inc(s_inv_ready, 1)

            def hyperbolic_evacuation(nxt):
                act.wait_ge(hf_filled, nxt + 1)
                act.activation(hqk[:].rearrange("p a b c -> p a (b c)"), banks[1][:, :, 0:HT * W2N], ACT.Tanh,
                               bias=bh4[:]).then_inc(hf_ready, 1)

            def hyperbolic_squares(nxt):
                act.wait_ge(hf_ready, nxt + 1)
                act.activation(hqk_sq[:].rearrange("p a b c -> p (a b c)"), hqk[:].rearrange("p a b c -> p (a b c)"),
                               ACT.Square).then_inc(h_squared, 1)

            def logs_of_denominators(nxt):
                act.wait_ge(den_ready, 2 * nxt + 2)
                act.activation(flat(rden[:]), flat(den[:]), ACT.Ln).then_inc(rden_step, 1)

            def inverse_denominators(nxt):
                act.wait_ge(rden_step, nxt + 1)
                act.activation(flat(rden[:]), flat(rden[:]), ACT.Exp, scale=-1.0).then_inc(rden_ready, 1)

            def roots_of_q(cur):
                act.wait_ge(q_ready, cur + 1)
                act.activation(flat(hs[:]), flat(mq[:]), ACT.Sqrt).then_inc(hs_rooted, 1)
                act.activation(flat(hr[:]), flat(mq[:]), ACT.Sqrt, bias=1.0).then_inc(hr_rooted, 1)

            def roots(cur, first):
                act.wait_ge(esb_ready, cur + 1)
                if not first:
                    act.wait_ge(dist_es, cur)
                act.activation(flat(droot[:]), flat(esb[:]), ACT.Sqrt, scale=c_e2[0:N, :]).then_inc(dist_rooted, 1)
                act.wait_ge(s_read, 2 * cur + 2)
                act.activation(flat(su[:]), flat(csb[:]), ACT.Sqrt, scale=-0.5, bias=0.5).then_inc(su_rooted, 1)
                act.activation(flat(sh[:]), flat(csb[:]), ACT.Sqrt, scale=0.5, bias=0.5).then_inc(sh_rooted, 1)

            def log_of_g(cur):
                act.wait_ge(g_ready, cur + 1)
                act.activation(flat(hs[:]), flat(hs[:]), ACT.Ln).then_inc(log_ready, 1)

            def logs(cur):
                act.wait_ge(sh_rooted, cur + 1)
                act.activation(flat(sh[:]), flat(sh[:]), ACT.Ln, bias=1.0).then_inc(w_step, 1)

            def inverses(cur):
                act.wait_ge(w_step, cur + 1)
                act.activation(flat(sh[:]), flat(sh[:]), ACT.Exp, scale=-1.0).then_inc(w_ready, 1)

            def arctangent(cur):
                act.wait_ge(t_ready, cur + 1)
                act.activation(flat(su[:]), flat(su[:]), ACT.Arctan).then_inc(atan_ready, 1)

            def exponent(cur):
                act.wait_ge(dist_shifted, cur + 1)
                act.activation(flat(dist[:]), flat(dist[:]), ACT.Exp).then_inc(exp_ready, 1)

            def attention_copy(cur, b):
                act.wait_ge(attn_turned, 2 * cur + b + 1)
                act.copy(attnT[:, b, :].rearrange("p (j w) -> p j w", j=2),
                         banks[2 + b][0:N, :, 0:4 * N]).then_inc(attnT_ready, 1)

            def cycle(i, new=True, mid=True, old=True, first=False):
                act.preload_act_table_set(SET_SQRT)
                if old:
                    roots_of_q(i - 2)
                if mid:
                    roots(i - 1, first)
                act.preload_act_table_set(SET_LN_EXP)
                if new:
                    feature_evacuation(i)
                if mid:
                    logs_of_denominators(i - 1)
                if old:
                    log_of_g(i - 2)
                if mid:
                    logs(i - 1)
                if new:
                    inverse_norms(i)
                if mid:
                    inverses(i - 1)
                if old:
                    exponent(i - 2)
                if mid:
                    inverse_denominators(i - 1)
                if new or mid:
                    act.preload_act_table_set(SET_ATAN_TANH)
                if new:
                    hyperbolic_evacuation(i)
                if old:
                    attention_copy(i - 2, 0)
                    attention_copy(i - 2, 1)
                if new:
                    hyperbolic_squares(i)
                if mid:
                    arctangent(i - 1)

            act.wait_ge(weights_loaded, WEIGHTS)
            act.wait_ge(c_ready, 1)
            cycle(0, mid=False, old=False)
            cycle(1, old=False, first=True)
            cycle(2)
            with act.Fori(3, PAIRS - 1) as i:
                cycle(i)
            cycle(PAIRS - 1)
            cycle(PAIRS, new=False)
            cycle(PAIRS + 1, new=False, mid=False)

        @block.vector
        def _(dve):
            dve.memset(eps_bias[:], LN_EPS)
            dve.wait_ge(consts_set, 3)
            for k in range(2):
                dve.memset(block64[64 * k:64 * k + 64, 64 * k:64 * k + 64], 1.0).then_inc(picks_set, 1)
                dve.memset(pick2[64 * k:64 * k + 64, k, :], 1.0).then_inc(picks_set, 1)
            for k in range(4):
                r = slice(32 * k, 32 * k + 32)
                dve.memset(block32[r, 32 * k:32 * k + 32], 1.0).then_inc(picks_set, 1)
                dve.memset(pick4[r, k, :], 1.0).then_inc(picks_set, 1)
            for k in range(2):
                last = dve.memset(segT[k][:], 1.0)
            last.then_inc(ones_set, 1)
            with dve.Fori(0, CHUNKS) as c:
                dve.wait_ge(u_ready, c + 1)
                for j in range(CH):
                    dve.bn_stats(stats[:, bass.ds(c * CH + j, 1), :].rearrange("n b k -> n (b k)"),
                                 u[:, bass.ds(c * CH + j, 1), :].rearrange("n b d -> n (b d)")).then_inc(stats_ready, 1)

            dve.wait_ge(softplus_step, 3)
            dve.scalar_tensor_tensor(sp[:], raw5[:, 0:4], 0.0, sp_abs[:], ALU.max, ALU.add).then_inc(softplus_step, 1)
            dve.wait_ge(softplus_step, 4)
            dve.reciprocal(sp_abs[:, 3:4], sp[:, 3:4]).then_inc(softplus_step, 1)
            dve.wait_ge(softplus_step, 5)
            dve.tensor_scalar(c_e2[:], sp[:, 0:1], sp_abs[:, 3:4], None, ALU.mult).then_inc(softplus_step, 1)
            dve.tensor_scalar(c_s[:], sp[:, 1:2], sp_abs[:, 3:4], 4.0, ALU.mult, ALU.mult).then_inc(softplus_step, 1)
            dve.tensor_scalar(c_h[:], sp[:, 2:3], sp_abs[:, 3:4], 2.0, ALU.mult, ALU.mult).then_inc(softplus_step, 1)
            dve.wait_ge(softplus_step, 8)
            dve.tensor_tensor(c_e2[:], c_e2[:], c_e2[:], ALU.mult).then_inc(c_ready, 1)

            half = D // 2
            step = [0]

            def done(ins):
                step[0] += 1
                ins.then_inc(stat_step, 1)
                dve.wait_ge(stat_step, step[0])

            dve.wait_ge(stats_ready, B)
            me, mo, ve, vo = stats[:, :, 1], stats[:, :, 4], stats[:, :, 2], stats[:, :, 5]
            done(dve.tensor_tensor(st["sum"][:], me, mo, ALU.add))
            done(dve.tensor_tensor(st["diff"][:], me, mo, ALU.subtract))
            done(dve.tensor_tensor(st["diff"][:], st["diff"][:], st["diff"][:], ALU.mult))
            done(dve.tensor_tensor(st["m2"][:], ve, vo, ALU.add))
            done(dve.scalar_tensor_tensor(st["m2"][:], st["diff"][:], half / 2.0, st["m2"][:], ALU.mult, ALU.add))
            done(dve.tensor_scalar(st["mean"][:], st["sum"][:], 0.5, None, ALU.mult))
            done(dve.tensor_tensor(st["sq"][:], st["mean"][:], st["mean"][:], ALU.mult))
            done(dve.scalar_tensor_tensor(st["norm"][:], st["sq"][:], float(D), st["m2"][:], ALU.mult, ALU.add))
            dve.wait_ge(stat_root, 1)
            done(dve.tensor_scalar(st["norm"][:], st["unorm"][:], MIN_NORM, None, ALU.max))
            done(dve.reciprocal(st["f"][:], st["norm"][:]))
            dve.wait_ge(stat_root, 2)
            done(dve.tensor_tensor(st["f"][:], st["f"][:], st["th"][:], ALU.mult))
            done(dve.tensor_tensor(st["yn"][:], st["f"][:], st["unorm"][:], ALU.mult))
            done(dve.tensor_scalar(st["yn"][:], st["yn"][:], MIN_NORM, None, ALU.max))
            done(dve.reciprocal(st["clip"][:], st["yn"][:]))
            done(dve.tensor_scalar(st["clip"][:], st["clip"][:], 1.0 - BALL_EPS, 1.0, ALU.mult, ALU.min))
            done(dve.tensor_tensor(st["f"][:], st["f"][:], st["clip"][:], ALU.mult))
            done(dve.tensor_tensor(st["var"][:], st["f"][:], st["f"][:], ALU.mult))
            done(dve.scalar_tensor_tensor(st["var"][:], st["var"][:], 1.0 / D, st["m2"][:], ALU.mult, ALU.mult))
            dve.wait_ge(stat_root, 3)
            done(dve.reciprocal(st["std"][:], st["std"][:]))
            done(dve.tensor_tensor(st["gain"][:], st["std"][:], st["f"][:], ALU.mult))
            done(dve.scalar_tensor_tensor(st["shift"][:], st["gain"][:], -1.0, st["mean"][:], ALU.mult, ALU.mult))

            def tiles(ap):
                return ap.rearrange("p (j t) w -> p j (t w)", j=2)

            def flat(ap):
                return ap.rearrange("p a b -> p (a b)")

            def normalise(nxt):
                for j in range(2):
                    b = 2 * nxt + j
                    dve.tensor_scalar(xn[:, j, :], u[:, bass.ds(b, 1), :].rearrange("n b d -> n (b d)"), st["gain"][:, bass.ds(b, 1)],
                                      st["shift"][:, bass.ds(b, 1)], ALU.mult, ALU.add).then_inc(xn_ready, 1)

            def keep_turned_tokens(nxt):
                dve.wait_ge(xT_filled, nxt + 1)
                dve.tensor_scalar(xT[:, bass.ds(nxt, 1), :].rearrange("p a w -> p (a w)"), banks[0][:, 0, 0:W2N], 1.0, None,
                                  ALU.mult).then_inc(xT_ready, 1)

            def fetch_turned_tokens(old, first):
                dve.wait_ge(xT_ready, old + 1)
                if not first:
                    dve.wait_ge(v_filled, old)
                dve.tensor_scalar(xT_old[:], xT[:, bass.ds(old, 1), :].rearrange("p a w -> p (a w)"), 1.0, None,
                                  ALU.mult).then_inc(xT_old_ready, 1)

            def key_evacuation(nxt):
                dve.wait_ge(ek_squared, nxt + 1)
                for h in range(2):
                    r = slice(64 * h, 64 * h + 64)
                    dve.tensor_scalar(ek_m2[r, :, h, :].rearrange("p (j t) w -> p j t w", j=2),
                                      banks[1][r, :, 0:2 * W2N].rearrange("p j (t w) -> p j t w", t=2),
                                      be2[r, :], -2.0, ALU.add, ALU.mult).then_inc(ek_ready, 1)

            def square_keys(nxt):
                dve.wait_ge(skf_ready, nxt + 1)
                dve.tensor_tensor(s_sq[:, 1], s_raw[:, 1], s_raw[:, 1], ALU.mult).then_inc(sk_squared, 1)

            def guarded_norms(nxt):
                for side, k, signal in ((0, 1, snq_filled), (1, 2, snk_filled)):
                    dve.wait_ge(signal, nxt + 1)
                    dve.tensor_scalar(tiles(s_inv[:, side]), banks[k][:, :, 0:2 * W2N], 1e-24,
                                      2.0 ** NORM_SHIFT, ALU.max, ALU.mult).then_inc(s_norm_ready, 1)

            def unit_keys(nxt):
                dve.wait_ge(s_inv_ready, nxt + 1)
                for h in range(2):
                    r = slice(64 * h, 64 * h + 64)
                    dve.tensor_tensor(sk_n[r, :, h, :], s_raw[r, 1], s_inv[r, 1], ALU.mult).then_inc(sn_ready, 1)

            def add_norms(dst, b, slot, norm, norm_ready, count):
                dve.tensor_copy(norm[:, b], slot[0:N, :, 4 * N:4 * N + 4]).then_inc(norm_ready, 1)
                dve.wait_ge(norm_ready, count)
                return dve.tensor_tensor(dst[:, b, :].rearrange("p (j h m) -> p j h m", j=2, m=N),
                                         slot[0:N, :, 0:4 * N].rearrange("p j (h m) -> p j h m", m=N),
                                         norm[:, b].unsqueeze(3).broadcast_to([N, 2, 4, N]), ALU.add)

            def euclid_to_sbuf(nxt, b, first):
                if b == 0 and not first:
                    dve.wait_ge(dist_rooted, nxt)
                dve.wait_ge(e_filled, 2 * nxt + b + 1)
                add_norms(esb, b, banks[(3 + b) % 4], eq_norm, eq_norm_ready, 2 * nxt + b + 1).then_inc(e_read, 1)

            def guard_euclid(nxt):
                dve.wait_ge(e_read, 2 * nxt + 2)
                dve.tensor_scalar(flat(esb[:]), flat(esb[:]), 1e-12, None, ALU.max).then_inc(esb_ready, 1)

            def sphere_to_sbuf(nxt, first):
                if not first:
                    dve.wait_ge(sh_rooted, nxt)
                for b in range(2):
                    dve.wait_ge(s_filled, 2 * nxt + b + 1)
                    dve.tensor_scalar(csb[:, b, :].rearrange("p (j w) -> p j w", j=2), banks[b][0:N, :, 0:4 * N],
                                      -SIM_MAX, SIM_MAX, ALU.max, ALU.min).then_inc(s_read, 1)

            def spread_keys(nxt):
                dve.wait_ge(hf_ready, nxt + 1)
                for h in range(4):
                    r = slice(32 * h, 32 * h + 32)
                    dve.tensor_scalar(hk_m2[r, :, h, :], hqk[r, 1], -2.0, None, ALU.mult)

            def query_norms(nxt):
                dve.wait_ge(un_filled, nxt + 1)
                dve.tensor_scalar(flat(one_un[:]), banks[1][:, 0, 0:HT * W2N], -1.0, 1.0, ALU.mult, ALU.add)\
                   .then_inc(un_ready, 1)

            def key_denominators(nxt):
                dve.wait_ge(h_squared, nxt + 1)
                for h in range(4):
                    r = slice(32 * h, 32 * h + 32)
                    dve.tensor_scalar(hk_den[r, :, h, :], hqk_sq[r, 1], -1.0, 1.0 / DHY, ALU.mult, ALU.add)\
                       .then_inc(hk_den_ready, 1)

            def hyperbolic_scores(mid, first, with_new):
                for b in range(2):
                    dve.wait_ge(hden_filled, 2 * mid + b + 1)
                    if b == 0 and not first:
                        dve.wait_ge(rden_step, mid)
                    dve.tensor_scalar(den[:, b, :].rearrange("p (j w) -> p j w", j=2), banks[2 * b + 1][0:N, :, 0:4 * N],
                                      1e-8, TINY, ALU.add, ALU.max).then_inc(den_ready, 1)
                    if b == 0 and with_new:
                        keep_turned_tokens(mid + 1)
                    dve.wait_ge(hdns_filled, 2 * mid + b + 1)
                    if b == 0 and not first:
                        dve.wait_ge(hr_rooted, mid)
                    add_norms(mq, b, banks[2 - 2 * b], hq_norm, hq_norm_ready, 2 * mid + b + 1).then_inc(mq_ready, 1)

            def place_values(mid, first):
                dve.wait_ge(v_filled, mid + 1)
                if not first:
                    dve.wait_ge(pv_filled, 2 * mid)
                dve.tensor_copy(v_aug[:, :, :, 0:DH], banks[0][0:N, :, :].rearrange("n b (h d) -> n b h d", d=DH))\
                   .then_inc(v_placed, 1)

            def clamp_q(mid):
                dve.wait_ge(mq_scaled, mid + 1)
                dve.scalar_tensor_tensor(flat(mq[:]), flat(den[:]), TINY, flat(mq[:]), ALU.is_gt, ALU.mult)\
                   .then_inc(q_masked, 1)
                dve.wait_ge(q_masked, mid + 1)
                dve.tensor_scalar(flat(mq[:]), flat(mq[:]), ARG_MIN_HALF, None, ALU.max).then_inc(q_ready, 1)

            def add_spherical(mid, first):
                if not first:
                    dve.wait_ge(attn_turned, 2 * mid)
                dve.wait_ge(atan_ready, mid + 1)
                dve.scalar_tensor_tensor(flat(dist[:]), flat(su[:]), c_s[0:N, :], flat(droot[:]), ALU.mult,
                                         ALU.add).then_inc(dist_es, 1)

            def add_roots(old):
                dve.wait_ge(hr_rooted, old + 1)
                dve.tensor_tensor(hs[:], hs[:], hr[:], ALU.add).then_inc(g_ready, 1)

            def add_hyperbolic(old):
                dve.wait_ge(dist_es, old + 1)
                dve.wait_ge(log_ready, old + 1)
                dve.scalar_tensor_tensor(flat(dist[:]), flat(hs[:]), c_h[0:N, :], flat(dist[:]), ALU.mult,
                                         ALU.add).then_inc(dist_whole, 1)
                dve.wait_ge(dist_whole, old + 1)
                dve.tensor_reduce(dmin[:], flat(dist[:]).rearrange("p (h m) -> p h m", m=N), AX, ALU.min)\
                   .then_inc(dmin_ready, 1)

            def shift_distance(old):
                dve.wait_ge(dmin_ready, old + 1)
                d3 = flat(dist[:]).rearrange("p (h m) -> p h m", m=N)
                dve.tensor_tensor(d3, dmin[:].unsqueeze(2).broadcast_to([N, 2 * HEADS, N]), d3, ALU.subtract)\
                   .then_inc(dist_shifted, 1)

            def divide_by_sum(old, b):
                n = 2 * old + b
                dve.wait_ge(pv_filled, n + 1)
                pv = banks[2 + b][0:N, :, 0:4 * (DH + 1)].rearrange("p j (h d) -> p j h d", h=4)
                dve.reciprocal(rsum[:, b, :].rearrange("p (j h) -> p j h", j=2), pv[:, :, :, DH]).then_inc(rsum_ready, 1)
                dve.wait_ge(rsum_ready, n + 1)
                for j in range(2):
                    dve.tensor_tensor(o_tok[b][:, 4 * j:4 * j + 4, :], pv[:, j, :, 0:DH],
                                      rsum[:, b, 4 * j:4 * j + 4].unsqueeze(2).broadcast_to([N, 4, DH]),
                                      ALU.mult).then_inc(o_ready, 1)

            def residual(old, b, first):
                n = 2 * old + b
                if b == 0 and not first:
                    dve.wait_ge(h2_saved, 16 * old)
                dve.scalar_tensor_tensor(hres[:, b, :], u[:, bass.ds(n, 1), :].rearrange("p a d -> p (a d)"),
                                         st["f"][:, bass.ds(n, 1)], bproj[0:N, :], ALU.mult, ALU.add)\
                   .then_inc(hres_ready, 1)

            def turned_output(old, b):
                dve.wait_ge(o_turned, 2 * old + b + 1)
                dve.tensor_copy(flat(oT[b][:]), banks[2 + b][:, 0, 0:4 * N]).then_inc(oT_ready, 1)

            def add_residual(old, b):
                n = 2 * old + b
                dve.wait_ge(hres_ready, n + 1)
                dve.wait_ge(proj_filled, n + 1)
                dve.tensor_tensor(h2_out[:, b, :], banks[2 + b][0:N, 1, 0:D], hres[:, b, :], ALU.add)\
                   .then_inc(h2_ready, 1)

            def cycle(i, new=True, mid=True, old=True, more=True, first_new=False, first_mid=False, first_old=False,
                      last=False):
                if mid:
                    hyperbolic_scores(i - 1, first_mid, new)
                    fetch_turned_tokens(i - 1, first_mid)
                if new and more:
                    normalise(i + 1)
                if new:
                    key_evacuation(i)
                    square_keys(i)
                    guarded_norms(i)
                if old:
                    add_hyperbolic(i - 2)
                    shift_distance(i - 2)
                if new:
                    euclid_to_sbuf(i, 0, first_new)
                    euclid_to_sbuf(i, 1, first_new)
                    unit_keys(i)
                    spread_keys(i)
                    key_denominators(i)
                if last:
                    dve.wait_ge(early_loaded, 16)
                    for t in range(early):
                        dve.bn_stats(h2_stats[:, t, :], h2[:, t, :]).then_inc(early_stats, 1)
                if mid and not new:
                    clamp_q(i - 1)
                if old:
                    divide_by_sum(i - 2, 0)
                    divide_by_sum(i - 2, 1)
                if new:
                    sphere_to_sbuf(i, first_new)
                if old:
                    turned_output(i - 2, 0)
                    turned_output(i - 2, 1)
                if new and mid:
                    clamp_q(i - 1)
                if old:
                    for b in range(2):
                        residual(i - 2, b, first_old)
                if mid and not new:
                    add_spherical(i - 1, first_mid)
                    add_roots(i - 1)
                if new:
                    query_norms(i)
                if mid:
                    place_values(i - 1, first_mid)
                if old:
                    for b in range(2):
                        add_residual(i - 2, b)
                if mid and new:
                    add_spherical(i - 1, first_mid)
                if new:
                    guard_euclid(i)

            normalise(0)
            keep_turned_tokens(0)
            cycle(0, mid=False, old=False, first_new=True)
            cycle(1, old=False, first_mid=True)
            cycle(2, first_old=True)
            with dve.Fori(3, PAIRS - 1) as i:
                cycle(i)
            cycle(PAIRS - 1, more=False)
            cycle(PAIRS, new=False)
            cycle(PAIRS + 1, new=False, mid=False, last=True)


def experts(nc, dims, banks, ident, handover, Wr, W1, b1, W2, b2, out):
    D, T, E, F, NT, NB, TPB, FC, PAIRS = dims
    h2, stats, h2_dram, h2_saved, early_loaded, early_stats, early = handover
    REPS = P // E
    AHEAD = 2
    SHIFTS = [26, 22, 18, 14, 10, 6, 2, 0]
    ROUNDS = len(SHIFTS)
    groups = (NT + 3) // 4
    early_groups = early // 4
    with ExitStack() as ctx:
        def sb(name, shape, dt=F32):
            return ctx.enter_context(nc.sbuf_tensor(name, shape, dt))

        x2 = sb("x2", [P, NT, D])
        x2T = sb("x2T", [P, T])
        x2T_hi = sb("x2T_hi", [P, T], F32R)
        x2T_lo = sb("x2T_lo", [P, T], F32R)
        w1_hi = [sb(f"w1_hi_{e}", [D, F], F32R) for e in range(E)]
        w1_lo = [sb(f"w1_lo_{e}", [D, F], F32R) for e in range(E)]
        w1 = [sb(f"w1_{e}", [D, F]) for e in range(E)]
        w2 = [sb(f"w2_{e}", [P, FC, D]) for e in range(E)]
        b1_rows = sb("b1_rows", [E * FC, P])
        b1T = sb("b1T", [P, E * FC])
        b2_sb = sb("b2_sb", [E, D])
        wr = sb("wr", [D, E])
        wr_reps = sb("wr_reps", [D, REPS, E])
        hid = [sb(f"hid{c}", [P, TB]) for c in range(FC)]
        ahead = sb("ahead", [P, AHEAD, NT, D])
        acc = sb("acc", [P, NT, D])
        st = {n: sb(f"st2_{n}", [P, NT]) for n in ("sum", "diff", "m2", "std", "shift")}
        eps2 = sb("eps2", [P, 1])
        probs = sb("probs", [P, T])
        above = sb("above", [P, T])
        ties = sb("ties", [E, T])
        ranks = sb("ranks", [E, T])
        gate = sb("gate", [P, NT, E])
        bmax = sb("bmax", [P, NB])
        nmax = sb("nmax", [P, 1])
        bsum = sb("bsum", [P, NB])
        psum_inv = sb("psum_inv", [P, 1])
        same = sb("same", [P, P])
        iota = sb("iota", [P, P], I32)
        rep = sb("rep", [P, 1], I32)
        trial = sb("trial", [P, ROUNDS], I32)
        low = sb("low", [P, 1], I32)
        thr = sb("thr", [P, 1], I32)
        count = sb("count", [P, 1])
        enough = sb("enough", [P, 1])
        digit = sb("digit", [P, 1], I32)
        need = sb("need", [P, 1])

        def sem(name):
            return ctx.enter_context(nc.semaphore(name + "2"))

        (h2_loaded, router_loaded, bias_loaded, iota_set, eps_set, sel_const, stats_ready, stat_step, std_rooted,
         x2_ready, x2_turned, x2T_ready, wr_reps_ready, x2T_rounded, x2T_split, w1_rounded, w1_split, b1_turned, b1T_ready, logits_filled, bmax_ready, nmax_ready, exp_ready,
         psum_step, probs_ready, thr_ready, counted, enough_ready, digits_filled, digit_ready, low_ready,
         gate_step, gates_ready, gates_turned, gate_ready, bias_filled, hid_filled, hid_ready, y_kept, acc_ready,
         y_added, out_stored, hid_used, kept_added) = (
             sem(n) for n in """h2_loaded router_loaded bias_loaded iota_set eps_set sel_const stats_ready stat_step std_rooted
                 x2_ready x2_turned x2T_ready wr_reps_ready x2T_rounded x2T_split w1_rounded w1_split b1_turned b1T_ready logits_filled bmax_ready nmax_ready exp_ready
                 psum_step probs_ready thr_ready counted enough_ready digits_filled digit_ready low_ready
                 gate_step gates_ready gates_turned gate_ready bias_filled hid_filled hid_ready y_kept acc_ready
                 y_added out_stored hid_used kept_added""".split())
        w_in = [ctx.enter_context(nc.semaphore(f"expert_in{e}")) for e in range(E)]
        block = ctx.enter_context(nc.Block())
        hid_bank = [banks[c // 2][:, c % 2, 0:TB] for c in range(FC)]
        y_bank = [banks[2][:, 0, :], banks[3][:, 0, :]]
        count_bank = banks[2][:, 1, :]
        gate_bank = banks[3][:, 1, 0:NT * E]
        bias_bank = [banks[2][:, 1, :], banks[3][:, 1, :]]
        seven = [banks[k // 2][:, k % 2, :] for k in range(8)]
        h2_rows = h2_dram.rearrange("(t p) c -> p t c", p=P)

        @block.sync
        def _(sp):
            sp.dma_start(wr[:], Wr).then_inc(router_loaded, 16)
            sp.dma_start(b1_rows[:], b1.rearrange("e (c p) -> (e c) p", p=P)).then_inc(bias_loaded, 16)
            sp.dma_start(b2_sb[:], b2).then_inc(bias_loaded, 16)
            def load_expert(e):
                sp.dma_start(w1[e][:], W1[e]).then_inc(w_in[e], 16)
                sp.dma_start(w2[e][:], W2[e].rearrange("(c p) d -> p c d", p=P)).then_inc(w_in[e], 16)

            load_expert(0)
            load_expert(1)
            sp.wait_ge(h2_saved, 16 * PAIRS)
            sp.dma_start(h2[:, early:, :], h2_rows[:, early:, :]).then_inc(h2_loaded, 16)
            for e in range(2, E):
                load_expert(e)
            sp.wait_ge(y_added, (E - AHEAD) * NT)
            sp.dma_start(out.rearrange("b n c -> (b n) c").rearrange("(t p) c -> p t c", p=P), acc[:]).then_inc(out_stored, 16)
            sp.wait_ge(out_stored, 16)

        @block.gpsimd
        def _(pool):
            pool.iota(iota[:], [[1, P]], base=P, channel_multiplier=-1).then_inc(iota_set, 1)
            pool.iota(rep[:], [[0, 1]], base=0, channel_multiplier=1).then_inc(iota_set, 1)

            def split_weights(e):
                pool.wait_ge(w_in[e], 32)
                pool.tensor_copy(w1_hi[e][:], w1[e][:]).then_inc(w1_rounded, 1)
                pool.wait_ge(w1_rounded, e + 1)
                pool.tensor_tensor(w1_lo[e][:], w1[e][:], w1_hi[e][:].bitcast(F32), ALU.subtract).then_inc(w1_split, 1)

            for e in range(AHEAD):
                split_weights(e)
            for n in range(NB):
                tok = slice(n * TB, (n + 1) * TB)
                pool.wait_ge(x2T_rounded, n + 1)
                pool.tensor_tensor(x2T_lo[:, tok], x2T[:, tok], x2T_hi[:, tok].bitcast(F32), ALU.subtract)\
                    .then_inc(x2T_split, 1)
            for e in range(AHEAD, E):
                split_weights(e)

        @block.tensor
        def _(pe):
            pe.wait_ge(bias_loaded, 32)
            pe.transpose(seven[7][:, 0:E * FC], b1_rows[:], ident[0:E * FC, 0:E * FC]).then_inc(b1_turned, 1)
            def turn_tiles(t0, t1):
                for t in range(t0, t1):
                    pe.wait_ge(x2_ready, t + 1)
                    last = pe.transpose(seven[t // 4][:, (t % 4) * P:(t % 4 + 1) * P], x2[:, t, :], ident[:])
                    if t % 4 == 3 or t == NT - 1:
                        last.then_inc(x2_turned, 1)

            def logits(n):
                pe.wait_ge(x2T_ready, min(n + 1, groups))
                pe.matmul(seven[n][:, 0:TB], wr_reps[:].rearrange("p r e -> p (r e)"), x2T[:, n * TB:(n + 1) * TB],
                          start=True, stop=True).then_inc(logits_filled, 1)

            turn_tiles(0, 4 * early_groups)
            for n in range(early_groups):
                if n == 0:
                    pe.wait_ge(wr_reps_ready, 1)
                logits(n)
            turn_tiles(4 * early_groups, NT)
            for n in range(early_groups, NB):
                logits(n)

            def first_layer(e, n, c, step):
                if step is not None:
                    pe.wait_ge(hid_ready, FC * step + (c - FC + 1))
                f, tok = slice(c * P, (c + 1) * P), bass.ds(n * TB, TB)
                pe.matmul(hid_bank[c], w1_lo[e][:, f], x2T_hi[:, tok], start=True, stop=False)
                pe.matmul(hid_bank[c], w1_hi[e][:, f], x2T_lo[:, tok], start=False, stop=False)
                pe.matmul(hid_bank[c], w1_hi[e][:, f], x2T_hi[:, tok], start=False, stop=True).then_inc(hid_filled, 1)

            def second_layer(e, k, c, step):
                pe.wait_ge(hid_ready, FC * step + c + 1)
                for t in range(TPB):
                    last = pe.matmul(y_bank[k][:, t * D:(t + 1) * D], hid[c][:, t * P:(t + 1) * P], w2[e][:, c, :],
                                     start=(c == 0 and t == 0), stop=(c == FC - 1), skip_group_check=True)
                last.then_inc(hid_used, 1)

            def y_bank_free(step, q, first):
                if q == 0:
                    if not first:
                        pe.wait_ge(y_kept, step - 1)
                elif first:
                    pe.wait_ge(y_kept, AHEAD * NB)
                else:
                    pe.wait_ge(y_added, (step - 1 - AHEAD * NB) * TPB)

            def both_experts(q, n, first=False, last_block=False, searching=False):
                step = 2 * NB * q + 2 * n
                for k in range(2):
                    y_bank_free(step + k, q, first)
                    for c in range(FC):
                        if k == 0:
                            first_layer(2 * q + 1, n, c, step + 1)
                        elif not last_block:
                            first_layer(2 * q, n + 1, c, step + 2)
                        elif q < E // 2 - 1:
                            if c == 0:
                                pe.wait_ge(w_in[2 * q + 2], 32)
                                pe.wait_ge(w_in[2 * q + 3], 32)
                                pe.wait_ge(w1_split, 2 * q + 4)
                            first_layer(2 * q + 2, 0, c, step + 2)
                        second_layer(2 * q + k, k, c, step + k)
                    if searching:
                        pe.wait_ge(enough_ready, 2 * n + k + 1)
                        pe.matmul(count_bank[:, 0:1], same[:], enough[:], start=True, stop=True).then_inc(digits_filled, 1)

            pe.wait_ge(exp_ready, NB)
            pe.wait_ge(b1T_ready, 1)
            pe.wait_ge(w_in[0], 32)
            pe.wait_ge(w_in[1], 32)
            pe.wait_ge(w1_split, AHEAD)
            pe.wait_ge(x2T_split, NB)
            for c in range(FC):
                first_layer(0, 0, c, None)
            both_experts(0, 0, first=True, searching=True)
            with pe.Fori(1, ROUNDS // 2) as n:
                both_experts(0, n, searching=True)
            with pe.Fori(ROUNDS // 2, NB - 1) as n:
                both_experts(0, n)
            both_experts(0, NB - 1, last_block=True)
            pe.wait_ge(gates_ready, 1)
            for t in range(NT):
                last = pe.transpose(gate_bank[:, t * E:(t + 1) * E], above[0:E, t * P:(t + 1) * P], ident[0:E, 0:E])
            last.then_inc(gates_turned, 1)
            for g in range(groups):
                if g == 1:
                    pe.wait_ge(gate_ready, 1)
                if g >= 2:
                    pe.wait_ge(acc_ready, g - 1)
                for t in range(4 * g, min(4 * g + 4, NT)):
                    last = pe.matmul(bias_bank[g % 2][:, (t % 4) * D:(t % 4 + 1) * D], above[0:E, t * P:(t + 1) * P],
                                     b2_sb[:], start=True, stop=True)
                last.then_inc(bias_filled, 1)
            for q in range(1, E // 2):
                if q == 1:
                    both_experts(1, 0, first=True)
                with pe.Fori(1 if q == 1 else 0, NB - 1) as n:
                    both_experts(q, n)
                both_experts(q, NB - 1, last_block=True)

        @block.scalar
        def _(act):
            act.preload_act_table_set(SET_SQRT)
            act.wait_ge(b1_turned, 1)
            act.copy(b1T[:], seven[7][:, 0:E * FC]).then_inc(b1T_ready, 1)
            act.wait_ge(eps_set, 1)

            def round_tokens(n):
                act.wait_ge(x2T_ready, min(n + 1, groups))
                act.copy(x2T_hi[:, n * TB:(n + 1) * TB], x2T[:, n * TB:(n + 1) * TB]).then_inc(x2T_rounded, 1)

            for g in range(groups):
                n = min(4, NT - 4 * g)
                if g == early_groups:
                    for m in range(early_groups):
                        round_tokens(m)
                if g == 0 or g == early_groups:
                    t0, t1 = (0, early) if g == 0 else (early, NT)
                    act.wait_ge(stat_step, 5 if g == 0 else 12)
                    act.activation(st["std"][:, t0:t1], st["m2"][:, t0:t1], ACT.Sqrt, scale=1.0 / D,
                                   bias=eps2[:]).then_inc(std_rooted, 1)
                act.wait_ge(x2_turned, g + 1)
                act.copy(x2T[:, 4 * g * P:(4 * g + n) * P], seven[g][:, 0:n * P]).then_inc(x2T_ready, 1)
            act.preload_act_table_set("exp_and_others")
            for n in range(early_groups, NB):
                round_tokens(n)
            act.wait_ge(nmax_ready, 1)
            for n in range(NB):
                act.activation(probs[:, n * TB:(n + 1) * TB], seven[n][:, 0:TB], ACT.Exp, bias=nmax[:],
                               accum_out=bsum[:, n:n + 1]).then_inc(exp_ready, 1)
            act.preload_act_table_set("gelu_and_others")

            def gelus(e, step, first=False):
                for c in range(FC):
                    act.wait_ge(hid_filled, FC * step + c + 1)
                    if not first:
                        act.wait_ge(hid_used, FC * step + (c - FC + 1))
                    act.activation(hid[c][:], hid_bank[c], ACT.Gelu, bias=b1T[:, bass.ds(e * FC + c, 1)])\
                       .then_inc(hid_ready, 1)

            def keep(n, k):
                act.wait_ge(hid_used, FC * (2 * n + k + 1))
                act.copy(ahead[:, k, bass.ds(n * TPB, TPB), :].rearrange("p t d -> p (t d)"),
                         y_bank[k][:, 0:TB]).then_inc(y_kept, 1)

            gelus(0, 0, first=True)
            with act.Fori(0, NB - 1) as n:
                gelus(1, 2 * n + 1)
                keep(n, 0)
                gelus(0, 2 * n + 2)
                keep(n, 1)
            gelus(1, 2 * NB - 1)
            keep(NB - 1, 0)
            gelus(2, 2 * NB)
            keep(NB - 1, 1)
            gelus(3, 2 * NB + 1)
            with act.Fori(1, NB) as n:
                gelus(2, 2 * NB + 2 * n)
                gelus(3, 2 * NB + 2 * n + 1)
            with act.Fori(2, E // 2) as q:
                with act.Fori(0, NB) as n:
                    gelus(2 * q, 2 * NB * q + 2 * n)
                    gelus(2 * q + 1, 2 * NB * q + 2 * n + 1)

        @block.vector
        def _(dve):
            dve.memset(eps2[:], LN_EPS).then_inc(eps_set, 1)
            step = [0]

            def done(ins):
                step[0] += 1
                ins.then_inc(stat_step, 1)
                dve.wait_ge(stat_step, step[0])

            def normalise(t0, t1):
                me, mo, ve, vo = (stats[:, t0:t1, k] for k in (1, 4, 2, 5))
                total, diff, m2, std, shift = (st[k][:, t0:t1] for k in ("sum", "diff", "m2", "std", "shift"))
                done(dve.tensor_tensor(total, me, mo, ALU.add))
                done(dve.tensor_tensor(diff, me, mo, ALU.subtract))
                done(dve.tensor_tensor(diff, diff, diff, ALU.mult))
                done(dve.tensor_tensor(m2, ve, vo, ALU.add))
                done(dve.scalar_tensor_tensor(m2, diff, D / 4.0, m2, ALU.mult, ALU.add))
                dve.wait_ge(std_rooted, 1 if t0 == 0 else 2)
                done(dve.reciprocal(std, std))
                done(dve.scalar_tensor_tensor(shift, total, -0.5, std, ALU.mult, ALU.mult))
                for t in range(t0, t1):
                    dve.tensor_scalar(x2[:, t, :], h2[:, t, :], st["std"][:, t:t + 1], st["shift"][:, t:t + 1], ALU.mult,
                                      ALU.add).then_inc(x2_ready, 1)

            dve.wait_ge(early_stats, early)
            normalise(0, early)

            consts = [0]

            def const(ins):
                consts[0] += 1
                ins.then_inc(sel_const, 1)
                dve.wait_ge(sel_const, consts[0])

            dve.wait_ge(iota_set, 2)
            const(dve.tensor_scalar(iota[:], iota[:], E - 1, None, ALU.bitwise_and))
            const(dve.tensor_scalar(same[:], iota[:], 0.0, None, ALU.is_equal))
            const(dve.tensor_scalar(rep[:], rep[:], int(np.log2(E)), None, ALU.logical_shift_right))
            for r, shift in enumerate(SHIFTS[:-1]):
                dve.tensor_scalar(trial[:, r:r + 1], rep[:], shift, None, ALU.logical_shift_left)
            dve.tensor_scalar(trial[:, ROUNDS - 1:ROUNDS], rep[:], 2, None, ALU.logical_shift_right)
            const(dve.memset(low[:], 0))
            dve.wait_ge(router_loaded, 16)
            dve.tensor_copy(wr_reps[:], wr[:].unsqueeze(1).broadcast_to([D, REPS, E])).then_inc(wr_reps_ready, 1)

            dve.wait_ge(h2_loaded, 16)
            for t in range(early, NT):
                dve.bn_stats(stats[:, t, :], h2[:, t, :]).then_inc(stats_ready, 1)
            dve.wait_ge(stats_ready, NT - early)
            normalise(early, NT)

            for n in range(NB):
                dve.wait_ge(logits_filled, n + 1)
                dve.tensor_reduce(bmax[:, n:n + 1], seven[n][:, 0:TB], AX, ALU.max).then_inc(bmax_ready, 1)
            dve.wait_ge(bmax_ready, NB)
            dve.tensor_reduce(nmax[:], bmax[:], AX, ALU.max).then_inc(psum_step, 1)
            dve.wait_ge(psum_step, 1)
            dve.tensor_scalar(nmax[:], nmax[:], -1.0, None, ALU.mult).then_inc(nmax_ready, 1)
            dve.wait_ge(exp_ready, NB)
            dve.tensor_reduce(psum_inv[:], bsum[:], AX, ALU.add).then_inc(psum_step, 1)
            dve.wait_ge(psum_step, 2)
            dve.reciprocal(psum_inv[:], psum_inv[:]).then_inc(psum_step, 1)
            dve.wait_ge(psum_step, 3)
            dve.tensor_scalar(probs[:], probs[:], psum_inv[:], None, ALU.mult).then_inc(probs_ready, 1)
            dve.wait_ge(probs_ready, 1)

            for r, shift in enumerate(SHIFTS):
                dve.tensor_tensor(thr[:], low[:], trial[:, r:r + 1], ALU.bitwise_or).then_inc(thr_ready, 1)
                dve.wait_ge(thr_ready, r + 1)
                dve.tensor_scalar(above[:], probs[:], thr[:].bitcast(F32), 0.0, ALU.is_ge, ALU.add,
                                  accum_out=count[:]).then_inc(counted, 1)
                dve.wait_ge(counted, r + 1)
                dve.tensor_scalar(enough[:], count[:], float(TOP), None, ALU.is_ge).then_inc(enough_ready, 1)
                dve.wait_ge(digits_filled, r + 1)
                share = 1.0 if r < ROUNDS - 1 else 4.0 / REPS
                dve.tensor_scalar(digit[:], count_bank[:, 0:1], share, -1.0, ALU.mult, ALU.add).then_inc(digit_ready, 1)
                dve.wait_ge(digit_ready, 2 * r + 1)
                dve.tensor_scalar(digit[:], digit[:], shift, None, ALU.logical_shift_left).then_inc(digit_ready, 1)
                dve.wait_ge(digit_ready, 2 * r + 2)
                dve.tensor_tensor(low[:], low[:], digit[:], ALU.bitwise_or).then_inc(low_ready, 1)
                dve.wait_ge(low_ready, r + 1)

            at = low[0:E, :].bitcast(F32)
            dve.tensor_scalar(above[0:E, :], probs[0:E, :], at, 0.0, ALU.is_gt, ALU.add,
                              accum_out=count[0:E, :]).then_inc(gate_step, 1)
            dve.tensor_scalar(ties[:], probs[0:E, :], at, None, ALU.is_equal).then_inc(gate_step, 1)
            dve.wait_ge(gate_step, 2)
            dve.tensor_tensor_scan(ranks[:], ties[:], ties[:], 0.0, ALU.add, ALU.max).then_inc(gate_step, 1)
            dve.tensor_scalar(need[0:E, :], count[0:E, :], -1.0, float(TOP), ALU.mult, ALU.add).then_inc(gate_step, 1)
            dve.wait_ge(gate_step, 4)
            dve.scalar_tensor_tensor(ties[:], ranks[:], need[0:E, :], ties[:], ALU.is_le, ALU.mult).then_inc(gate_step, 1)
            dve.wait_ge(gate_step, 5)
            dve.tensor_tensor(above[0:E, :], above[0:E, :], ties[:], ALU.add).then_inc(gate_step, 1)
            dve.wait_ge(gate_step, 6)
            dve.tensor_tensor(above[0:E, :], above[0:E, :], probs[0:E, :], ALU.mult).then_inc(gates_ready, 1)
            dve.wait_ge(gates_turned, 1)
            dve.tensor_copy(gate[:].rearrange("p t e -> p (t e)"), gate_bank).then_inc(gate_ready, 1)
            dve.wait_ge(gate_ready, 1)

            for g in range(groups):
                n = min(4, NT - 4 * g)
                dve.wait_ge(bias_filled, g + 1)
                dve.tensor_tensor(acc[:, 4 * g:4 * g + n, :].rearrange("p t d -> p (t d)"), bias_bank[g % 2][:, 0:n * D],
                                  h2[:, 4 * g:4 * g + n, :].rearrange("p t d -> p (t d)"), ALU.add).then_inc(acc_ready, 1)
            dve.wait_ge(acc_ready, groups)
            dve.wait_ge(y_kept, AHEAD * NB)

            def add_gated(product, t, e, signal):
                tile = acc[:, bass.ds(t, 1), :].rearrange("p t d -> p (t d)")
                dve.scalar_tensor_tensor(tile, product, gate[:, bass.ds(t, 1), bass.ds(e, 1)].rearrange("p t e -> p (t e)"),
                                         tile, ALU.mult, ALU.add).then_inc(signal, 1)

            def add_step(q, n, k):
                step = 2 * NB * q + 2 * n + k
                dve.wait_ge(hid_used, FC * (step + 1))
                if k == 1:
                    dve.wait_ge(y_added, (step - AHEAD * NB) * TPB)
                for j in range(TPB):
                    add_gated(y_bank[k][:, j * D:(j + 1) * D], n * TPB + j, 2 * q + k, y_added)

            with dve.Fori(0, NB) as n:
                for k in range(AHEAD):
                    if k:
                        dve.wait_ge(kept_added, (n * AHEAD + k) * TPB)
                    for j in range(TPB):
                        t = n * TPB + j
                        add_gated(ahead[:, k, bass.ds(t, 1), :].rearrange("p t d -> p (t d)"), t, k, kept_added)
                dve.wait_ge(kept_added, (n + 1) * (AHEAD * TPB))
                for k in range(2):
                    add_step(1, n, k)
            with dve.Fori(2, E // 2) as q:
                with dve.Fori(0, NB) as n:
                    for k in range(2):
                        add_step(q, n, k)


_INS = ['x', 'L0_tok_W', 'L0_tok_b', 'L0_tok_effective_scale', 'L0_attn_w_qkv', 'L0_attn_w_proj', 'L0_attn_b_proj',
        'L0_attn_w_e', 'L0_attn_b_e', 'L0_attn_w_s', 'L0_attn_b_s', 'L0_attn_w_h', 'L0_attn_b_h', 'L0_attn_alpha',
        'L0_attn_beta', 'L0_attn_gamma', 'L0_attn_temperature', 'L0_ffn_Wr', 'L0_ffn_W1', 'L0_ffn_b1', 'L0_ffn_W2',
        'L0_ffn_b2']
_OUTS = [((32, 84, 128), 'float32')]


def kernel(**inputs):
    import numpy as _np
    import concourse.bacc as _bacc
    from concourse import mybir as _mybir
    from concourse.bass_utils import run_bass_kernel_spmd as _run

    nc = _bacc.Bacc("TRN2", target_bir_lowering=False, num_devices=1)
    arrays, args = {}, []
    for name in _INS:
        a = _np.ascontiguousarray(inputs[name])
        if a.ndim == 0:
            a = a.reshape(1)
        arrays[f"in_{name}_dram"] = a
        args.append(nc.dram_tensor(f"in_{name}_dram", a.shape, _mybir.dt.from_np(a.dtype), kind="ExternalInput").ap())
    for i, (shape, dtype) in enumerate(_OUTS):
        dt = _mybir.dt.from_np(_np.dtype(dtype))
        args.append(nc.dram_tensor(f"out_{i}_dram", shape, dt, kind="ExternalOutput").ap())
    tower(nc, *args)
    r = _run(nc, [arrays], core_ids=[0])
    got = tuple(r.results[0][f"out_{i}_dram"] for i in range(len(_OUTS)))
    return got[0]
```
